# Optimizing a Trainium2 kernel written in Bass

```python
import numpy as np
import jax
import jax.numpy as jnp

def _softmax(x, axis=-1):
    return jax.nn.softmax(x, axis=axis)

def _gelu(x):
    return jax.nn.gelu(x, approximate=True)

def _silu(x):
    return jax.nn.silu(x)

def _sigmoid(x):
    return jax.nn.sigmoid(x)

def _layernorm(x, axis=-1, eps=1e-05):
    m = jnp.mean(x, axis=axis, keepdims=True)
    v = jnp.var(x, axis=axis, keepdims=True)
    return (x - m) / jnp.sqrt(v + eps)

def _scatter_add(tgt, idx, src, axis=0):
    return tgt.at[idx].add(src)

def _segment_sum(src, seg, n):
    return jax.ops.segment_sum(src, seg, n)
kernel_name = 'mk_perceiver_d1_seqx_r4_f98502'

def setup_inputs(seed: int=0):
    np.random.seed(seed)
    _w = jnp.asarray

    def _rec_inputs():
        import jax
        import jax.numpy as jnp
        _rk = jax.random.key(seed)
        x = -0.0003929 + 0.9999 * jax.random.normal(jax.random.fold_in(_rk, 1), (1, 256, 512), jnp.float32)
        _lenS = 256 - jax.random.randint(jax.random.fold_in(_rk, 7), (1,), 0, max(1, 256 // 4) + 1, jnp.int32)
        _lenS2 = 4096 - jax.random.randint(jax.random.fold_in(_rk, 8), (1,), 0, max(1, 4096 // 4) + 1, jnp.int32)
        _ctx_1024P = jax.random.normal(jax.random.fold_in(_rk, 11), (1, 16, 256), jnp.float32)
        _ctx_1024c = jax.random.dirichlet(jax.random.fold_in(_rk, 511), 0.3 * jnp.ones((16,), jnp.float32), (1, 4096))
        _ctx_1024t = jnp.einsum('bsk,bkd->bsd', _ctx_1024c, _ctx_1024P)
        _ctx_1024t = _ctx_1024t * jax.lax.rsqrt(jnp.mean(jnp.square(_ctx_1024t)) + 1e-12) * 0.953939
        ctx_1024 = 0.000227908 + 0.99994 * (_ctx_1024t + 0.3 * jax.random.normal(jax.random.fold_in(_rk, 611), (1, 4096, 256), jnp.float32))
        return (x, ctx_1024)
    x, ctx_1024 = _rec_inputs()

    def _L0_xattn_setup():
        import jax, jax.numpy as jnp
        import numpy as np
        EPS = 1e-05

        def rmsnorm(x, g, eps=EPS):
            var = jnp.mean(jnp.square(x), axis=-1, keepdims=True)
            return x * jax.lax.rsqrt(var + eps) * g
        key = jax.random.key(seed)
        ks = jax.random.split(key, 8)
        B, Sq, Skv = (2, 1024, 128)
        dim, cdim, H, D = (512, 256, 16, 128)
        inner = H * D
        s = lambda f: 1.0 / np.sqrt(f)
        return {'hidden_states': jax.random.normal(ks[0], (B, Sq, dim), jnp.float32), 'encoder_hidden_states': jax.random.normal(ks[1], (B, Skv, cdim), jnp.float32), 'Wq': jax.random.normal(ks[2], (dim, inner), jnp.float32) * s(dim), 'Wk': jax.random.normal(ks[3], (cdim, inner), jnp.float32) * s(cdim), 'Wv': jax.random.normal(ks[4], (cdim, inner), jnp.float32) * s(cdim), 'Wo': jax.random.normal(ks[5], (inner, dim), jnp.float32) * s(inner), 'gq': jnp.ones((D,), jnp.float32), 'gk': jnp.ones((D,), jnp.float32)}
    _L0_xattn_all = _L0_xattn_setup()
    _L0_xattn_in = {k: v for k, v in _L0_xattn_all.items() if k in ('Wq', 'Wk', 'Wv', 'Wo', 'gq', 'gk')}
    del _L0_xattn_all

    def _L0_attn_setup():
        import jax, jax.numpy as jnp
        import numpy as np
        HEADS = 16
        key = jax.random.key(seed)
        ks = jax.random.split(key, 5)
        B, T, D = (2, 512, 512)
        s = 0.02
        return {'x': jax.random.normal(ks[0], (B, T, D), dtype=jnp.float32), 'Wq': jax.random.normal(ks[1], (D, D), dtype=jnp.float32) * s, 'Wk': jax.random.normal(ks[2], (D, D), dtype=jnp.float32) * s, 'Wv': jax.random.normal(ks[3], (D, D), dtype=jnp.float32) * s, 'Wo': jax.random.normal(ks[4], (D, D), dtype=jnp.float32) * s}
    _L0_attn_all = _L0_attn_setup()
    _L0_attn_in = {k: v for k, v in _L0_attn_all.items() if k in ('Wq', 'Wk', 'Wv', 'Wo')}
    del _L0_attn_all

    def _L0_ffn_setup():
        import jax, jax.numpy as jnp
        import numpy as np
        B, S, D = (4, 128, 512)
        E, K, H = (8, 2, 352)
        HS = 2 * 352
        ALPHA = 0.001
        W_SCALE = 0.02

        def _moe_forward(hidden_states, gate_w, w_gate, w_up, w_down, sw_gate, sw_up, sw_down):
            b, s, d = hidden_states.shape
            x = hidden_states.reshape(-1, d)
            T = x.shape[0]
            logits = x @ gate_w
            scores = jax.nn.softmax(logits, axis=-1)
            topk_w, topk_idx = jax.lax.top_k(scores, K)
            mask = jax.nn.one_hot(topk_idx, E, dtype=scores.dtype).sum(axis=1)
            ce = mask.mean(axis=0)
            Pi = scores.mean(axis=0)
            aux_loss = (Pi * ce * E).sum() * ALPHA
            comb = jnp.zeros((T, E), dtype=x.dtype)
            comb = comb.at[jnp.arange(T)[:, None], topk_idx].add(topk_w)
            g = jax.nn.silu(jnp.einsum('td,edh->teh', x, w_gate)) * jnp.einsum('td,edh->teh', x, w_up)
            routed = jnp.einsum('teh,ehd,te->td', g, w_down, comb)
            shared = jax.nn.silu(x @ sw_gate) * (x @ sw_up) @ sw_down
            out = (routed + shared).reshape(b, s, d)
            return (out, aux_loss)
        key = jax.random.key(seed)
        ks = jax.random.split(key, 8)
        rn = lambda k, sh: jax.random.normal(k, sh, dtype=jnp.float32)
        return {'hidden_states': rn(ks[0], (B, S, D)), 'gate_w': rn(ks[1], (D, E)) * W_SCALE, 'w_gate': rn(ks[2], (E, D, H)) * W_SCALE, 'w_up': rn(ks[3], (E, D, H)) * W_SCALE, 'w_down': rn(ks[4], (E, H, D)) * W_SCALE, 'sw_gate': rn(ks[5], (D, HS)) * W_SCALE, 'sw_up': rn(ks[6], (D, HS)) * W_SCALE, 'sw_down': rn(ks[7], (HS, D)) * W_SCALE}
    _L0_ffn_all = _L0_ffn_setup()
    _L0_ffn_in = {k: v for k, v in _L0_ffn_all.items() if k in ('gate_w', 'w_gate', 'w_up', 'w_down', 'sw_gate', 'sw_up', 'sw_down')}
    del _L0_ffn_all
    return {'x': x, 'ctx_1024': ctx_1024, 'L0_xattn_Wq': _L0_xattn_in['Wq'], 'L0_xattn_Wk': _L0_xattn_in['Wk'], 'L0_xattn_Wv': _L0_xattn_in['Wv'], 'L0_xattn_Wo': _L0_xattn_in['Wo'], 'L0_xattn_gq': _L0_xattn_in['gq'], 'L0_xattn_gk': _L0_xattn_in['gk'], 'L0_attn_Wq': _L0_attn_in['Wq'], 'L0_attn_Wk': _L0_attn_in['Wk'], 'L0_attn_Wv': _L0_attn_in['Wv'], 'L0_attn_Wo': _L0_attn_in['Wo'], 'L0_ffn_gate_w': _L0_ffn_in['gate_w'], 'L0_ffn_w_gate': _L0_ffn_in['w_gate'], 'L0_ffn_w_up': _L0_ffn_in['w_up'], 'L0_ffn_w_down': _L0_ffn_in['w_down'], 'L0_ffn_sw_gate': _L0_ffn_in['sw_gate'], 'L0_ffn_sw_up': _L0_ffn_in['sw_up'], 'L0_ffn_sw_down': _L0_ffn_in['sw_down']}

def reference(x, ctx_1024, L0_xattn_Wq, L0_xattn_Wk, L0_xattn_Wv, L0_xattn_Wo, L0_xattn_gq, L0_xattn_gk, L0_attn_Wq, L0_attn_Wk, L0_attn_Wv, L0_attn_Wo, L0_ffn_gate_w, L0_ffn_w_gate, L0_ffn_w_up, L0_ffn_w_down, L0_ffn_sw_gate, L0_ffn_sw_up, L0_ffn_sw_down):
    import jax
    import jax.numpy as jnp

    def _L0_xattn_ref(hidden_states, encoder_hidden_states, Wq, Wk, Wv, Wo, gq, gk):
        import jax, jax.numpy as jnp
        import numpy as np
        EPS = 1e-05

        def rmsnorm(x, g, eps=EPS):
            var = jnp.mean(jnp.square(x), axis=-1, keepdims=True)
            return x * jax.lax.rsqrt(var + eps) * g
        B, Sq, _ = hidden_states.shape
        Skv = encoder_hidden_states.shape[1]
        D = gq.shape[0]
        H = Wq.shape[1] // D
        scale = 1.0 / np.sqrt(D)
        q = (hidden_states @ Wq).reshape(B, Sq, H, D)
        k = (encoder_hidden_states @ Wk).reshape(B, Skv, H, D)
        v = (encoder_hidden_states @ Wv).reshape(B, Skv, H, D)
        q = rmsnorm(q, gq)
        k = rmsnorm(k, gk)
        scores = jnp.einsum('bqhd,bkhd->bhqk', q, k) * scale
        attn = jax.nn.softmax(scores, axis=-1)
        out = jnp.einsum('bhqk,bkhd->bqhd', attn, v)
        out = out.reshape(B, Sq, H * D)
        return out @ Wo

    def _L0_attn_ref(x, Wq, Wk, Wv, Wo):
        import jax, jax.numpy as jnp
        import numpy as np
        HEADS = 16
        B, T, _ = x.shape
        H = HEADS
        Dh = Wq.shape[1] // H
        q = (x @ Wq).reshape(B, T, H, Dh)
        k = (x @ Wk).reshape(B, T, H, Dh)
        v = (x @ Wv).reshape(B, T, H, Dh)
        scores = jnp.einsum('bthd,bshd->bhts', q, k)
        mask = jnp.tril(jnp.ones((T, T), dtype=scores.dtype))
        scores = scores * mask
        attn = jax.nn.softmax(scores / T ** 0.5, axis=-1)
        out = jnp.einsum('bhts,bshd->bthd', attn, v).reshape(B, T, H * Dh)
        return out @ Wo

    def _L0_ffn_ref(hidden_states, gate_w, w_gate, w_up, w_down, sw_gate, sw_up, sw_down):
        import jax, jax.numpy as jnp
        import numpy as np
        B, S, D = (4, 128, 512)
        E, K, H = (8, 2, 352)
        HS = 2 * 352
        ALPHA = 0.001
        W_SCALE = 0.02

        def _moe_forward(hidden_states, gate_w, w_gate, w_up, w_down, sw_gate, sw_up, sw_down):
            b, s, d = hidden_states.shape
            x = hidden_states.reshape(-1, d)
            T = x.shape[0]
            logits = x @ gate_w
            scores = jax.nn.softmax(logits, axis=-1)
            topk_w, topk_idx = jax.lax.top_k(scores, K)
            mask = jax.nn.one_hot(topk_idx, E, dtype=scores.dtype).sum(axis=1)
            ce = mask.mean(axis=0)
            Pi = scores.mean(axis=0)
            aux_loss = (Pi * ce * E).sum() * ALPHA
            comb = jnp.zeros((T, E), dtype=x.dtype)
            comb = comb.at[jnp.arange(T)[:, None], topk_idx].add(topk_w)
            g = jax.nn.silu(jnp.einsum('td,edh->teh', x, w_gate)) * jnp.einsum('td,edh->teh', x, w_up)
            routed = jnp.einsum('teh,ehd,te->td', g, w_down, comb)
            shared = jax.nn.silu(x @ sw_gate) * (x @ sw_up) @ sw_down
            out = (routed + shared).reshape(b, s, d)
            return (out, aux_loss)
        out, _aux = _moe_forward(hidden_states, gate_w, w_gate, w_up, w_down, sw_gate, sw_up, sw_down)
        return out
    x = x + _L0_xattn_ref(_layernorm(x, axis=-1), ctx_1024, L0_xattn_Wq, L0_xattn_Wk, L0_xattn_Wv, L0_xattn_Wo, L0_xattn_gq, L0_xattn_gk)
    x = x + _L0_attn_ref(_layernorm(x, axis=-1), L0_attn_Wq, L0_attn_Wk, L0_attn_Wv, L0_attn_Wo)
    x = x + _L0_ffn_ref(_layernorm(x, axis=-1), L0_ffn_gate_w, L0_ffn_w_gate, L0_ffn_w_up, L0_ffn_w_down, L0_ffn_sw_gate, L0_ffn_sw_up, L0_ffn_sw_down)
    return x

_drawn_inputs = setup_inputs


def setup_inputs(seed=0):
    import zlib

    import numpy as np

    out = dict(_drawn_inputs(seed))
    spreads = {'L0_xattn_gq': (1.0, 0.2), 'L0_xattn_gk': (1.0, 0.2)}
    factors = {'L0_attn_Wq': 8.0,
     'L0_attn_Wk': 8.0,
     'L0_ffn_gate_w': 6.09,
     'L0_ffn_w_gate': 5.563,
     'L0_ffn_w_up': 5.446,
     'L0_ffn_w_down': 5.432,
     'L0_ffn_sw_gate': 6.37,
     'L0_ffn_sw_up': 6.152,
     'L0_ffn_sw_down': 6.148}
    for name, (base, spread) in spreads.items():
        noise = np.random.default_rng([zlib.crc32(name.encode()), seed]).standard_normal(out[name].shape)
        drawn = base * np.exp(spread * noise) if base else spread * noise
        out[name] = jnp.asarray(drawn.astype(out[name].dtype))
    for name, factor in factors.items():
        out[name] = (out[name] * factor).astype(out[name].dtype)
    return out
```

```python
import concourse.bass as bass
from concourse import mybir
from contextlib import ExitStack

fp32 = mybir.dt.float32
fp16 = mybir.dt.float16
u32 = mybir.dt.uint32
ALU = mybir.AluOpType
ACT = mybir.ActivationFunctionType
AX = mybir.AxisListType

P = 128
TOK, DM = 256, 512
QT = TOK // P
CT = DM // P
CTX, CD = 4096, 256
KC = CD // P
XH, XD = 16, 128
NTILE = CTX // P
PER = 4
CHUNK = PER * P
NCH = NTILE // PER
TOTAL = XH * NCH
SLOTS = 2 * NCH
EXP_LAG, PV_LAG = NCH + 1, NCH + 2
WS = 64.0
KS = 0.5
SHIFT = 10.0
EPS = 1e-5
SH, SD = 16, 32
HPT = P // SD
NE, HID = 8, 352
ALLE = NE + 2
HT = [128, 128, 96]
ESLOT = 4
WQG = 4


class Signals:

    def __init__(self, sem):
        self.x_in = sem("x_in")
        self.gains_in = sem("gains_in")
        self.stage_in0 = sem("stage_in0")
        self.stage_in1 = sem("stage_in1")
        self.stage_in2 = sem("stage_in2")
        self.x1_in = sem("x1_in")
        self.wo_in = sem("wo_in")
        self.watt_in = sem("watt_in")
        self.gate_in = sem("gate_in")
        self.e_in0 = sem("e_in0")
        self.e_in1 = sem("e_in1")
        self.e_in2 = sem("e_in2")
        self.e_in3 = sem("e_in3")
        self.out_done = sem("out_done")
        self.consts = sem("consts")
        self.stage_hi = sem("stage_hi")
        self.stage_lo = sem("stage_lo")
        self.dve_step = sem("dve_step")
        self.ln_stats = sem("ln_stats")
        self.ln_rstd = sem("ln_rstd")
        self.ln_xn = sem("ln_xn")
        self.ln_T = sem("ln_T")
        self.ln_hi = sem("ln_hi")
        self.ln_out = sem("ln_out")
        self.q_psum = sem("q_psum")
        self.q_raw = sem("q_raw")
        self.q_ss = sem("q_ss")
        self.q_rs = sem("q_rs")
        self.q_scaled = sem("q_scaled")
        self.q_T = sem("q_T")
        self.q_hi = sem("q_hi")
        self.q_lo = sem("q_lo")
        self.c_T = sem("c_T")
        self.c_hi = sem("c_hi")
        self.c_lo = sem("c_lo")
        self.k_psum = sem("k_psum")
        self.k_sq = sem("k_sq")
        self.k_hi = sem("k_hi")
        self.k_lo = sem("k_lo")
        self.sq_split = sem("sq_split")
        self.norm_psum = sem("norm_psum")
        self.norm_read = sem("norm_read")
        self.r_ready = sem("r_ready")
        self.s_psum = sem("s_psum")
        self.s_kept = sem("s_kept")
        self.s_shifted = sem("s_shifted")
        self.p_hi = sem("p_hi")
        self.p_full = sem("p_full")
        self.p_lo = sem("p_lo")
        self.pv_done = sem("pv_done")
        self.max_done = sem("max_done")
        self.max_T = sem("max_T")
        self.max_q = sem("max_q")
        self.max_diag = sem("max_diag")
        self.max_b = sem("max_b")
        self.max_row = sem("max_row")
        self.t_norm = sem("t_norm")
        self.t_T = sem("t_T")
        self.t_hi = sem("t_hi")
        self.t_lo = sem("t_lo")
        self.o_psum = sem("o_psum")
        self.o_kept = sem("o_kept")
        self.y_psum = sem("y_psum")
        self.qk_psum = sem("qk_psum")
        self.q_kept = sem("q_kept")
        self.k_kept = sem("k_kept")
        self.v_kept = sem("v_kept")
        self.mask_done = sem("mask_done")
        self.a_psum = sem("a_psum")
        self.a_masked = sem("a_masked")
        self.a_exp = sem("a_exp")
        self.a_T = sem("a_T")
        self.a_Tkept = sem("a_Tkept")
        self.ao_psum = sem("ao_psum")
        self.an_done = sem("an_done")
        self.an_T = sem("an_T")
        self.an_kept = sem("an_kept")
        self.ay_psum = sem("ay_psum")
        self.g_psum = sem("g_psum")
        self.gate_max = sem("gate_max")
        self.g_exp = sem("g_exp")
        self.h_psum = sem("h_psum")
        self.h_silu = sem("h_silu")
        self.h_kept = sem("h_kept")
        self.d_psum = sem("d_psum")
        self.moe_acc = sem("moe_acc")


def perceiver_layer(nc, x, ctx, wq, wk, wv, wo, gq, gk, swq, swk, swv, swo,
                    gate_w, w_gate, w_up, w_down, sw_gate, sw_up, sw_down, out):
    stack = ExitStack()
    with stack:
        def sem(name):
            return stack.enter_context(nc.semaphore(name))

        def pool_of(st):
            return lambda name, shape, dt: st.enter_context(nc.sbuf_tensor(name, shape, dt))

        keep = pool_of(stack)
        ident = keep("ident", [P, P], fp32)
        ones = keep("ones", [P, P], fp32)
        ones16 = keep("ones16", [P, 2], fp16)
        half_neg = keep("half_neg", [P, 32], fp32)
        ggT = keep("ggT", [P, 4], fp32)
        stats = keep("stats", [P, QT, 6], fp32)
        moments = keep("moments", [P, QT, 2], fp32)
        rstd = keep("rstd", [P, QT], fp32)
        q16 = keep("q16", [P, XH, 2, TOK], fp16)
        o32 = q16[:, :, :, :].rearrange("p h a q -> p (h a q)").bitcast(fp32).rearrange(
            "p (h q) -> p h q", h=XH)

        main = ExitStack()
        buf = pool_of(main)
        ctxT = buf("ctxT", [P, 2, KC, CTX], fp16)
        ctx_hi = buf("ctx_hi", [P, NTILE, CD + 2], fp16)
        ctx_lo = buf("ctx_lo", [P, NTILE, CD], fp16)
        wk16 = buf("wk16", [P, 2, KC, XH * XD], fp16)
        wv16 = buf("wv16", [P, 2, KC, XH * XD], fp16)
        k16 = buf("k16", [P, 2, 2, CHUNK], fp16)
        ksq = buf("ksq", [P, CHUNK], fp32)
        ksq16 = buf("ksq16", [P, 2, 2, CHUNK], fp16)
        p16 = buf("p16", [P, 2, 2, PER, TOK], fp16)
        norm = buf("norm", [P, 2, PER], fp32)
        r_key = buf("r_key", [P, 2, PER], fp32)
        runmax = buf("runmax", [P, PER, TOK], fp32)
        foldmax = buf("foldmax", [P, TOK], fp32)
        maxq = buf("maxq", [P, QT], fp32)
        diag = buf("diag", [P, QT, P], fp32)
        maxrow = buf("maxrow", [P, TOK], fp32)
        rsum = buf("rsum", [P, QT], fp32)
        tn = buf("tn", [P, QT, CD], fp32)
        tT16 = buf("tT16", [P, 2, KC, TOK], fp16)
        scores_at = nc.sbuf_base
        scores = buf("scores", [P, SLOTS, PER, TOK], fp32)
        main_end = nc.sbuf_base
        main.close()

        pre = ExitStack()
        pad = pre.enter_context(nc.sbuf_tensor("pad", [P, (scores_at - nc.sbuf_base) // 4], fp32))
        buf = pool_of(pre)
        x0 = buf("x0", [P, QT, DM], fp32)
        xn0T = buf("xn0T", [P, 2, CT, TOK], fp16)
        STG = 3
        stage = [buf(f"stage{i}", [P, 2048], fp32) for i in range(STG)]
        wq16 = buf("wq16", [P, 2, 2, CT, DM], fp16)
        q32 = buf("q32", [P, QT, XH, XD], fp32)
        assert nc.sbuf_base <= main_end, (nc.sbuf_base, main_end)
        pre.close()
        qsq = runmax[:, :, :].rearrange("p a q -> p (a q)")[:, 0:DM]
        tail = ExitStack()
        buf = pool_of(tail)
        x1 = buf("x1", [P, QT, DM], fp32)
        wo_x = buf("wo_x", [P, XH, DM], fp32)
        w_att = [buf(f"w_att{i}", [P, CT, DM], fp32) for i in range(4)]
        gate_sb = buf("gate_sb", [P, CT, NE], fp32)
        xn = buf("xn", [P, QT, DM], fp32)
        xnT = buf("xnT", [P, CT, TOK], fp32)
        aq = buf("aq", [P, CT, TOK], fp32)
        ak = buf("ak", [P, CT, TOK], fp32)
        av = buf("av", [P, QT, DM], fp32)
        mask = buf("mask", [P, QT, TOK], fp32)
        sm = buf("sm", [P, 2, QT, TOK], fp32)
        pr = buf("pr", [P, 2, QT, TOK], fp32)
        prT = buf("prT", [P, 2, QT, TOK], fp32)
        nmax = buf("nmax", [P, SH, QT], fp32)
        nbias = buf("nbias", [P, SH, QT], fp32)
        den = buf("den", [P, SH, QT], fp32)
        rden = buf("rden", [P, SH, QT], fp32)
        an = buf("an", [P, QT, DM], fp32)
        anT = buf("anT", [P, CT, TOK], fp32)
        lg = buf("lg", [P, QT, NE], fp32)
        gmax = buf("gmax", [P, QT], fp32)
        gsum = buf("gsum", [P, QT], fp32)
        grs = buf("grs", [P, QT], fp32)
        probs = buf("probs", [P, QT, NE], fp32)
        top = buf("top", [P, QT, 8], fp32)
        topi = buf("topi", [P, QT, 8], u32)
        topf = buf("topf", [P, QT, 8], fp32)
        lane = buf("lane", [P, NE], fp32)
        pick = buf("pick", [P, QT, 2, NE], fp32)
        comb = buf("comb", [P, QT, ALLE], fp32)
        wg_e = [buf(f"wg_e{i}", [P, CT, HID], fp32) for i in range(ESLOT)]
        wu_e = [buf(f"wu_e{i}", [P, CT, HID], fp32) for i in range(ESLOT)]
        wd_e = [buf(f"wd_e{i}", [P, len(HT), DM], fp32) for i in range(ESLOT)]
        silu = buf("silu", [P, 2, TOK], fp32)
        hT = buf("hT", [P, 2, len(HT), TOK], fp32)
        tail.close()

        bank = [stack.enter_context(nc.psum_tensor(f"bank{i}", [P, 512], fp32)) for i in range(8)]
        K_BANK, S_BANK, T_BANK, NORM_BANK, MISC = (0, 1), (2, 3), (4, 5), 6, 7

        s = Signals(sem)
        stage_in = [s.stage_in0, s.stage_in1, s.stage_in2]
        e_in = [s.e_in0, s.e_in1, s.e_in2, s.e_in3]

        block = stack.enter_context(nc.Block())

        def due(value):
            return not isinstance(value, int) or value > 0

        ctx_v = ctx.rearrange("(p t) c -> p t c", p=P)
        LOADS = ([("wq", g) for g in range(WQG)] + [("ctx", g) for g in range(4)] +
                 [("wk", g) for g in range(2)] + [("wv", g) for g in range(2)])

        def staged(kind, g):
            if kind == "wq":
                return wq.rearrange("(t p) n -> p t n", p=P)[:, :, g * DM:(g + 1) * DM]
            if kind == "ctx":
                return ctx_v[:, g * 8:(g + 1) * 8, :]
            w = wk if kind == "wk" else wv
            return w.rearrange("(t p) n -> p t n", p=P)[:, :, g * 1024:(g + 1) * 1024]

        def stage_view(i, kind):
            t = {"wq": CT, "ctx": 8, "wk": KC, "wv": KC}[kind]
            return stage[i % STG][:, :].rearrange("p (t n) -> p t n", t=t)

        def stage_parts(kind, g):
            if kind == "wq":
                return wq16[:, g % 2, 0, :, :], wq16[:, g % 2, 1, :, :]
            if kind == "ctx":
                return ctx_hi[:, g * 8:(g + 1) * 8, 0:CD], ctx_lo[:, g * 8:(g + 1) * 8, :]
            w = wk16 if kind == "wk" else wv16
            return w[:, 0, :, g * 1024:(g + 1) * 1024], w[:, 1, :, g * 1024:(g + 1) * 1024]

        def in_loops(eng, step, lo_peel, hi_peel, last):
            for n in range(*lo_peel):
                step(0, 0, n)
            with eng.Fori(hi_peel[0] // NCH, hi_peel[1] // NCH, 2) as hb:
                for i in range(SLOTS):
                    step(hb * NCH, hb, i)
            for i in range(last - hi_peel[1]):
                step(hi_peel[1], hi_peel[1] // NCH, i)

        def pipeline(eng, step):
            in_loops(eng, step, (-2, SLOTS), (SLOTS, TOTAL - SLOTS), TOTAL + PV_LAG + 3)

        def active(base, i, off):
            return not isinstance(base, int) or 0 <= base + i + off < TOTAL

        def head_ended(base, i):
            return not isinstance(base, int) or 1 <= (base + i - PV_LAG) // NCH <= XH

        @block.sync
        def _(sp):
            sp.dma_start(x0[:, :, :], x.rearrange("b (t p) d -> p (b t) d", p=P)).then_inc(s.x_in, 16)
            sp.dma_start(ggT[:, 0:1], gq.rearrange("(p a) -> p a", a=1)).then_inc(s.gains_in, 16)
            sp.dma_start(ggT[:, 1:2], gk.rearrange("(p a) -> p a", a=1)).then_inc(s.gains_in, 16)
            ctx_tiles = 0
            for i, (kind, g) in enumerate(LOADS):
                if i >= STG:
                    sp.wait_ge(s.stage_hi, i - STG + 1)
                    sp.wait_ge(s.stage_lo, i - STG + 1)
                    if LOADS[i - STG][0] == "ctx":
                        ctx_tiles += 8
                        sp.wait_ge(s.c_T, ctx_tiles // 2)
                sp.dma_start(stage_view(i, kind), staged(kind, g)).then_inc(stage_in[i % STG], 16)

            sp.wait_ge(s.pv_done, TOTAL)
            sp.wait_ge(s.o_psum, XH)
            sp.dma_start(wo_x[:, :, :], wo.rearrange("(h p) n -> p h n", p=P)).then_inc(s.wo_in, 16)
            sp.dma_start(x1[:, :, :], x.rearrange("b (t p) d -> p (b t) d", p=P)).then_inc(s.x1_in, 16)
            for w, dst in zip((swq, swk, swv, swo), w_att):
                sp.dma_start(dst[:, :, :], w.rearrange("(t p) n -> p t n", p=P)).then_inc(s.watt_in, 16)
            sp.dma_start(gate_sb[:, :, :], gate_w.rearrange("(t p) n -> p t n", p=P)).then_inc(s.gate_in, 16)
            for e in range(ALLE):
                if e >= ESLOT:
                    sp.wait_ge(s.d_psum, (e - ESLOT + 1) * QT)
                j = e % ESLOT
                if e < NE:
                    parts = (w_gate[e], w_up[e], w_down[e])
                else:
                    a = (e - NE) * HID
                    parts = (sw_gate[:, a:a + HID], sw_up[:, a:a + HID], sw_down[a:a + HID, :])
                sp.dma_start(wg_e[j][:, :, :], parts[0].rearrange("(t p) n -> p t n", p=P)).then_inc(e_in[j], 16)
                sp.dma_start(wu_e[j][:, :, :], parts[1].rearrange("(t p) n -> p t n", p=P)).then_inc(e_in[j], 16)
                sp.dma_start(wd_e[j][:, 0:2, :],
                             parts[2][0:2 * P, :].rearrange("(t p) n -> p t n", p=P)).then_inc(e_in[j], 16)
                sp.dma_start(wd_e[j][0:HT[2], 2, :], parts[2][2 * P:HID, :]).then_inc(e_in[j], 16)
            sp.wait_ge(s.moe_acc, ALLE * QT)
            sp.dma_start(out.rearrange("b (t p) d -> p (b t) d", p=P), x1[:, :, :]).then_inc(s.out_done, 16)
            sp.wait_ge(s.out_done, 16)

        @block.gpsimd
        def _(pool):
            pool.memset(ident[:, :], 0.0).then_inc(s.consts, 1)
            pool.wait_ge(s.consts, 1)
            pool.affine_select(out=ident[:, :], in_=ident[:, :], compare_op=ALU.not_equal, fill=1.0, base=0,
                               pattern=[[-1, P]], channel_multiplier=1).then_inc(s.consts, 1)
            pool.memset(ones[:, :], 1.0).then_inc(s.consts, 1)
            pool.memset(ones16[:, :], 1.0).then_inc(s.consts, 1)
            pool.memset(half_neg[:, :], -0.5).then_inc(s.consts, 1)
            pool.wait_ge(s.consts, 5)

            def ln_pool(k):
                pool.wait_ge(s.ln_stats, k + 1)
                pool.tensor_tensor(out=rstd[:, :], in0=moments[:, :, 1], in1=half_neg[:, 0:QT],
                                   op=ALU.pow).then_inc(s.ln_rstd, 1)

            ln_pool(0)
            pool.wait_ge(s.q_ss, 1)
            for t in range(QT):
                pool.tensor_tensor(out=foldmax[:, t * XH:(t + 1) * XH], in0=diag[:, 0, t * XH:(t + 1) * XH], in1=half_neg[:, 0:XH],
                                   op=ALU.pow).then_inc(s.q_rs, 1)

            def step(base, hb, i):
                n = base + i
                if active(base, i, 2):
                    a = (i + 2) % 2
                    pool.wait_ge(s.k_sq, n + 3)
                    if not isinstance(base, int) or n + 2 >= 2:
                        pool.wait_ge(s.norm_psum, n + 1)
                    pool.tensor_tensor(out=ksq16[:, a, 0, :], in0=ksq[:, :], in1=ones[:, 0:1].to_broadcast([P, CHUNK]),
                                       op=ALU.mult).then_inc(s.sq_split, 1)
                    pool.wait_ge(s.sq_split, (n + 2) * 2 + 1)
                    pool.tensor_tensor(out=ksq16[:, a, 1, :], in0=ksq[:, :], in1=ksq16[:, a, 0, :],
                                       op=ALU.subtract).then_inc(s.sq_split, 1)
                if active(base, i, 1):
                    a = (i + 1) % 2
                    pool.wait_ge(s.norm_read, n + 2)
                    if not isinstance(base, int) or n + 1 >= 2:
                        pool.wait_ge(s.s_kept, (n - 1 + 1) * PER)
                    pool.tensor_tensor(out=r_key[:, a, :], in0=norm[:, a, :], in1=half_neg[:, 0:PER],
                                       op=ALU.pow).then_inc(s.r_ready, 1)

            pipeline(pool, step)

            pool.wait_ge(s.pv_done, TOTAL)
            pool.wait_ge(s.o_psum, XH)
            pool.memset(mask[:, :, :], 1.0).then_inc(s.mask_done, 1)
            pool.iota(lane[:, :], [[1, NE]], channel_multiplier=0, allow_small_or_imprecise_dtypes=True
                      ).then_inc(s.mask_done, 1)
            pool.memset(comb[:, :, :], 1.0).then_inc(s.mask_done, 1)
            pool.wait_ge(s.mask_done, 3)
            pool.affine_select(out=mask[:, :, :], in_=mask[:, :, :], compare_op=ALU.is_ge, fill=0.0, base=0,
                               pattern=[[P, QT], [-1, TOK]], channel_multiplier=1).then_inc(s.mask_done, 1)
            ln_pool(1)
            ln_pool(2)

        @block.scalar
        def _(act):
            act_ = nc.scalar
            for t in range(2):
                act.wait_ge(s.ln_T, t + 1)
                act_.activation(xn0T[:, 0, 2 * t:2 * t + 2, :],
                                bank[t][:, :].rearrange("p (a q) -> p a q", a=2), ACT.Copy
                                ).then_inc(s.ln_hi, 1)
            qe = [0]

            def stage_hi(i):
                kind, g = LOADS[i]
                act.wait_ge(stage_in[i % STG], 16 * (i // STG + 1))
                if kind == "wq" and g >= 2:
                    act.wait_ge(s.q_psum, (g - 1) * QT)
                act_.activation(stage_parts(kind, g)[0], stage_view(i, kind), ACT.Copy,
                                scale=1.0 if kind == "ctx" else WS).then_inc(s.stage_hi, 1)

            def q_evac(g):
                for t in range(QT):
                    act.wait_ge(s.q_psum, g * QT + t + 1)
                    act_.activation(q32[:, t, 4 * g:4 * g + 4, :],
                                    bank[2 + (g * QT + t) % 2][:, :].rearrange("p (h d) -> p h d", h=4),
                                    ACT.Copy, scale=1.0 / WS).then_inc(s.q_raw, 1)

            for i in range(4):
                stage_hi(i)
                if i >= 1:
                    q_evac(i - 1)
            for i in range(4, 8):
                stage_hi(i)
                if i == 4:
                    q_evac(3)
                for u in range(4):
                    b = (i - 4) * 4 + u
                    act.wait_ge(s.c_T, b + 1)
                    act_.activation(ctxT[:, 0, :, b * 2 * P:(b + 1) * 2 * P],
                                    bank[4 + b % 2][:, :].rearrange("p (c r) -> p c r", c=KC),
                                    ACT.Copy).then_inc(s.c_hi, 1)
            for i in range(8, 12):
                stage_hi(i)
            for b in range(XH // 2):
                act.wait_ge(s.q_T, b + 1)
                act_.activation(q16[:, 2 * b:2 * b + 2, 0, :],
                                bank[6 + b % 2][:, :].rearrange("p (h q) -> p h q", h=2),
                                ACT.Copy, scale=ggT[:, 2:3]).then_inc(s.q_hi, 1)

            def step(base, hb, i):
                n = base + i
                if active(base, i, 2):
                    a = (i + 2) % 2
                    act.wait_ge(s.k_psum, n + 3)
                    if due((n + 2) * 2):
                        act.wait_ge(s.sq_split, (n + 2) * 2)
                    act_.activation(ksq[:, :], bank[K_BANK[a]][:, :], ACT.Square,
                                    scale=KS / WS).then_inc(s.k_sq, 1)
                    if not isinstance(base, int) or n >= 0:
                        act.wait_ge(s.s_psum, (n + 1) * 2)
                    act_.activation(k16[:, a, 0, :], bank[K_BANK[a]][:, :], ACT.Copy,
                                    scale=1.0 / WS).then_inc(s.k_hi, 1)
                if active(base, i, 0):
                    a = i % 2
                    slot = i % SLOTS
                    act.wait_ge(s.r_ready, n + 1)
                    if not isinstance(base, int) or n >= SLOTS:
                        act.wait_ge(s.p_lo, n - SLOTS + 1)
                    for b in range(2):
                        act.wait_ge(s.s_psum, n * 2 + b + 1)
                        for k in range(2):
                            kt = 2 * b + k
                            act_.activation(scores[:, slot, kt, :], bank[S_BANK[b]][:, k * TOK:(k + 1) * TOK],
                                            ACT.Copy, scale=r_key[:, a, kt:kt + 1]).then_inc(s.s_kept, 1)
                if active(base, i, -EXP_LAG):
                    v = n - EXP_LAG
                    slot = (i - EXP_LAG) % SLOTS
                    a = (i - EXP_LAG) % 2
                    act.wait_ge(s.s_shifted, v + 1)
                    if not isinstance(base, int) or v >= 2:
                        act.wait_ge(s.pv_done, v - 1)
                    act_.activation(p16[:, a, 0, :, :], scores[:, slot, :, :], ACT.Exp).then_inc(s.p_hi, 1)
                    act_.activation(scores[:, slot, :, :], scores[:, slot, :, :], ACT.Exp).then_inc(s.p_full, 1)
                if (i - PV_LAG) % NCH == 1 and head_ended(base, i):
                    h = hb + (i - PV_LAG - 1) // NCH
                    act.wait_ge(s.t_T, h)
                    act_.activation(tT16[:, 0, :, :], bank[MISC][:, :].rearrange("p (c q) -> p c q", c=KC),
                                    ACT.Copy).then_inc(s.t_hi, 1)

            pipeline(act, step)

            act.wait_ge(s.qk_psum, CT)
            for m in range(2):
                act_.activation(aq[:, 2 * m:2 * m + 2, :],
                                bank[m][:, :].rearrange("p (a q) -> p a q", a=2), ACT.Copy
                                ).then_inc(s.q_kept, 1)
            for h in range(SH):
                a = h % 2
                act.wait_ge(s.a_masked, h + 1)
                if h >= 2:
                    act.wait_ge(s.a_T, h - 1)
                for t in range(QT):
                    act_.activation(pr[:, a, t, :], sm[:, a, t, :], ACT.Exp, scale=1.0 / TOK ** 0.5,
                                    bias=nbias[:, h, t:t + 1], accum_out=den[:, h, t:t + 1]
                                    ).then_inc(s.a_exp, 1)
            for t in range(QT):
                act.wait_ge(s.g_psum, t + 1)
            act.wait_ge(s.gate_max, 1)
            for t in range(QT):
                act_.activation(probs[:, t, :], lg[:, t, :], ACT.Exp, bias=gmax[:, t:t + 1],
                                accum_out=gsum[:, t:t + 1]).then_inc(s.g_exp, 1)
            for e in range(ALLE):
                for j, rows in enumerate(HT):
                    u = e * len(HT) + j
                    act.wait_ge(s.h_psum, u + 1)
                    if u >= 2:
                        act.wait_ge(s.h_kept, u - 1)
                    act_.activation(silu[0:rows, u % 2, :], bank[u % 3][0:rows, 0:TOK], ACT.Silu
                                    ).then_inc(s.h_silu, 1)

        @block.vector
        def _(dve):
            vec = nc.vector

            def chained(ins, count):
                ins.then_inc(s.dve_step, 1)
                dve.wait_ge(s.dve_step, count)

            steps = [0]

            def then(ins):
                steps[0] += 1
                chained(ins, steps[0])

            def ln_dve(k, src, dst):
                for t in range(QT):
                    last = vec.bn_stats(out=stats[:, t, :], in_=src[:, t, :])
                then(last)
                for t in range(QT):
                    last = vec.bn_aggr(out=moments[:, t, :], in_=stats[:, t, :])
                then(last)
                vec.tensor_scalar(moments[:, :, 1], moments[:, :, 1], EPS, None, ALU.add
                                  ).then_inc(s.ln_stats, 1)
                dve.wait_ge(s.ln_rstd, k + 1)
                for t in range(QT):
                    vec.tensor_scalar(dst[:, t, :], src[:, t, :], moments[:, t, 0:1], rstd[:, t:t + 1],
                                      ALU.subtract, ALU.mult).then_inc(s.ln_xn, 1)

            vec.memset(ctx_hi[:, :, CD:CD + 2], 1.0).then_inc(s.o_kept, 1)
            dve.wait_ge(s.gains_in, 32)
            then(vec.tensor_tensor(ggT[:, 2:3], ggT[:, 0:1], ggT[:, 1:2], ALU.mult))
            dve.wait_ge(s.x_in, 16)
            ln_dve(0, x0, x0)
            for t in range(2):
                dve.wait_ge(s.ln_hi, t + 1)
                vec.tensor_tensor(xn0T[:, 1, 2 * t:2 * t + 2, :],
                                  bank[t][:, :].rearrange("p (a q) -> p a q", a=2),
                                  xn0T[:, 0, 2 * t:2 * t + 2, :], ALU.subtract).then_inc(s.ln_out, 1)
                if t == 0:
                    dve.wait_ge(s.ln_T, 2)

            def stage_lo(i):
                kind, g = LOADS[i]
                dve.wait_ge(s.stage_hi, i + 1)
                hi, lo = stage_parts(kind, g)
                vec.scalar_tensor_tensor(out=lo, in0=stage_view(i, kind), scalar=1.0 if kind == "ctx" else WS,
                                         in1=hi, op0=ALU.mult, op1=ALU.subtract).then_inc(s.stage_lo, 1)

            def q_sums(g):
                for t in range(QT):
                    dve.wait_ge(s.q_raw, g * QT + t + 1)
                    qg = q32[:, t, 4 * g:4 * g + 4, :]
                    sq = qsq.rearrange("p (h d) -> p h d", h=4)
                    then(vec.tensor_tensor(sq, qg, qg, ALU.mult))
                    then(vec.tensor_reduce(diag[:, 0, t * XH + 4 * g:t * XH + 4 * g + 4], sq, AX.X, ALU.add))

            for i in range(4):
                stage_lo(i)
                if i >= 1:
                    q_sums(i - 1)
            for i in range(4, 8):
                stage_lo(i)
                if i == 4:
                    q_sums(3)
                    vec.tensor_scalar(diag[:, 0, 0:QT * XH], diag[:, 0, 0:QT * XH], 1.0 / XD, EPS,
                                      ALU.mult, ALU.add).then_inc(s.q_ss, 1)
                for u in range(4):
                    b = (i - 4) * 4 + u
                    dve.wait_ge(s.c_hi, b + 1)
                    vec.tensor_tensor(ctxT[:, 1, :, b * 2 * P:(b + 1) * 2 * P],
                                      bank[4 + b % 2][:, :].rearrange("p (c r) -> p c r", c=KC),
                                      ctxT[:, 0, :, b * 2 * P:(b + 1) * 2 * P], ALU.subtract
                                      ).then_inc(s.c_lo, 1)
                if i == 4:
                    dve.wait_ge(s.q_rs, QT)
                    for t in range(QT):
                        last = vec.tensor_tensor(q32[:, t, :, :], q32[:, t, :, :],
                                                 foldmax[:, t * XH:(t + 1) * XH].unsqueeze(2).to_broadcast(
                                                     [P, XH, XD]), ALU.mult)
                    last.then_inc(s.q_scaled, 1)
            for i in range(8, 12):
                stage_lo(i)
            for b in range(XH // 2):
                dve.wait_ge(s.q_hi, b + 1)
                vec.scalar_tensor_tensor(out=q16[:, 2 * b:2 * b + 2, 1, :],
                                         in0=bank[6 + b % 2][:, :].rearrange("p (h q) -> p h q", h=2),
                                         scalar=ggT[:, 2:3], in1=q16[:, 2 * b:2 * b + 2, 0, :],
                                         op0=ALU.mult, op1=ALU.subtract).then_inc(s.q_lo, 1)

            def step(base, hb, i):
                n = base + i
                if (i - PV_LAG) % NCH == 0 and head_ended(base, i):
                    h = hb + (i - PV_LAG) // NCH
                    dve.wait_ge(s.pv_done, h * NCH)
                    for t in range(QT):
                        last = vec.reciprocal(rsum[:, t:t + 1], bank[T_BANK[t]][:, CD:CD + 1])
                    last.then_inc(s.t_norm, 1)
                    dve.wait_ge(s.t_norm, 3 * h - 2)
                    for t in range(QT):
                        vec.tensor_scalar(tn[:, t, :], bank[T_BANK[t]][:, 0:CD], rsum[:, t:t + 1], None,
                                          ALU.mult).then_inc(s.t_norm, 1)
                if i % NCH == 1 and active(base, i, -2):
                    h = hb + i // NCH - 1
                    dve.wait_ge(s.max_b, h + 1)
                    vec.tensor_scalar(maxrow[:, :], bank[MISC][:, 0:TOK], -SHIFT, None, ALU.add
                                      ).then_inc(s.max_row, 1)
                if active(base, i, -EXP_LAG):
                    v = n - EXP_LAG
                    slot = (i - EXP_LAG) % SLOTS
                    dve.wait_ge(s.max_row, hb + (i - EXP_LAG) // NCH + 1)
                    vec.tensor_tensor(scores[:, slot, :, :], scores[:, slot, :, :],
                                      maxrow[:, :].unsqueeze(1).to_broadcast([P, PER, TOK]),
                                      ALU.subtract).then_inc(s.s_shifted, 1)
                if active(base, i, 2):
                    a = (i + 2) % 2
                    dve.wait_ge(s.k_hi, n + 3)
                    vec.scalar_tensor_tensor(out=k16[:, a, 1, :], in0=bank[K_BANK[a]][:, :], scalar=1.0 / WS,
                                             in1=k16[:, a, 0, :], op0=ALU.mult, op1=ALU.subtract
                                             ).then_inc(s.k_lo, 1)
                if active(base, i, 1):
                    a = (i + 1) % 2
                    dve.wait_ge(s.norm_psum, n + 2)
                    if not isinstance(base, int) or n + 1 >= 2:
                        dve.wait_ge(s.r_ready, n)
                    vec.tensor_scalar(norm[:, a, :], bank[NORM_BANK][:, a * PER:(a + 1) * PER],
                                      1.0 / KS ** 2, XD * EPS, ALU.mult, ALU.add).then_inc(s.norm_read, 1)
                if active(base, i, 0):
                    j, slot = i % NCH, i % SLOTS
                    if j:
                        dve.wait_ge(s.s_kept, (n + 1) * PER)
                        first = scores[:, slot - 1, :, :] if j == 1 else runmax[:, :, :]
                        vec.tensor_tensor(runmax[:, :, :], first, scores[:, slot, :, :], ALU.max
                                          ).then_inc(s.max_done, 1)
                    if j == NCH - 1:
                        h = hb + i // NCH
                        done = h * (NCH + 1) + NCH - 1
                        dve.wait_ge(s.max_done, done)
                        vec.tensor_tensor(runmax[:, 0:2, :], runmax[:, 0:2, :], runmax[:, 2:4, :], ALU.max
                                          ).then_inc(s.max_done, 1)
                        dve.wait_ge(s.max_done, done + 1)
                        if not isinstance(base, int) or h >= 1:
                            dve.wait_ge(s.max_T, h)
                        vec.tensor_tensor(foldmax[:, :], runmax[:, 0, :], runmax[:, 1, :], ALU.max
                                          ).then_inc(s.max_done, 1)
                    elif j >= 1:
                        done = (hb + i // NCH) * (NCH + 1) + j
                        dve.wait_ge(s.max_done, done)
                if i % NCH == 0 and active(base, i, -1):
                    h = hb + i // NCH - 1
                    dve.wait_ge(s.max_T, h + 1)
                    vec.tensor_reduce(maxq[:, :], bank[MISC][:, 0:TOK].rearrange("p (t r) -> p t r", t=QT),
                                      AX.X, ALU.max).then_inc(s.max_q, 1)
                    dve.wait_ge(s.max_q, h + 1)
                    for t in range(QT):
                        last = vec.tensor_scalar(diag[:, t, :], ident[:, :], maxq[:, t:t + 1], None, ALU.mult)
                    last.then_inc(s.max_diag, 1)
                if active(base, i, -EXP_LAG):
                    a = (i - EXP_LAG) % 2
                    slot = (i - EXP_LAG) % SLOTS
                    dve.wait_ge(s.p_full, n - EXP_LAG + 1)
                    vec.tensor_tensor(p16[:, a, 1, :, :], scores[:, slot, :, :], p16[:, a, 0, :, :], ALU.subtract
                                      ).then_inc(s.p_lo, 1)
                if (i - PV_LAG) % NCH == 1 and head_ended(base, i):
                    h = hb + (i - PV_LAG - 1) // NCH
                    dve.wait_ge(s.t_hi, h)
                    vec.tensor_tensor(tT16[:, 1, :, :], bank[MISC][:, :].rearrange("p (c q) -> p c q", c=KC),
                                      tT16[:, 0, :, :], ALU.subtract).then_inc(s.t_lo, 1)
                if (i - PV_LAG) % NCH == 2 and head_ended(base, i):
                    h = hb + (i - PV_LAG - 2) // NCH
                    dve.wait_ge(s.o_psum, h)
                    vec.tensor_scalar(o32[:, h - 1, :], bank[MISC][:, 0:TOK], 1.0 / WS, None, ALU.mult
                                      ).then_inc(s.o_kept, 1)

            pipeline(dve, step)

            dve.wait_ge(s.x1_in, 16)
            for t in range(QT):
                dve.wait_ge(s.y_psum, t + 1)
                then(vec.tensor_tensor(x1[:, t, :], bank[t][:, :], x1[:, t, :], ALU.add))
            ln_dve(1, x1, xn)

            def xT_evac(k):
                for t in range(2):
                    dve.wait_ge(s.ln_T, 2 * k + t + 1)
                    vec.tensor_copy(xnT[:, 2 * t:2 * t + 2, :],
                                    bank[6 + t][:, :].rearrange("p (a q) -> p a q", a=2)).then_inc(s.ln_out, 1)

            xT_evac(1)
            dve.wait_ge(s.qk_psum, 2 * CT)
            for m in range(2):
                vec.tensor_copy(ak[:, 2 * m:2 * m + 2, :],
                                bank[2 + m][:, :].rearrange("p (a q) -> p a q", a=2)).then_inc(s.k_kept, 1)
            for t in range(QT):
                dve.wait_ge(s.qk_psum, 2 * CT + t + 1)
                vec.tensor_copy(av[:, t, :], bank[4 + t][:, :]).then_inc(s.v_kept, 1)
            dve.wait_ge(s.mask_done, 4)

            def masked(h):
                a = h % 2
                dve.wait_ge(s.a_psum, h + 1)
                if h >= 2:
                    dve.wait_ge(s.a_exp, (h - 1) * QT)
                then(vec.tensor_tensor(sm[:, a, :, :], bank[a][:, :].rearrange("p (t q) -> p t q", t=QT),
                                       mask[:, :, :], ALU.mult))
                then(vec.tensor_reduce(nmax[:, h, :], sm[:, a, :, :], AX.X, ALU.max))
                vec.tensor_scalar(nbias[:, h, :], nmax[:, h, :], -1.0 / TOK ** 0.5, None, ALU.mult
                                  ).then_inc(s.a_masked, 1)

            def pT_evac(h):
                a = h % 2
                dve.wait_ge(s.a_T, h + 1)
                if h >= 2:
                    dve.wait_ge(s.ao_psum, h - 1)
                vec.tensor_copy(prT[:, a, :, :], bank[2 + a][:, :].rearrange("p (t q) -> p t q", t=QT)
                                ).then_inc(s.a_Tkept, 1)

            for h in range(SH + 1):
                if h < SH:
                    masked(h)
                if h >= 1:
                    pT_evac(h - 1)
            dve.wait_ge(s.a_exp, SH * QT)
            dve.wait_ge(s.ao_psum, SH)
            then(vec.reciprocal(rden[:, :, :], den[:, :, :]))
            for t in range(QT):
                vec.tensor_tensor(an[:, t, :].rearrange("p (h d) -> p h d", h=SH),
                                  bank[4 + t][:, :].rearrange("p (h d) -> p h d", h=SH),
                                  rden[:, :, t].unsqueeze(2).to_broadcast([P, SH, SD]), ALU.mult
                                  ).then_inc(s.an_done, 1)
            for t in range(2):
                dve.wait_ge(s.an_T, t + 1)
                vec.tensor_copy(anT[:, 2 * t:2 * t + 2, :],
                                bank[6 + t][:, :].rearrange("p (a q) -> p a q", a=2)).then_inc(s.an_kept, 1)
            for t in range(QT):
                dve.wait_ge(s.ay_psum, t + 1)
                then(vec.tensor_tensor(x1[:, t, :], bank[t][:, :], x1[:, t, :], ALU.add))
            ln_dve(2, x1, xn)
            xT_evac(2)
            for t in range(QT):
                dve.wait_ge(s.g_psum, t + 1)
                then(vec.tensor_copy(lg[:, t, :], bank[2 + t][:, 0:NE]))
            then(vec.tensor_reduce(gmax[:, :], lg[:, :, :], AX.X, ALU.max))
            vec.tensor_scalar(gmax[:, :], gmax[:, :], -1.0, None, ALU.mult).then_inc(s.gate_max, 1)
            dve.wait_ge(s.g_exp, QT)
            then(vec.reciprocal(grs[:, :], gsum[:, :]))
            for t in range(QT):
                then(vec.tensor_scalar(probs[:, t, :], probs[:, t, :], grs[:, t:t + 1], None, ALU.mult))
                then(vec.max(out=top[:, t, :], in_=probs[:, t, :]))
                then(vec.max_index(out=topi[:, t, :], in_max=top[:, t, :], in_values=probs[:, t, :]))
                then(vec.tensor_copy(topf[:, t, :], topi[:, t, :]))
                for c in range(2):
                    then(vec.tensor_scalar(pick[:, t, c, :], lane[:, :], topf[:, t, c:c + 1], None, ALU.is_equal))
                then(vec.tensor_tensor(pick[:, t, 0, :], pick[:, t, 0, :], pick[:, t, 1, :], ALU.add))
                then(vec.tensor_tensor(comb[:, t, 0:NE], pick[:, t, 0, :], probs[:, t, :], ALU.mult))

            def down(e):
                for t in range(QT):
                    u = e * QT + t
                    dve.wait_ge(s.d_psum, u + 1)
                    vec.scalar_tensor_tensor(out=x1[:, t, :], in0=bank[6 + t][:, :], scalar=comb[:, t, e:e + 1],
                                             in1=x1[:, t, :], op0=ALU.mult, op1=ALU.add
                                             ).then_inc(s.moe_acc, 1)
                    dve.wait_ge(s.moe_acc, u + 1)

            for e in range(ALLE):
                for j, rows in enumerate(HT):
                    u = e * len(HT) + j
                    dve.wait_ge(s.h_silu, u + 1)
                    if e >= 2 and j == 0:
                        dve.wait_ge(s.d_psum, (e - 1) * QT)
                    vec.tensor_tensor(hT[0:rows, e % 2, j, :], silu[0:rows, u % 2, :],
                                      bank[3 + u % 3][0:rows, 0:TOK], ALU.mult).then_inc(s.h_kept, 1)
                if e:
                    down(e - 1)
            down(ALLE - 1)

        @block.tensor
        def _(pe):
            mm = nc.tensor.matmul

            def split_products(out_, w_hi, w_lo, x_hi, x_lo, steps):
                last = None
                for k in steps:
                    first, final = k == steps[0], k == steps[-1]
                    mm(out_, w_hi(k), x_hi(k), start=first, stop=False)
                    mm(out_, w_hi(k), x_lo(k), start=False, stop=False)
                    last = mm(out_, w_lo(k), x_hi(k), start=False, stop=final)
                return last

            def ln_pe(k, src, banks):
                pe.wait_ge(s.ln_xn, (k + 1) * QT)
                for b in range(2):
                    for c in range(2):
                        for t in range(QT):
                            last = nc.tensor.transpose(banks[b][:, c * TOK + t * P:c * TOK + (t + 1) * P],
                                                       src[:, t, (2 * b + c) * P:(2 * b + c + 1) * P],
                                                       ident[:, :])
                    last.then_inc(s.ln_T, 1)

            pe.wait_ge(s.consts, 5)
            ln_pe(0, x0, bank[0:2])
            pe.wait_ge(s.ln_out, 2)

            def ctx_blocks(b):
                i = 4 + b // 4
                if b % 4 == 0:
                    pe.wait_ge(stage_in[i % STG], 16 * (i // STG + 1))
                if b >= 2:
                    pe.wait_ge(s.c_lo, b - 1)
                src = stage_view(i, "ctx")
                for c in range(KC):
                    for k in range(2):
                        last = nc.tensor.transpose(bank[4 + b % 2][:, c * 2 * P + k * P:c * 2 * P + (k + 1) * P],
                                                   src[:, (2 * b + k) % 8, c * P:(c + 1) * P], ident[:, :])
                last.then_inc(s.c_T, 1)

            for g in range(WQG):
                pe.wait_ge(s.stage_lo, g + 1)
                for t in range(QT):
                    u = g * QT + t
                    if u >= 2:
                        pe.wait_ge(s.q_raw, u - 1)
                    last = split_products(bank[2 + u % 2][:, :],
                                          lambda k: xn0T[:, 0, k, t * P:(t + 1) * P],
                                          lambda k: xn0T[:, 1, k, t * P:(t + 1) * P],
                                          lambda k: wq16[:, g % 2, 0, k, :],
                                          lambda k: wq16[:, g % 2, 1, k, :], range(CT))
                    last.then_inc(s.q_psum, 1)
            for b in range(NTILE // 2):
                ctx_blocks(b)
            pe.wait_ge(s.q_scaled, 1)
            for b in range(XH // 2):
                if b >= 2:
                    pe.wait_ge(s.q_lo, b - 1)
                for c in range(2):
                    for t in range(QT):
                        last = nc.tensor.transpose(bank[6 + b % 2][:, c * TOK + t * P:c * TOK + (t + 1) * P],
                                                   q32[:, t, 2 * b + c, :], ident[:, :])
                last.then_inc(s.q_T, 1)
            pe.wait_ge(s.stage_lo, len(LOADS))
            pe.wait_ge(s.q_lo, XH // 2)
            pe.wait_ge(s.c_lo, NTILE // 2)

            def head_slice(hb, i, off):
                return bass.ds((hb + (i + off) // NCH) * XD, XD)

            def step(base, hb, i):
                n = base + i
                if active(base, i, 2):
                    a, j = (i + 2) % 2, (i + 2) % NCH
                    if due(n + 1):
                        pe.wait_ge(s.k_lo, n + 1)
                    cols = slice(j * CHUNK, (j + 1) * CHUNK)
                    hs = head_slice(hb, i, 2)
                    split_products(bank[K_BANK[a]][:, :],
                                   lambda k: wk16[:, 0, k, hs], lambda k: wk16[:, 1, k, hs],
                                   lambda k: ctxT[:, 0, k, cols], lambda k: ctxT[:, 1, k, cols], range(KC)
                                   ).then_inc(s.k_psum, 1)
                if active(base, i, 1):
                    a = (i + 1) % 2
                    pe.wait_ge(s.sq_split, (n + 2) * 2)
                    if due(n + 1):
                        pe.wait_ge(s.norm_read, n + 1)
                    for kt in range(PER):
                        for part in range(2):
                            last = mm(bank[NORM_BANK][:, a * PER + kt:a * PER + kt + 1],
                                      ksq16[:, a, part, kt * P:(kt + 1) * P], ones16[:, 0:1],
                                      start=part == 0, stop=part == 1)
                    last.then_inc(s.norm_psum, 1)
                if active(base, i, 0):
                    a = i % 2
                    h = hb + i // NCH
                    pe.wait_ge(s.k_lo, n + 1)
                    for b in range(2):
                        if due(n * PER - PER + 2 * b + 2):
                            pe.wait_ge(s.s_kept, n * PER - PER + 2 * b + 2)
                        for k in range(2):
                            rows = slice((2 * b + k) * P, (2 * b + k + 1) * P)
                            dst = bank[S_BANK[b]][:, k * TOK:(k + 1) * TOK]
                            q_hi, q_lo = (q16[:, bass.ds(h, 1), part, :] for part in range(2))
                            mm(dst, k16[:, a, 0, rows], q_hi, start=True, stop=False)
                            mm(dst, k16[:, a, 0, rows], q_lo, start=False, stop=False)
                            last = mm(dst, k16[:, a, 1, rows], q_hi, start=False, stop=True)
                        last.then_inc(s.s_psum, 1)
                if i % NCH == 0 and active(base, i, -1):
                    h = hb + i // NCH - 1
                    pe.wait_ge(s.max_done, (h + 1) * (NCH + 1))
                    if due(h):
                        pe.wait_ge(s.max_row, h)
                    if due(h):
                        pe.wait_ge(s.o_kept, h)
                    for t in range(QT):
                        last = nc.tensor.transpose(bank[MISC][:, t * P:(t + 1) * P],
                                                   foldmax[:, t * P:(t + 1) * P], ident[:, :])
                    last.then_inc(s.max_T, 1)
                if active(base, i, -PV_LAG):
                    v = n - PV_LAG
                    a, j = (i - PV_LAG) % 2, (i - PV_LAG) % NCH
                    pe.wait_ge(s.p_lo, v + 1)
                    if j == 0:
                        if due((hb + (i - PV_LAG) // NCH) * 3):
                            pe.wait_ge(s.t_norm, (hb + (i - PV_LAG) // NCH) * 3)
                    for t in range(QT):
                        cols = slice(t * P, (t + 1) * P)
                        dst = bank[T_BANK[t]]
                        for kt in range(PER):
                            tile = j * PER + kt
                            mm(dst[:, 0:CD + 1], p16[:, a, 0, kt, cols], ctx_hi[:, tile, 0:CD + 1],
                               start=j == 0 and kt == 0, stop=False)
                            mm(dst[:, 0:CD], p16[:, a, 0, kt, cols], ctx_lo[:, tile, :], start=False, stop=False)
                            last = mm(dst[:, 0:CD + 1], p16[:, a, 1, kt, cols], ctx_hi[:, tile, 0:CD + 1],
                                      start=False, stop=j == NCH - 1 and kt == PER - 1)
                    last.then_inc(s.pv_done, 1)
                if i % NCH == 0 and active(base, i, -1):
                    h = hb + i // NCH - 1
                    pe.wait_ge(s.max_diag, h + 1)
                    mm(bank[MISC][:, 0:TOK], ones[:, :], diag[:, :, :], start=True, stop=True
                       ).then_inc(s.max_b, 1)
                if (i - PV_LAG) % NCH == 1 and head_ended(base, i):
                    h = hb + (i - PV_LAG - 1) // NCH
                    pe.wait_ge(s.t_norm, h * 3)
                    pe.wait_ge(s.max_row, min(h + 1, XH) if isinstance(h, int) else h + 1)
                    for c in range(KC):
                        for t in range(QT):
                            last = nc.tensor.transpose(bank[MISC][:, c * TOK + t * P:c * TOK + (t + 1) * P],
                                                       tn[:, t, c * P:(c + 1) * P], ident[:, :])
                    last.then_inc(s.t_T, 1)
                if (i - PV_LAG) % NCH == 2 and head_ended(base, i):
                    h = hb + (i - PV_LAG - 2) // NCH
                    pe.wait_ge(s.t_lo, h)
                    hs = bass.ds((h - 1) * XD, XD)
                    split_products(bank[MISC][:, 0:TOK],
                                   lambda k: wv16[:, 0, k, hs], lambda k: wv16[:, 1, k, hs],
                                   lambda k: tT16[:, 0, k, :], lambda k: tT16[:, 1, k, :], range(KC)
                                   ).then_inc(s.o_psum, 1)

            pipeline(pe, step)

            pe.wait_ge(s.o_kept, XH + 1)
            pe.wait_ge(s.wo_in, 16)
            for t in range(QT):
                for h in range(XH):
                    last = mm(bank[t][:, :], o32[:, h, t * P:(t + 1) * P], wo_x[:, h, :],
                              start=h == 0, stop=h == XH - 1)
                last.then_inc(s.y_psum, 1)
            ln_pe(1, xn, bank[6:8])
            pe.wait_ge(s.ln_out, 4)
            pe.wait_ge(s.watt_in, 64)
            for w, b0 in ((w_att[0], 0), (w_att[1], 2)):
                for m in range(CT):
                    for k in range(CT):
                        last = mm(bank[b0 + m // 2][:, (m % 2) * TOK:(m % 2 + 1) * TOK],
                                  w[:, k, m * P:(m + 1) * P], xnT[:, k, :], start=k == 0, stop=k == CT - 1)
                    last.then_inc(s.qk_psum, 1)
            for t in range(QT):
                for k in range(CT):
                    last = mm(bank[4 + t][:, :], xnT[:, k, t * P:(t + 1) * P], w_att[2][:, k, :],
                              start=k == 0, stop=k == CT - 1)
                last.then_inc(s.qk_psum, 1)

            def a_scores(h):
                m, r = h // HPT, SD * (h % HPT)
                if h == 0:
                    pe.wait_ge(s.q_kept, 2)
                    pe.wait_ge(s.k_kept, 2)
                if h >= 2:
                    pe.wait_ge(s.a_masked, h - 1)
                for t in range(QT):
                    last = mm(bank[h % 2][:, t * TOK:(t + 1) * TOK], aq[r:r + SD, m, t * P:(t + 1) * P],
                              ak[r:r + SD, m, :], start=True, stop=True)
                last.then_inc(s.a_psum, 1)

            def a_transpose(h):
                pe.wait_ge(s.a_exp, (h + 1) * QT)
                if h >= 2:
                    pe.wait_ge(s.a_Tkept, h - 1)
                for k in range(QT):
                    for t in range(QT):
                        last = nc.tensor.transpose(bank[2 + h % 2][:, k * TOK + t * P:k * TOK + (t + 1) * P],
                                                   pr[:, h % 2, t, k * P:(k + 1) * P], ident[:, :])
                last.then_inc(s.a_T, 1)

            def a_out(h):
                pe.wait_ge(s.a_Tkept, h + 1)
                if h == 0:
                    pe.wait_ge(s.v_kept, 2)
                for t in range(QT):
                    for k in range(QT):
                        last = mm(bank[4 + t][:, h * SD:(h + 1) * SD], prT[:, h % 2, k, t * P:(t + 1) * P],
                                  av[:, k, h * SD:(h + 1) * SD], start=k == 0, stop=k == QT - 1)
                last.then_inc(s.ao_psum, 1)

            for h in range(SH + 2):
                if h < SH:
                    a_scores(h)
                if 1 <= h <= SH:
                    a_transpose(h - 1)
                if h >= 2:
                    a_out(h - 2)
            pe.wait_ge(s.an_done, QT)
            for b in range(2):
                for c in range(2):
                    for t in range(QT):
                        last = nc.tensor.transpose(bank[6 + b][:, c * TOK + t * P:c * TOK + (t + 1) * P],
                                                   an[:, t, (2 * b + c) * P:(2 * b + c + 1) * P], ident[:, :])
                last.then_inc(s.an_T, 1)
            pe.wait_ge(s.an_kept, 2)
            for t in range(QT):
                for k in range(CT):
                    last = mm(bank[t][:, :], anT[:, k, t * P:(t + 1) * P], w_att[3][:, k, :],
                              start=k == 0, stop=k == CT - 1)
                last.then_inc(s.ay_psum, 1)
            ln_pe(2, xn, bank[6:8])
            pe.wait_ge(s.ln_out, 6)
            pe.wait_ge(s.gate_in, 16)
            for t in range(QT):
                for k in range(CT):
                    last = mm(bank[2 + t][:, 0:NE], xnT[:, k, t * P:(t + 1) * P], gate_sb[:, k, :],
                              start=k == 0, stop=k == CT - 1)
                last.then_inc(s.g_psum, 1)
            pe.wait_ge(s.gate_max, 1)

            def e_down(e):
                for t in range(QT):
                    pe.wait_ge(s.h_kept, (e + 1) * len(HT))
                    if due((e - 1) * QT + t + 1):
                        pe.wait_ge(s.moe_acc, (e - 1) * QT + t + 1)
                    for j, rows in enumerate(HT):
                        last = mm(bank[6 + t][:, :], hT[0:rows, e % 2, j, t * P:(t + 1) * P],
                                  wd_e[e % ESLOT][0:rows, j, :], start=j == 0, stop=j == len(HT) - 1)
                    last.then_inc(s.d_psum, 1)

            for e in range(ALLE):
                pe.wait_ge(e_in[e % ESLOT], 64 * (e // ESLOT + 1))
                for j, rows in enumerate(HT):
                    u = e * len(HT) + j
                    if due(u - 2):
                        pe.wait_ge(s.h_kept, u - 2)
                    for w, b0 in ((wu_e, 3), (wg_e, 0)):
                        for k in range(CT):
                            last = mm(bank[b0 + u % 3][0:rows, 0:TOK], w[e % ESLOT][:, k, j * P:j * P + rows],
                                      xnT[:, k, :], start=k == 0, stop=k == CT - 1)
                    last.then_inc(s.h_psum, 1)
                if e:
                    e_down(e - 1)
            e_down(ALLE - 1)


_INS = ['x', 'ctx_1024', 'L0_xattn_Wq', 'L0_xattn_Wk', 'L0_xattn_Wv', 'L0_xattn_Wo', 'L0_xattn_gq', 'L0_xattn_gk',
        'L0_attn_Wq', 'L0_attn_Wk', 'L0_attn_Wv', 'L0_attn_Wo', 'L0_ffn_gate_w', 'L0_ffn_w_gate', 'L0_ffn_w_up',
        'L0_ffn_w_down', 'L0_ffn_sw_gate', 'L0_ffn_sw_up', 'L0_ffn_sw_down']
_OUTS = [((1, 256, 512), 'float32')]


def kernel(**inputs):
    import numpy as _np
    import concourse.bacc as _bacc
    from concourse import mybir as _mybir
    from concourse.bass_utils import run_bass_kernel_spmd as _run

    nc = _bacc.Bacc("TRN2", target_bir_lowering=False, num_devices=1)
    arrays, args = {}, []
    for name in _INS:
        a = _np.ascontiguousarray(inputs[name])
        if name == 'ctx_1024':
            a = a.reshape(a.shape[1:])
        arrays[f"in_{name}_dram"] = a
        args.append(nc.dram_tensor(f"in_{name}_dram", a.shape, _mybir.dt.from_np(a.dtype), kind="ExternalInput").ap())
    for i, (shape, dtype) in enumerate(_OUTS):
        dt = _mybir.dt.from_np(_np.dtype(dtype))
        args.append(nc.dram_tensor(f"out_{i}_dram", shape, dt, kind="ExternalOutput").ap())
    perceiver_layer(nc, *args)
    r = _run(nc, [arrays], core_ids=[0])
    return r.results[0]["out_0_dram"]
```

```python
import concourse.bass as bass
from concourse import mybir
from contextlib import ExitStack

fp32 = mybir.dt.float32
fp16 = mybir.dt.float16
u32 = mybir.dt.uint32
ALU = mybir.AluOpType
ACT = mybir.ActivationFunctionType
AX = mybir.AxisListType

P = 128
TOK, DM = 256, 512
QT = TOK // P
CT = DM // P
CTX, CD = 4096, 256
KC = CD // P
XH, XD = 16, 128
NTILE = CTX // P
PER = 4
CHUNK = PER * P
NCH = NTILE // PER
TOTAL = XH * NCH
SLOTS = 2 * NCH
EXP_LAG, LO_LAG, PV_LAG = NCH + 1, NCH + 2, NCH + 3
WS = 64.0
KS = 0.5
SHIFT = 10.0
EPS = 1e-5
SH, SD = 16, 32
HPT = P // SD
NE, HID = 8, 352
ALLE = NE + 2
HT = [128, 128, 96]
WQG = 4


class Signals:

    def __init__(self, sem):
        self.x_in = sem("x_in")
        self.gains_in = sem("gains_in")
        self.stage_in0 = sem("stage_in0")
        self.stage_in1 = sem("stage_in1")
        self.stage_in2 = sem("stage_in2")
        self.x1_in = sem("x1_in")
        self.wo_in = sem("wo_in")
        self.watt_in = sem("watt_in")
        self.watt3_in = sem("watt3_in")
        self.gate_in = sem("gate_in")
        self.gu_in0 = sem("gu_in0")
        self.gu_in1 = sem("gu_in1")
        self.wd_in0 = sem("wd_in0")
        self.wd_in1 = sem("wd_in1")
        self.out_done = sem("out_done")
        self.consts = sem("consts")
        self.stage_hi = sem("stage_hi")
        self.stage_lo = sem("stage_lo")
        self.dve_step = sem("dve_step")
        self.ln_stats = sem("ln_stats")
        self.ln_rstd = sem("ln_rstd")
        self.ln_xn = sem("ln_xn")
        self.ln_T = sem("ln_T")
        self.ln_hi = sem("ln_hi")
        self.ln_out = sem("ln_out")
        self.q_psum = sem("q_psum")
        self.q_raw = sem("q_raw")
        self.q_ss = sem("q_ss")
        self.q_rs = sem("q_rs")
        self.q_scaled = sem("q_scaled")
        self.q_T = sem("q_T")
        self.q_hi = sem("q_hi")
        self.q_lo = sem("q_lo")
        self.c_T = sem("c_T")
        self.c_hi = sem("c_hi")
        self.c_lo = sem("c_lo")
        self.k_psum = sem("k_psum")
        self.k_sq = sem("k_sq")
        self.k_hi = sem("k_hi")
        self.k_lo = sem("k_lo")
        self.sq_split = sem("sq_split")
        self.norm_psum = sem("norm_psum")
        self.norm_read = sem("norm_read")
        self.r_ready = sem("r_ready")
        self.s_psum = sem("s_psum")
        self.s_kept = sem("s_kept")
        self.s_shifted = sem("s_shifted")
        self.p_hi = sem("p_hi")
        self.p_full = sem("p_full")
        self.p_lo = sem("p_lo")
        self.pv_done = sem("pv_done")
        self.max_done = sem("max_done")
        self.max_T = sem("max_T")
        self.max_q = sem("max_q")
        self.max_diag = sem("max_diag")
        self.max_b = sem("max_b")
        self.max_row = sem("max_row")
        self.t_sum = sem("t_sum")
        self.t_rsum = sem("t_rsum")
        self.t_norm = sem("t_norm")
        self.t_T = sem("t_T")
        self.t_hi = sem("t_hi")
        self.t_lo = sem("t_lo")
        self.o_psum = sem("o_psum")
        self.o_kept = sem("o_kept")
        self.y_psum = sem("y_psum")
        self.qk_psum = sem("qk_psum")
        self.q_kept = sem("q_kept")
        self.k_kept = sem("k_kept")
        self.v_kept = sem("v_kept")
        self.mask_done = sem("mask_done")
        self.a_psum = sem("a_psum")
        self.a_masked = sem("a_masked")
        self.a_exp = sem("a_exp")
        self.a_T = sem("a_T")
        self.a_Tkept = sem("a_Tkept")
        self.ao_psum = sem("ao_psum")
        self.an_done = sem("an_done")
        self.an_T = sem("an_T")
        self.an_kept = sem("an_kept")
        self.ay_psum = sem("ay_psum")
        self.gate_hi = sem("gate_hi")
        self.gate_lo = sem("gate_lo")
        self.g_psum = sem("g_psum")
        self.gate_max = sem("gate_max")
        self.g_exp = sem("g_exp")
        self.gu_hi = sem("gu_hi")
        self.gu_lo = sem("gu_lo")
        self.wd_hi = sem("wd_hi")
        self.wd_lo = sem("wd_lo")
        self.h_psum = sem("h_psum")
        self.h_silu = sem("h_silu")
        self.h_full = sem("h_full")
        self.h_hi = sem("h_hi")
        self.h_kept = sem("h_kept")
        self.d_psum = sem("d_psum")
        self.moe_acc = sem("moe_acc")


def perceiver_layer(nc, x, ctx, wq, wk, wv, wo, gq, gk, swq, swk, swv, swo,
                    gate_w, w_gate, w_up, w_down, sw_gate, sw_up, sw_down, out):
    stack = ExitStack()
    with stack:
        def sem(name):
            return stack.enter_context(nc.semaphore(name))

        def pool_of(st):
            return lambda name, shape, dt: st.enter_context(nc.sbuf_tensor(name, shape, dt))

        keep = pool_of(stack)
        ident = keep("ident", [P, P], fp32)
        ones = keep("ones", [P, P], fp32)
        ones16 = keep("ones16", [P, 2], fp16)
        half_neg = keep("half_neg", [P, 32], fp32)
        ggT = keep("ggT", [P, 4], fp32)
        stats = keep("stats", [P, QT, 6], fp32)
        moments = keep("moments", [P, QT, 2], fp32)
        rstd = keep("rstd", [P, QT], fp32)
        q16 = keep("q16", [P, XH, 2, TOK], fp16)
        o32 = q16[:, :, :, :].rearrange("p h a q -> p (h a q)").bitcast(fp32).rearrange(
            "p (h q) -> p h q", h=XH)

        main = ExitStack()
        buf = pool_of(main)
        ctxT = buf("ctxT", [P, 2, KC, CTX], fp16)
        wk16 = buf("wk16", [P, 2, KC, XH * XD], fp16)
        early_end = nc.sbuf_base
        ctx_hi = buf("ctx_hi", [P, NTILE, CD + 2], fp16)
        ctx_lo = buf("ctx_lo", [P, NTILE, CD], fp16)
        ctx_end = nc.sbuf_base
        wv16 = buf("wv16", [P, 2, KC, XH * XD], fp16)
        k16 = buf("k16", [P, 2, 2, CHUNK], fp16)
        ksq = buf("ksq", [P, CHUNK], fp32)
        ksq16 = buf("ksq16", [P, 2, 2, CHUNK], fp16)
        p16 = buf("p16", [P, 2, 2, PER, TOK], fp16)
        norm = buf("norm", [P, 2, PER], fp32)
        r_key = buf("r_key", [P, 2, PER], fp32)
        runmax = buf("runmax", [P, PER, TOK], fp32)
        foldmax = buf("foldmax", [P, TOK], fp32)
        maxq = buf("maxq", [P, QT], fp32)
        diag = buf("diag", [P, QT, P], fp32)
        maxrow = buf("maxrow", [P, TOK], fp32)
        rsum = buf("rsum", [P, QT], fp32)
        tn = buf("tn", [P, QT, CD], fp32)
        tT16 = buf("tT16", [P, 2, KC, TOK], fp16)
        scores_at = nc.sbuf_base
        scores = buf("scores", [P, SLOTS, PER, TOK], fp32)
        main_end = nc.sbuf_base
        main.close()

        pre = ExitStack()
        pad = pre.enter_context(nc.sbuf_tensor("pad", [P, (scores_at - nc.sbuf_base) // 4], fp32))
        buf = pool_of(pre)
        x0 = buf("x0", [P, QT, DM], fp32)
        xn0T = buf("xn0T", [P, 2, CT, TOK], fp16)
        STG = 3
        stage = [buf(f"stage{i}", [P, 2048], fp32) for i in range(STG)]
        wq16 = buf("wq16", [P, 2, 2, CT, DM], fp16)
        q32 = buf("q32", [P, QT, XH, XD], fp32)
        assert nc.sbuf_base <= main_end, (nc.sbuf_base, main_end)
        pre.close()
        qsq = runmax[:, :, :].rearrange("p a q -> p (a q)")[:, 0:DM]
        tail = ExitStack()
        buf = pool_of(tail)
        wo_x = buf("wo_x", [P, XH, DM], fp32)
        x1 = buf("x1", [P, QT, DM], fp32)
        w_att3 = buf("w_att3", [P, CT, DM], fp32)
        gate_sb = buf("gate_sb", [P, CT, NE], fp32)
        assert nc.sbuf_base <= early_end
        gu_raw = [buf(f"gu_raw{i}", [P, 2, CT, HID], fp32) for i in range(2)]
        wd_raw = [buf(f"wd_raw{i}", [P, len(HT), DM], fp32) for i in range(2)]
        assert nc.sbuf_base <= ctx_end
        gu16 = [buf(f"gu16_{i}", [P, 2, 2, CT, HID], fp16) for i in range(2)]
        wd16_0 = buf("wd16_0", [P, 2, len(HT), DM], fp16)
        xn = buf("xn", [P, QT, DM], fp32)
        xnT = buf("xnT", [P, CT, TOK], fp32)
        tail.enter_context(nc.sbuf_tensor("gap", [P, (scores_at - nc.sbuf_base) // 4], fp32))
        w_att = [buf(f"w_att{i}", [P, CT, DM], fp32) for i in range(3)] + [w_att3]
        assert nc.sbuf_base <= scores_at + (main_end - scores_at) // 2
        wd16 = [wd16_0, buf("wd16_1", [P, 2, len(HT), DM], fp16)]
        xn16T = buf("xn16T", [P, 2, CT, TOK], fp16)
        aq = buf("aq", [P, CT, TOK], fp32)
        ak = buf("ak", [P, CT, TOK], fp32)
        av = buf("av", [P, QT, DM], fp32)
        an, anT = xn, xnT
        lg = buf("lg", [P, QT, NE], fp32)
        gate16 = buf("gate16", [P, 2, CT, NE], fp16)
        gmax = buf("gmax", [P, QT], fp32)
        gsum = buf("gsum", [P, QT], fp32)
        grs = buf("grs", [P, QT], fp32)
        probs = buf("probs", [P, QT, NE], fp32)
        top = buf("top", [P, QT, 8], fp32)
        topi = buf("topi", [P, QT, 8], u32)
        topf = buf("topf", [P, QT, 8], fp32)
        lane = buf("lane", [P, NE], fp32)
        pick = buf("pick", [P, QT, 2, NE], fp32)
        comb = buf("comb", [P, QT, ALLE], fp32)
        att = ExitStack()
        buf = pool_of(att)
        mask = buf("mask", [P, QT, TOK], fp32)
        sm = buf("sm", [P, 2, QT, TOK], fp32)
        pr = buf("pr", [P, 2, QT, TOK], fp32)
        prT = buf("prT", [P, 2, QT, TOK], fp32)
        nmax = buf("nmax", [P, SH, QT], fp32)
        den = buf("den", [P, SH, QT], fp32)
        rden = buf("rden", [P, SH, QT], fp32)
        att.close()
        buf = pool_of(tail)
        silu = buf("silu", [P, 2, TOK], fp32)
        h32 = buf("h32", [P, 2, TOK], fp32)
        h16 = buf("h16", [P, 2, 2, len(HT), TOK], fp16)
        tail.close()

        bank = [stack.enter_context(nc.psum_tensor(f"bank{i}", [P, 512], fp32)) for i in range(8)]
        K_BANK, S_BANK, T_BANK, NORM_BANK, MISC = (0, 1), (2, 3), (4, 5), 6, 7

        s = Signals(sem)
        stage_in = [s.stage_in0, s.stage_in1, s.stage_in2]
        gu_in, wd_in = [s.gu_in0, s.gu_in1], [s.wd_in0, s.wd_in1]

        block = stack.enter_context(nc.Block())

        def due(value):
            return not isinstance(value, int) or value > 0

        ctx_v = ctx.rearrange("(p t) c -> p t c", p=P)
        LOADS = ([("wq", g) for g in range(WQG)] + [("ctx", g) for g in range(4)] +
                 [("wk", g) for g in range(2)] + [("wv", g) for g in range(2)])

        def staged(kind, g):
            if kind == "wq":
                return wq.rearrange("(t p) n -> p t n", p=P)[:, :, g * DM:(g + 1) * DM]
            if kind == "ctx":
                return ctx_v[:, g * 8:(g + 1) * 8, :]
            w = wk if kind == "wk" else wv
            return w.rearrange("(t p) n -> p t n", p=P)[:, :, g * 1024:(g + 1) * 1024]

        def stage_view(i, kind):
            t = {"wq": CT, "ctx": 8, "wk": KC, "wv": KC}[kind]
            return stage[i % STG][:, :].rearrange("p (t n) -> p t n", t=t)

        def stage_parts(kind, g):
            if kind == "wq":
                return wq16[:, g % 2, 0, :, :], wq16[:, g % 2, 1, :, :]
            if kind == "ctx":
                return ctx_hi[:, g * 8:(g + 1) * 8, 0:CD], ctx_lo[:, g * 8:(g + 1) * 8, :]
            w = wk16 if kind == "wk" else wv16
            return w[:, 0, :, g * 1024:(g + 1) * 1024], w[:, 1, :, g * 1024:(g + 1) * 1024]

        def in_loops(eng, step, lo_peel, hi_peel, last):
            for n in range(*lo_peel):
                step(0, 0, n)
            with eng.Fori(hi_peel[0] // NCH, hi_peel[1] // NCH, 2) as hb:
                for i in range(SLOTS):
                    step(hb * NCH, hb, i)
            for i in range(last - hi_peel[1]):
                step(hi_peel[1], hi_peel[1] // NCH, i)

        def pipeline(eng, step):
            in_loops(eng, step, (-2, SLOTS), (SLOTS, TOTAL - SLOTS), TOTAL + PV_LAG + 3)

        def active(base, i, off):
            return not isinstance(base, int) or 0 <= base + i + off < TOTAL

        def head_ended(base, i):
            return not isinstance(base, int) or 1 <= (base + i - PV_LAG) // NCH <= XH

        def expert_loads(e, a):
            return (e - a) * 16 + 32

        def experts(eng, expert):
            expert(0, 0, True, False)
            expert(1, 1, False, False)
            with eng.Fori(2, NE - 1, 2) as e0:
                for a in range(2):
                    expert(e0 + a, a, False, False)
            expert(NE, 0, False, False)
            expert(NE + 1, 1, False, True)

        @block.sync
        def _(sp):
            sp.dma_start(x0[:, :, :], x.rearrange("b (t p) d -> p (b t) d", p=P)).then_inc(s.x_in, 16)
            sp.dma_start(ggT[:, 0:1], gq.rearrange("(p a) -> p a", a=1)).then_inc(s.gains_in, 16)
            sp.dma_start(ggT[:, 1:2], gk.rearrange("(p a) -> p a", a=1)).then_inc(s.gains_in, 16)
            ctx_tiles = 0
            for i, (kind, g) in enumerate(LOADS):
                if i >= STG:
                    sp.wait_ge(s.stage_hi, i - STG + 1)
                    sp.wait_ge(s.stage_lo, i - STG + 1)
                    if LOADS[i - STG][0] == "ctx":
                        ctx_tiles += 8
                        sp.wait_ge(s.c_T, ctx_tiles // 2)
                sp.dma_start(stage_view(i, kind), staged(kind, g)).then_inc(stage_in[i % STG], 16)

            sp.wait_ge(s.k_psum, TOTAL)
            sp.dma_start(wo_x[:, :, :], wo.rearrange("(h p) n -> p h n", p=P)).then_inc(s.wo_in, 16)
            sp.dma_start(x1[:, :, :], x.rearrange("b (t p) d -> p (b t) d", p=P)).then_inc(s.x1_in, 16)
            sp.dma_start(w_att3[:, :, :], swo.rearrange("(t p) n -> p t n", p=P)).then_inc(s.watt3_in, 16)
            sp.dma_start(gate_sb[:, :, :], gate_w.rearrange("(t p) n -> p t n", p=P)).then_inc(s.gate_in, 16)
            sp.wait_ge(s.p_lo, TOTAL - SLOTS // 2)
            for w, dst in zip((swq, swk, swv), w_att):
                sp.dma_start(dst[:, :, :], w.rearrange("(t p) n -> p t n", p=P)).then_inc(s.watt_in, 16)
            sp.wait_ge(s.pv_done, TOTAL)

            def load_gate_up(a, w_g, w_u):
                sp.dma_start(gu_raw[a][:, 0, :, :], w_g.rearrange("(t p) n -> p t n", p=P)).then_inc(gu_in[a], 16)
                sp.dma_start(gu_raw[a][:, 1, :, :], w_u.rearrange("(t p) n -> p t n", p=P)).then_inc(gu_in[a], 16)

            def load_down(a, w_d):
                sp.dma_start(wd_raw[a][:, 0:2, :],
                             w_d[0:2 * P, :].rearrange("(t p) n -> p t n", p=P)).then_inc(wd_in[a], 16)
                sp.dma_start(wd_raw[a][0:HT[2], 2, :], w_d[2 * P:HID, :]).then_inc(wd_in[a], 16)

            for e in range(2):
                load_gate_up(e, w_gate[e], w_up[e])
                load_down(e, w_down[e])
            with sp.Fori(2, NE - 1, 2) as e0:
                for a in range(2):
                    e = e0 + a
                    sp.wait_ge(s.gu_lo, e - 1)
                    row = bass.ds(e, 1)
                    load_gate_up(a, w_gate[row].rearrange("a d n -> (a d) n"),
                                 w_up[row].rearrange("a d n -> (a d) n"))
                    sp.wait_ge(s.wd_lo, e - 1)
                    load_down(a, w_down[row].rearrange("a d n -> (a d) n"))
            for e in range(NE, ALLE):
                a, c = e % 2, slice((e - NE) * HID, (e - NE + 1) * HID)
                sp.wait_ge(s.gu_lo, e - 1)
                load_gate_up(a, sw_gate[:, c], sw_up[:, c])
                sp.wait_ge(s.wd_lo, e - 1)
                load_down(a, sw_down[c, :])
            sp.wait_ge(s.moe_acc, ALLE * QT)
            sp.dma_start(out.rearrange("b (t p) d -> p (b t) d", p=P), x1[:, :, :]).then_inc(s.out_done, 16)
            sp.wait_ge(s.out_done, 16)

        @block.gpsimd
        def _(pool):
            pool.memset(ident[:, :], 0.0).then_inc(s.consts, 1)
            pool.wait_ge(s.consts, 1)
            pool.affine_select(out=ident[:, :], in_=ident[:, :], compare_op=ALU.not_equal, fill=1.0, base=0,
                               pattern=[[-1, P]], channel_multiplier=1).then_inc(s.consts, 1)
            pool.memset(ones[:, :], 1.0).then_inc(s.consts, 1)
            pool.memset(ones16[:, :], 1.0).then_inc(s.consts, 1)
            pool.memset(half_neg[:, :], -0.5).then_inc(s.consts, 1)
            pool.wait_ge(s.consts, 5)

            def ln_pool(k):
                for t in range(QT):
                    pool.wait_ge(s.ln_stats, k * QT + t + 1)
                    pool.tensor_tensor(out=rstd[:, t:t + 1], in0=moments[:, t, 1:2], in1=half_neg[:, 0:1],
                                       op=ALU.pow).then_inc(s.ln_rstd, 1)

            ln_pool(0)
            pool.wait_ge(s.q_ss, 1)
            for t in range(QT):
                pool.tensor_tensor(out=foldmax[:, t * XH:(t + 1) * XH], in0=diag[:, 0, t * XH:(t + 1) * XH], in1=half_neg[:, 0:XH],
                                   op=ALU.pow).then_inc(s.q_rs, 1)

            def step(base, hb, i):
                n = base + i
                if active(base, i, 2):
                    a = (i + 2) % 2
                    pool.wait_ge(s.k_sq, n + 3)
                    if not isinstance(base, int) or n + 2 >= 2:
                        pool.wait_ge(s.norm_psum, n + 1)
                    pool.tensor_tensor(out=ksq16[:, a, 0, :], in0=ksq[:, :], in1=ones[:, 0:1].to_broadcast([P, CHUNK]),
                                       op=ALU.mult).then_inc(s.sq_split, 1)
                    pool.wait_ge(s.sq_split, (n + 2) * 2 + 1)
                    pool.tensor_tensor(out=ksq16[:, a, 1, :], in0=ksq[:, :], in1=ksq16[:, a, 0, :],
                                       op=ALU.subtract).then_inc(s.sq_split, 1)
                if active(base, i, 1):
                    a = (i + 1) % 2
                    pool.wait_ge(s.norm_read, n + 2)
                    if not isinstance(base, int) or n + 1 >= 2:
                        pool.wait_ge(s.s_kept, (n - 1 + 1) * PER)
                    pool.tensor_tensor(out=r_key[:, a, :], in0=norm[:, a, :], in1=half_neg[:, 0:PER],
                                       op=ALU.pow).then_inc(s.r_ready, 1)

            pipeline(pool, step)

            pool.wait_ge(s.pv_done, TOTAL)
            pool.memset(mask[:, :, :], 1.0).then_inc(s.mask_done, 1)
            pool.memset(comb[:, :, :], 1.0 / WS).then_inc(s.mask_done, 1)
            pool.wait_ge(s.mask_done, 2)
            pool.iota(lane[:, :], [[1, NE]], channel_multiplier=0, allow_small_or_imprecise_dtypes=True
                      ).then_inc(s.mask_done, 1)
            pool.affine_select(out=mask[:, :, :], in_=mask[:, :, :], compare_op=ALU.is_ge, fill=0.0, base=0,
                               pattern=[[P, QT], [-1, TOK]], channel_multiplier=1).then_inc(s.mask_done, 1)
            ln_pool(1)
            ln_pool(2)

        @block.scalar
        def _(act):
            act_ = nc.scalar
            for t in range(QT):
                act.wait_ge(s.ln_T, t + 1)
                act_.activation(xn0T[:, 0, :, t * P:(t + 1) * P], bank[t][:, :].rearrange("p (a q) -> p a q", a=CT),
                                ACT.Copy).then_inc(s.ln_hi, 1)

            def stage_hi(i):
                kind, g = LOADS[i]
                act.wait_ge(stage_in[i % STG], 16 * (i // STG + 1))
                if kind == "wq" and g >= 2:
                    act.wait_ge(s.q_psum, (g - 1) * QT)
                act_.activation(stage_parts(kind, g)[0], stage_view(i, kind), ACT.Copy,
                                scale=1.0 if kind == "ctx" else WS).then_inc(s.stage_hi, 1)

            def q_evac(g):
                for t in range(QT):
                    act.wait_ge(s.q_psum, g * QT + t + 1)
                    act_.activation(q32[:, t, 4 * g:4 * g + 4, :],
                                    bank[2 + (g * QT + t) % 2][:, :].rearrange("p (h d) -> p h d", h=4),
                                    ACT.Copy, scale=1.0 / WS).then_inc(s.q_raw, 1)

            for i in range(4):
                stage_hi(i)
                if i >= 1:
                    q_evac(i - 1)
            for i in range(4, 8):
                stage_hi(i)
                if i == 4:
                    q_evac(3)
                for u in range(4):
                    b = (i - 4) * 4 + u
                    act.wait_ge(s.c_T, b + 1)
                    act_.activation(ctxT[:, 0, :, b * 2 * P:(b + 1) * 2 * P],
                                    bank[4 + b % 2][:, :].rearrange("p (c r) -> p c r", c=KC),
                                    ACT.Copy).then_inc(s.c_hi, 1)
            for i in range(8, 12):
                stage_hi(i)
            for b in range(XH // 2):
                act.wait_ge(s.q_T, b + 1)
                act_.activation(q16[:, 2 * b:2 * b + 2, 0, :],
                                bank[6 + b % 2][:, :].rearrange("p (h q) -> p h q", h=2),
                                ACT.Copy, scale=ggT[:, 2:3]).then_inc(s.q_hi, 1)

            def step(base, hb, i):
                n = base + i
                if active(base, i, 2):
                    a = (i + 2) % 2
                    act.wait_ge(s.k_psum, n + 3)
                    if due((n + 2) * 2):
                        act.wait_ge(s.sq_split, (n + 2) * 2)
                    act_.activation(ksq[:, :], bank[K_BANK[a]][:, :], ACT.Square,
                                    scale=KS / WS).then_inc(s.k_sq, 1)
                    if not isinstance(base, int) or n >= 0:
                        act.wait_ge(s.s_psum, (n + 1) * 2)
                    act_.activation(k16[:, a, 0, :], bank[K_BANK[a]][:, :], ACT.Copy,
                                    scale=1.0 / WS).then_inc(s.k_hi, 1)
                if active(base, i, -LO_LAG):
                    v = n - LO_LAG
                    slot = (i - LO_LAG) % SLOTS
                    a = (i - LO_LAG) % 2
                    act.wait_ge(s.p_full, v + 1)
                    if not isinstance(base, int) or v >= 2:
                        act.wait_ge(s.pv_done, v - 1)
                    act_.activation(p16[:, a, 0, :, :], scores[:, slot, :, :], ACT.Copy).then_inc(s.p_hi, 1)
                if active(base, i, 0):
                    a = i % 2
                    slot = i % SLOTS
                    act.wait_ge(s.r_ready, n + 1)
                    if not isinstance(base, int) or n >= SLOTS:
                        act.wait_ge(s.p_lo, n - SLOTS + 1)
                    for b in range(2):
                        act.wait_ge(s.s_psum, n * 2 + b + 1)
                        for k in range(2):
                            kt = 2 * b + k
                            act_.activation(scores[:, slot, kt, :], bank[S_BANK[b]][:, k * TOK:(k + 1) * TOK],
                                            ACT.Copy, scale=r_key[:, a, kt:kt + 1]).then_inc(s.s_kept, 1)
                if active(base, i, -EXP_LAG):
                    v = n - EXP_LAG
                    slot = (i - EXP_LAG) % SLOTS
                    act.wait_ge(s.s_shifted, v + 1)
                    act_.activation(scores[:, slot, :, :], scores[:, slot, :, :], ACT.Exp).then_inc(s.p_full, 1)
                if (i - PV_LAG) % NCH == 1 and head_ended(base, i):
                    h = hb + (i - PV_LAG - 1) // NCH
                    act.wait_ge(s.t_T, h)
                    act_.activation(tT16[:, 0, :, :], bank[MISC][:, :].rearrange("p (c q) -> p c q", c=KC),
                                    ACT.Copy).then_inc(s.t_hi, 1)

            pipeline(act, step)

            def gu_hi(e, a, expert_used):
                act.wait_ge(gu_in[a], expert_loads(e, a))
                if expert_used:
                    act.wait_ge(s.h_psum, (e - 1) * len(HT))
                for w in range(2):
                    act_.activation(gu16[a][:, 0, w, :, :], gu_raw[a][:, w, :, :], ACT.Copy, scale=WS
                                    ).then_inc(s.gu_hi, 1)

            def wd_hi(e, a, expert_used):
                act.wait_ge(wd_in[a], expert_loads(e, a))
                if expert_used:
                    act.wait_ge(s.d_psum, (e - 1) * QT)
                act_.activation(wd16[a][:, 0, 0:2, :], wd_raw[a][:, 0:2, :], ACT.Copy, scale=WS
                                ).then_inc(s.wd_hi, 1)
                act_.activation(wd16[a][0:HT[2], 0, 2, :], wd_raw[a][0:HT[2], 2, :], ACT.Copy, scale=WS
                                ).then_inc(s.wd_hi, 1)

            act.wait_ge(s.o_kept, XH + 1)
            for e in range(2):
                gu_hi(e, e, False)
                wd_hi(e, e, False)
            act.wait_ge(s.qk_psum, CT)
            for m in range(2):
                act_.activation(aq[:, 2 * m:2 * m + 2, :],
                                bank[m][:, :].rearrange("p (a q) -> p a q", a=2), ACT.Copy,
                                scale=1.0 / TOK ** 0.5).then_inc(s.q_kept, 1)

            def a_exps(h):
                a = h % 2
                act.wait_ge(s.a_masked, h + 1)
                if h >= 2:
                    act.wait_ge(s.a_T, h - 1)
                for t in range(QT):
                    act_.activation(pr[:, a, t, :], sm[:, a, t, :], ACT.Exp,
                                    bias=nmax[:, h, t:t + 1], accum_out=den[:, h, t:t + 1]
                                    ).then_inc(s.a_exp, 1)

            def pT_kept(h):
                a = h % 2
                act.wait_ge(s.a_T, h + 1)
                if h >= 2:
                    act.wait_ge(s.ao_psum, h - 1)
                act_.activation(prT[:, a, :, :], bank[2 + a][:, :].rearrange("p (t q) -> p t q", t=QT), ACT.Copy
                                ).then_inc(s.a_Tkept, 1)

            for h in range(SH + 1):
                if h < SH:
                    a_exps(h)
                if h >= 1:
                    pT_kept(h - 1)
            act.wait_ge(s.gate_in, 16)
            act_.activation(gate16[:, 0, :, :], gate_sb[:, :, :], ACT.Copy, scale=WS).then_inc(s.gate_hi, 1)
            for t in range(QT):
                act.wait_ge(s.ln_T, 2 * QT + t + 1)
                act_.activation(xn16T[:, 0, :, t * P:(t + 1) * P], bank[6 + t][:, :].rearrange("p (a q) -> p a q", a=CT),
                                ACT.Copy).then_inc(s.ln_hi, 1)
            act.wait_ge(s.gate_max, 1)
            for t in range(QT):
                act_.activation(probs[:, t, :], lg[:, t, :], ACT.Exp, bias=gmax[:, t:t + 1],
                                accum_out=gsum[:, t:t + 1]).then_inc(s.g_exp, 1)

            def expert(e, a, first, last):
                if not first and not last:
                    gu_hi(e + 1, 1 - a, True)
                for j, rows in enumerate(HT):
                    u = e * len(HT) + j
                    b = (a * len(HT) + j) % 2
                    act.wait_ge(s.h_psum, u + 1)
                    if not first or j >= 2:
                        act.wait_ge(s.h_full, u - 1)
                    act_.activation(silu[0:rows, b, :], bank[b][0:rows, 0:TOK], ACT.Silu, scale=1.0 / WS
                                    ).then_inc(s.h_silu, 1)
                    act.wait_ge(s.h_full, u + 1)
                    if not first and j == 0:
                        if not isinstance(e, int) or e >= 2:
                            act.wait_ge(s.d_psum, (e - 1) * QT)
                    act_.activation(h16[0:rows, a, 0, j, :], h32[0:rows, b, :], ACT.Copy).then_inc(s.h_hi, 1)
                if not isinstance(e, int) or e >= 2:
                    wd_hi(e, a, True)

            experts(act, expert)

        @block.vector
        def _(dve):
            vec = nc.vector

            def chained(ins, count):
                ins.then_inc(s.dve_step, 1)
                dve.wait_ge(s.dve_step, count)

            steps = [0]

            def then(ins):
                steps[0] += 1
                chained(ins, steps[0])

            def ln_stats(k, t, src):
                then(vec.bn_stats(out=stats[:, t, :], in_=src[:, t, :]))
                then(vec.bn_aggr(out=moments[:, t, :], in_=stats[:, t, :]))
                vec.tensor_scalar(moments[:, t, 1:2], moments[:, t, 1:2], EPS, None, ALU.add
                                  ).then_inc(s.ln_stats, 1)

            def ln_scale(k, t, src, dst):
                dve.wait_ge(s.ln_rstd, k * QT + t + 1)
                vec.tensor_scalar(dst[:, t, :], src[:, t, :], moments[:, t, 0:1], rstd[:, t:t + 1],
                                  ALU.subtract, ALU.mult).then_inc(s.ln_xn, 1)

            def ln_lo(k, t, b, dst):
                cols = slice(t * P, (t + 1) * P)
                dve.wait_ge(s.ln_hi, (k // 2) * QT + t + 1)
                vec.tensor_tensor(dst[:, 1, :, cols], bank[b][:, :].rearrange("p (a q) -> p a q", a=CT),
                                  dst[:, 0, :, cols], ALU.subtract).then_inc(s.ln_out, 1)

            vec.memset(ctx_hi[:, :, CD:CD + 2], 1.0).then_inc(s.o_kept, 1)
            dve.wait_ge(s.gains_in, 32)
            then(vec.tensor_tensor(ggT[:, 2:3], ggT[:, 0:1], ggT[:, 1:2], ALU.mult))
            dve.wait_ge(s.x_in, 16)
            for t in range(QT):
                ln_stats(0, t, x0)
            for t in range(QT):
                ln_scale(0, t, x0, x0)
            for t in range(QT):
                ln_lo(0, t, t, xn0T)

            def stage_lo(i):
                kind, g = LOADS[i]
                dve.wait_ge(s.stage_hi, i + 1)
                hi, lo = stage_parts(kind, g)
                vec.scalar_tensor_tensor(out=lo, in0=stage_view(i, kind), scalar=1.0 if kind == "ctx" else WS,
                                         in1=hi, op0=ALU.mult, op1=ALU.subtract).then_inc(s.stage_lo, 1)

            def q_sums(g):
                for t in range(QT):
                    dve.wait_ge(s.q_raw, g * QT + t + 1)
                    qg = q32[:, t, 4 * g:4 * g + 4, :]
                    sq = qsq.rearrange("p (h d) -> p h d", h=4)
                    then(vec.tensor_tensor(sq, qg, qg, ALU.mult))
                    then(vec.tensor_reduce(diag[:, 0, t * XH + 4 * g:t * XH + 4 * g + 4], sq, AX.X, ALU.add))

            for i in range(4):
                stage_lo(i)
                if i >= 1:
                    q_sums(i - 1)
            for i in range(4, 8):
                stage_lo(i)
                if i == 4:
                    q_sums(3)
                    vec.tensor_scalar(diag[:, 0, 0:QT * XH], diag[:, 0, 0:QT * XH], 1.0 / XD, EPS,
                                      ALU.mult, ALU.add).then_inc(s.q_ss, 1)
                for u in range(4):
                    b = (i - 4) * 4 + u
                    dve.wait_ge(s.c_hi, b + 1)
                    vec.tensor_tensor(ctxT[:, 1, :, b * 2 * P:(b + 1) * 2 * P],
                                      bank[4 + b % 2][:, :].rearrange("p (c r) -> p c r", c=KC),
                                      ctxT[:, 0, :, b * 2 * P:(b + 1) * 2 * P], ALU.subtract
                                      ).then_inc(s.c_lo, 1)
                if i == 4:
                    dve.wait_ge(s.q_rs, QT)
                    for t in range(QT):
                        last = vec.tensor_tensor(q32[:, t, :, :], q32[:, t, :, :],
                                                 foldmax[:, t * XH:(t + 1) * XH].unsqueeze(2).to_broadcast(
                                                     [P, XH, XD]), ALU.mult)
                    last.then_inc(s.q_scaled, 1)
            for i in range(8, 12):
                stage_lo(i)
            for b in range(XH // 2):
                dve.wait_ge(s.q_hi, b + 1)
                vec.scalar_tensor_tensor(out=q16[:, 2 * b:2 * b + 2, 1, :],
                                         in0=bank[6 + b % 2][:, :].rearrange("p (h q) -> p h q", h=2),
                                         scalar=ggT[:, 2:3], in1=q16[:, 2 * b:2 * b + 2, 0, :],
                                         op0=ALU.mult, op1=ALU.subtract).then_inc(s.q_lo, 1)

            def step(base, hb, i):
                n = base + i
                if (i - PV_LAG) % NCH == 0 and head_ended(base, i):
                    h = hb + (i - PV_LAG) // NCH
                    for t in range(QT):
                        if t == 0:
                            dve.wait_ge(s.t_sum, h)
                        else:
                            dve.wait_ge(s.pv_done, h * NCH)
                        vec.reciprocal(rsum[:, t:t + 1], bank[T_BANK[t]][:, CD:CD + 1]).then_inc(s.t_rsum, 1)
                        dve.wait_ge(s.t_rsum, h * QT - QT + t + 1)
                        vec.tensor_scalar(tn[:, t, :], bank[T_BANK[t]][:, 0:CD], rsum[:, t:t + 1], None,
                                          ALU.mult).then_inc(s.t_norm, 1)
                if i % NCH == 1 and active(base, i, -2):
                    h = hb + i // NCH - 1
                    dve.wait_ge(s.max_T, h + 1)
                    vec.tensor_reduce(maxq[:, :], bank[MISC][:, 0:TOK].rearrange("p (t r) -> p t r", t=QT),
                                      AX.X, ALU.max).then_inc(s.max_q, 1)
                    dve.wait_ge(s.max_q, h + 1)
                    for t in range(QT):
                        last = vec.tensor_scalar(diag[:, t, :], ident[:, :], maxq[:, t:t + 1], None, ALU.mult)
                    last.then_inc(s.max_diag, 1)
                if active(base, i, 2):
                    a = (i + 2) % 2
                    dve.wait_ge(s.k_hi, n + 3)
                    vec.scalar_tensor_tensor(out=k16[:, a, 1, :], in0=bank[K_BANK[a]][:, :], scalar=1.0 / WS,
                                             in1=k16[:, a, 0, :], op0=ALU.mult, op1=ALU.subtract
                                             ).then_inc(s.k_lo, 1)
                if active(base, i, 1):
                    a = (i + 1) % 2
                    dve.wait_ge(s.norm_psum, n + 2)
                    if not isinstance(base, int) or n + 1 >= 2:
                        dve.wait_ge(s.r_ready, n)
                    vec.tensor_scalar(norm[:, a, :], bank[NORM_BANK][:, a * PER:(a + 1) * PER],
                                      1.0 / KS ** 2, XD * EPS, ALU.mult, ALU.add).then_inc(s.norm_read, 1)
                if i % NCH == 1 and active(base, i, -2):
                    h = hb + i // NCH - 1
                    dve.wait_ge(s.max_b, h + 1)
                    vec.tensor_scalar(maxrow[:, :], bank[MISC][:, 0:TOK], -SHIFT, None, ALU.add
                                      ).then_inc(s.max_row, 1)
                if active(base, i, -EXP_LAG):
                    v = n - EXP_LAG
                    slot = (i - EXP_LAG) % SLOTS
                    dve.wait_ge(s.max_row, hb + (i - EXP_LAG) // NCH + 1)
                    vec.tensor_tensor(scores[:, slot, :, :], scores[:, slot, :, :],
                                      maxrow[:, :].unsqueeze(1).to_broadcast([P, PER, TOK]),
                                      ALU.subtract).then_inc(s.s_shifted, 1)
                if active(base, i, -LO_LAG):
                    a = (i - LO_LAG) % 2
                    slot = (i - LO_LAG) % SLOTS
                    dve.wait_ge(s.p_hi, n - LO_LAG + 1)
                    vec.tensor_tensor(p16[:, a, 1, :, :], scores[:, slot, :, :], p16[:, a, 0, :, :], ALU.subtract
                                      ).then_inc(s.p_lo, 1)
                if active(base, i, 0):
                    j, slot = i % NCH, i % SLOTS
                    if j:
                        dve.wait_ge(s.s_kept, (n + 1) * PER)
                        first = scores[:, slot - 1, :, :] if j == 1 else runmax[:, :, :]
                        vec.tensor_tensor(runmax[:, :, :], first, scores[:, slot, :, :], ALU.max
                                          ).then_inc(s.max_done, 1)
                    if j == NCH - 1:
                        h = hb + i // NCH
                        done = h * (NCH + 1) + NCH - 1
                        dve.wait_ge(s.max_done, done)
                        vec.tensor_tensor(runmax[:, 0:2, :], runmax[:, 0:2, :], runmax[:, 2:4, :], ALU.max
                                          ).then_inc(s.max_done, 1)
                        dve.wait_ge(s.max_done, done + 1)
                        if not isinstance(base, int) or h >= 1:
                            dve.wait_ge(s.max_T, h)
                        vec.tensor_tensor(foldmax[:, :], runmax[:, 0, :], runmax[:, 1, :], ALU.max
                                          ).then_inc(s.max_done, 1)
                    elif j >= 1:
                        done = (hb + i // NCH) * (NCH + 1) + j
                        dve.wait_ge(s.max_done, done)
                if (i - PV_LAG) % NCH == 1 and head_ended(base, i):
                    h = hb + (i - PV_LAG - 1) // NCH
                    dve.wait_ge(s.t_hi, h)
                    vec.tensor_tensor(tT16[:, 1, :, :], bank[MISC][:, :].rearrange("p (c q) -> p c q", c=KC),
                                      tT16[:, 0, :, :], ALU.subtract).then_inc(s.t_lo, 1)
                if (i - PV_LAG) % NCH == 2 and head_ended(base, i):
                    h = hb + (i - PV_LAG - 2) // NCH
                    dve.wait_ge(s.o_psum, h)
                    vec.tensor_scalar(o32[:, h - 1, :], bank[MISC][:, 0:TOK], 1.0 / WS, None, ALU.mult
                                      ).then_inc(s.o_kept, 1)

            pipeline(dve, step)

            def gu_lo(e, a):
                for w in range(2):
                    dve.wait_ge(s.gu_hi, 2 * e + w + 1)
                    last = vec.scalar_tensor_tensor(out=gu16[a][:, 1, w, :, :], in0=gu_raw[a][:, w, :, :], scalar=WS,
                                                    in1=gu16[a][:, 0, w, :, :], op0=ALU.mult, op1=ALU.subtract)
                last.then_inc(s.gu_lo, 1)

            def wd_lo(e, a):
                for part in (slice(0, 2), slice(2, 3)):
                    rows = slice(0, P) if part.start == 0 else slice(0, HT[2])
                    dve.wait_ge(s.wd_hi, 2 * e + (part.start > 0) + 1)
                    last = vec.scalar_tensor_tensor(out=wd16[a][rows, 1, part, :], in0=wd_raw[a][rows, part, :],
                                                    scalar=WS, in1=wd16[a][rows, 0, part, :],
                                                    op0=ALU.mult, op1=ALU.subtract)
                last.then_inc(s.wd_lo, 1)

            for e in range(2):
                gu_lo(e, e)
                wd_lo(e, e)
            dve.wait_ge(s.x1_in, 16)
            for t in range(QT):
                dve.wait_ge(s.y_psum, t + 1)
                then(vec.tensor_tensor(x1[:, t, :], bank[t][:, :], x1[:, t, :], ALU.add))
                ln_stats(1, t, x1)
                ln_scale(1, t, x1, xn)
                dve.wait_ge(s.ln_T, QT + t + 1)
                vec.tensor_copy(xnT[:, :, t * P:(t + 1) * P],
                                bank[6 + t][:, :].rearrange("p (a q) -> p a q", a=CT)).then_inc(s.ln_out, 1)
            dve.wait_ge(s.qk_psum, 2 * CT)
            for m in range(2):
                vec.tensor_copy(ak[:, 2 * m:2 * m + 2, :],
                                bank[2 + m][:, :].rearrange("p (a q) -> p a q", a=2)).then_inc(s.k_kept, 1)
            dve.wait_ge(s.mask_done, 4)

            def masked(h):
                a = h % 2
                dve.wait_ge(s.a_psum, h + 1)
                if h >= 2:
                    dve.wait_ge(s.a_exp, (h - 1) * QT)
                then(vec.tensor_tensor(sm[:, a, :, :], bank[a][:, :].rearrange("p (t q) -> p t q", t=QT),
                                       mask[:, :, :], ALU.mult))
                vec.tensor_reduce(nmax[:, h, :], sm[:, a, :, :], AX.X, ALU.max, negate=True
                                  ).then_inc(s.a_masked, 1)

            masked(0)
            masked(1)
            for t in range(QT):
                dve.wait_ge(s.qk_psum, 2 * CT + t + 1)
                vec.tensor_copy(av[:, t, :], bank[4 + t][:, :]).then_inc(s.v_kept, 1)
            for h in range(2, SH):
                masked(h)
            dve.wait_ge(s.gate_hi, 1)
            vec.scalar_tensor_tensor(out=gate16[:, 1, :, :], in0=gate_sb[:, :, :], scalar=WS, in1=gate16[:, 0, :, :],
                                     op0=ALU.mult, op1=ALU.subtract).then_inc(s.gate_lo, 1)
            dve.wait_ge(s.a_exp, SH * QT)
            then(vec.reciprocal(rden[:, :, :], den[:, :, :]))
            dve.wait_ge(s.ao_psum, SH)
            for t in range(QT):
                vec.tensor_tensor(an[:, t, :].rearrange("p (h d) -> p h d", h=SH),
                                  bank[4 + t][:, :].rearrange("p (h d) -> p h d", h=SH),
                                  rden[:, :, t].unsqueeze(2).to_broadcast([P, SH, SD]), ALU.mult
                                  ).then_inc(s.an_done, 1)
            for t in range(QT):
                dve.wait_ge(s.an_T, t + 1)
                vec.tensor_copy(anT[:, :, t * P:(t + 1) * P],
                                bank[6 + t][:, :].rearrange("p (a q) -> p a q", a=CT)).then_inc(s.an_kept, 1)
            for t in range(QT):
                dve.wait_ge(s.ay_psum, t + 1)
                then(vec.tensor_tensor(x1[:, t, :], bank[t][:, :], x1[:, t, :], ALU.add))
                ln_stats(2, t, x1)
                ln_scale(2, t, x1, xn)
            for t in range(QT):
                ln_lo(2, t, 6 + t, xn16T)
            for t in range(QT):
                dve.wait_ge(s.g_psum, t + 1)
                then(vec.tensor_scalar(lg[:, t, :], bank[4 + t][:, 0:NE], 1.0 / WS, None, ALU.mult))
            vec.tensor_reduce(gmax[:, :], lg[:, :, :], AX.X, ALU.max, negate=True).then_inc(s.gate_max, 1)

            def gate_shares():
                dve.wait_ge(s.g_exp, QT)
                then(vec.reciprocal(grs[:, :], gsum[:, :]))
                for t in range(QT):
                    then(vec.tensor_scalar(probs[:, t, :], probs[:, t, :], grs[:, t:t + 1], None, ALU.mult))
                    then(vec.max(out=top[:, t, :], in_=probs[:, t, :]))
                    then(vec.max_index(out=topi[:, t, :], in_max=top[:, t, :], in_values=probs[:, t, :]))
                    then(vec.tensor_copy(topf[:, t, :], topi[:, t, :]))
                    for c in range(2):
                        then(vec.tensor_scalar(pick[:, t, c, :], lane[:, :], topf[:, t, c:c + 1], 1.0 / WS,
                                               ALU.is_equal, ALU.mult))
                    then(vec.tensor_tensor(pick[:, t, 0, :], pick[:, t, 0, :], pick[:, t, 1, :], ALU.add))
                    then(vec.tensor_tensor(comb[:, t, 0:NE], pick[:, t, 0, :], probs[:, t, :], ALU.mult))

            def down(e, at):
                for t in range(QT):
                    dve.wait_ge(s.d_psum, e * QT + t + 1)
                    vec.scalar_tensor_tensor(out=x1[:, t, :], in0=bank[6 + t][:, :], scalar=comb[:, t, at],
                                             in1=x1[:, t, :], op0=ALU.mult, op1=ALU.add
                                             ).then_inc(s.moe_acc, 1)

            def expert(e, a, first, last):
                if not first and not last:
                    gu_lo(e + 1, 1 - a)
                for j, rows in enumerate(HT):
                    u = e * len(HT) + j
                    b = (a * len(HT) + j) % 2
                    dve.wait_ge(s.h_silu, u + 1)
                    if not first or j >= 2:
                        dve.wait_ge(s.h_hi, u - 1)
                    vec.scalar_tensor_tensor(out=h32[0:rows, b, :], in0=bank[2 + b][0:rows, 0:TOK], scalar=1.0 / WS,
                                             in1=silu[0:rows, b, :], op0=ALU.mult, op1=ALU.mult
                                             ).then_inc(s.h_full, 1)
                    dve.wait_ge(s.h_hi, u + 1)
                    vec.tensor_tensor(h16[0:rows, a, 1, j, :], h32[0:rows, b, :], h16[0:rows, a, 0, j, :],
                                      ALU.subtract).then_inc(s.h_kept, 1)
                if first:
                    gate_shares()
                if not isinstance(e, int) or e >= 2:
                    wd_lo(e, a)
                if not first:
                    down(e - 1, bass.ds(e - 1, 1))

            experts(dve, expert)
            down(ALLE - 1, slice(ALLE - 1, ALLE))

        @block.tensor
        def _(pe):
            mm = nc.tensor.matmul

            def split_products(out_, w_hi, w_lo, x_hi, x_lo, steps):
                last = None
                for k in steps:
                    first, final = k == steps[0], k == steps[-1]
                    mm(out_, w_hi(k), x_hi(k), start=first, stop=False)
                    mm(out_, w_hi(k), x_lo(k), start=False, stop=False)
                    last = mm(out_, w_lo(k), x_hi(k), start=False, stop=final)
                return last

            def ln_pe(k, t, src, dst):
                pe.wait_ge(s.ln_xn, k * QT + t + 1)
                for c in range(CT):
                    last = nc.tensor.transpose(dst[:, c * P:(c + 1) * P], src[:, t, c * P:(c + 1) * P], ident[:, :])
                last.then_inc(s.ln_T, 1)

            pe.wait_ge(s.consts, 5)
            for t in range(QT):
                ln_pe(0, t, x0, bank[t])
            pe.wait_ge(s.ln_out, QT)

            def ctx_blocks(b):
                i = 4 + b // 4
                if b % 4 == 0:
                    pe.wait_ge(stage_in[i % STG], 16 * (i // STG + 1))
                if b >= 2:
                    pe.wait_ge(s.c_lo, b - 1)
                src = stage_view(i, "ctx")
                for c in range(KC):
                    for k in range(2):
                        last = nc.tensor.transpose(bank[4 + b % 2][:, c * 2 * P + k * P:c * 2 * P + (k + 1) * P],
                                                   src[:, (2 * b + k) % 8, c * P:(c + 1) * P], ident[:, :])
                last.then_inc(s.c_T, 1)

            for g in range(WQG):
                pe.wait_ge(s.stage_lo, g + 1)
                for t in range(QT):
                    u = g * QT + t
                    if u >= 2:
                        pe.wait_ge(s.q_raw, u - 1)
                    last = split_products(bank[2 + u % 2][:, :],
                                          lambda k: xn0T[:, 0, k, t * P:(t + 1) * P],
                                          lambda k: xn0T[:, 1, k, t * P:(t + 1) * P],
                                          lambda k: wq16[:, g % 2, 0, k, :],
                                          lambda k: wq16[:, g % 2, 1, k, :], range(CT))
                    last.then_inc(s.q_psum, 1)
            for b in range(NTILE // 2):
                ctx_blocks(b)
            pe.wait_ge(s.q_scaled, 1)
            for b in range(XH // 2):
                if b >= 2:
                    pe.wait_ge(s.q_lo, b - 1)
                for c in range(2):
                    for t in range(QT):
                        last = nc.tensor.transpose(bank[6 + b % 2][:, c * TOK + t * P:c * TOK + (t + 1) * P],
                                                   q32[:, t, 2 * b + c, :], ident[:, :])
                last.then_inc(s.q_T, 1)
            pe.wait_ge(s.stage_lo, len(LOADS))
            pe.wait_ge(s.q_lo, XH // 2)
            pe.wait_ge(s.c_lo, NTILE // 2)

            def head_slice(hb, i, off):
                return bass.ds((hb + (i + off) // NCH) * XD, XD)

            def step(base, hb, i):
                n = base + i
                if active(base, i, 2):
                    a, j = (i + 2) % 2, (i + 2) % NCH
                    if due(n + 1):
                        pe.wait_ge(s.k_lo, n + 1)
                    cols = slice(j * CHUNK, (j + 1) * CHUNK)
                    hs = head_slice(hb, i, 2)
                    split_products(bank[K_BANK[a]][:, :],
                                   lambda k: wk16[:, 0, k, hs], lambda k: wk16[:, 1, k, hs],
                                   lambda k: ctxT[:, 0, k, cols], lambda k: ctxT[:, 1, k, cols], range(KC)
                                   ).then_inc(s.k_psum, 1)
                if active(base, i, 1):
                    a = (i + 1) % 2
                    pe.wait_ge(s.sq_split, (n + 2) * 2)
                    if due(n + 1):
                        pe.wait_ge(s.norm_read, n + 1)
                    for kt in range(PER):
                        for part in range(2):
                            last = mm(bank[NORM_BANK][:, a * PER + kt:a * PER + kt + 1],
                                      ksq16[:, a, part, kt * P:(kt + 1) * P], ones16[:, 0:1],
                                      start=part == 0, stop=part == 1)
                    last.then_inc(s.norm_psum, 1)
                if i % NCH == 1 and active(base, i, -2):
                    h = hb + i // NCH - 1
                    pe.wait_ge(s.max_diag, h + 1)
                    mm(bank[MISC][:, 0:TOK], ones[:, :], diag[:, :, :], start=True, stop=True
                       ).then_inc(s.max_b, 1)
                if active(base, i, 0):
                    a = i % 2
                    h = hb + i // NCH
                    pe.wait_ge(s.k_lo, n + 1)
                    for b in range(2):
                        if due(n * PER - PER + 2 * b + 2):
                            pe.wait_ge(s.s_kept, n * PER - PER + 2 * b + 2)
                        for k in range(2):
                            rows = slice((2 * b + k) * P, (2 * b + k + 1) * P)
                            dst = bank[S_BANK[b]][:, k * TOK:(k + 1) * TOK]
                            q_hi, q_lo = (q16[:, bass.ds(h, 1), part, :] for part in range(2))
                            mm(dst, k16[:, a, 0, rows], q_hi, start=True, stop=False)
                            mm(dst, k16[:, a, 0, rows], q_lo, start=False, stop=False)
                            last = mm(dst, k16[:, a, 1, rows], q_hi, start=False, stop=True)
                        last.then_inc(s.s_psum, 1)
                if active(base, i, -PV_LAG):
                    v = n - PV_LAG
                    a, j = (i - PV_LAG) % 2, (i - PV_LAG) % NCH
                    pe.wait_ge(s.p_lo, v + 1)
                    for t in range(QT):
                        cols = slice(t * P, (t + 1) * P)
                        dst = bank[T_BANK[t]]
                        ended = (hb + (i - PV_LAG) // NCH) * QT - QT + t + 1
                        if j == 0 and due(ended):
                            pe.wait_ge(s.t_norm, ended)
                        for kt in range(PER):
                            tile = j * PER + kt
                            mm(dst[:, 0:CD + 1], p16[:, a, 0, kt, cols], ctx_hi[:, tile, 0:CD + 1],
                               start=j == 0 and kt == 0, stop=False)
                            mm(dst[:, 0:CD], p16[:, a, 0, kt, cols], ctx_lo[:, tile, :], start=False, stop=False)
                            last = mm(dst[:, 0:CD + 1], p16[:, a, 1, kt, cols], ctx_hi[:, tile, 0:CD + 1],
                                      start=False, stop=j == NCH - 1 and kt == PER - 1)
                        if j == NCH - 1 and t == 0:
                            last.then_inc(s.t_sum, 1)
                    last.then_inc(s.pv_done, 1)
                if i % NCH == 0 and active(base, i, -1):
                    h = hb + i // NCH - 1
                    pe.wait_ge(s.max_done, (h + 1) * (NCH + 1))
                    if due(h):
                        pe.wait_ge(s.max_row, h)
                    if due(h):
                        pe.wait_ge(s.o_kept, h)
                    for t in range(QT):
                        last = nc.tensor.transpose(bank[MISC][:, t * P:(t + 1) * P],
                                                   foldmax[:, t * P:(t + 1) * P], ident[:, :])
                    last.then_inc(s.max_T, 1)
                if (i - PV_LAG) % NCH == 1 and head_ended(base, i):
                    h = hb + (i - PV_LAG - 1) // NCH
                    pe.wait_ge(s.t_norm, h * QT)
                    pe.wait_ge(s.max_row, min(h + 1, XH) if isinstance(h, int) else h + 1)
                    for c in range(KC):
                        for t in range(QT):
                            last = nc.tensor.transpose(bank[MISC][:, c * TOK + t * P:c * TOK + (t + 1) * P],
                                                       tn[:, t, c * P:(c + 1) * P], ident[:, :])
                    last.then_inc(s.t_T, 1)
                if (i - PV_LAG) % NCH == 2 and head_ended(base, i):
                    h = hb + (i - PV_LAG - 2) // NCH
                    pe.wait_ge(s.t_lo, h)
                    hs = bass.ds((h - 1) * XD, XD)
                    split_products(bank[MISC][:, 0:TOK],
                                   lambda k: wv16[:, 0, k, hs], lambda k: wv16[:, 1, k, hs],
                                   lambda k: tT16[:, 0, k, :], lambda k: tT16[:, 1, k, :], range(KC)
                                   ).then_inc(s.o_psum, 1)

            pipeline(pe, step)

            pe.wait_ge(s.o_kept, XH + 1)
            pe.wait_ge(s.wo_in, 16)
            for t in range(QT):
                for h in range(XH):
                    last = mm(bank[t][:, :], o32[:, h, t * P:(t + 1) * P], wo_x[:, h, :],
                              start=h == 0, stop=h == XH - 1)
                last.then_inc(s.y_psum, 1)
                if t:
                    ln_pe(1, 0, xn, bank[6])
            ln_pe(1, 1, xn, bank[7])
            pe.wait_ge(s.ln_out, 2 * QT)
            pe.wait_ge(s.watt_in, 48)
            for w, b0 in ((w_att[0], 0), (w_att[1], 2)):
                for m in range(CT):
                    for k in range(CT):
                        last = mm(bank[b0 + m // 2][:, (m % 2) * TOK:(m % 2 + 1) * TOK],
                                  w[:, k, m * P:(m + 1) * P], xnT[:, k, :], start=k == 0, stop=k == CT - 1)
                    last.then_inc(s.qk_psum, 1)

            def values(t):
                for k in range(CT):
                    last = mm(bank[4 + t][:, :], xnT[:, k, t * P:(t + 1) * P], w_att[2][:, k, :],
                              start=k == 0, stop=k == CT - 1)
                last.then_inc(s.qk_psum, 1)

            def a_scores(h):
                m, r = h // HPT, SD * (h % HPT)
                if h == 0:
                    pe.wait_ge(s.q_kept, 2)
                    pe.wait_ge(s.k_kept, 2)
                if h >= 2:
                    pe.wait_ge(s.a_masked, h - 1)
                for t in range(QT):
                    last = mm(bank[h % 2][:, t * TOK:(t + 1) * TOK], aq[r:r + SD, m, t * P:(t + 1) * P],
                              ak[r:r + SD, m, :], start=True, stop=True)
                last.then_inc(s.a_psum, 1)

            def a_transpose(h):
                pe.wait_ge(s.a_exp, (h + 1) * QT)
                if h >= 2:
                    pe.wait_ge(s.a_Tkept, h - 1)
                for k in range(QT):
                    for t in range(QT):
                        last = nc.tensor.transpose(bank[2 + h % 2][:, k * TOK + t * P:k * TOK + (t + 1) * P],
                                                   pr[:, h % 2, t, k * P:(k + 1) * P], ident[:, :])
                last.then_inc(s.a_T, 1)

            def a_out(h):
                pe.wait_ge(s.a_Tkept, h + 1)
                if h == 0:
                    pe.wait_ge(s.v_kept, 2)
                for t in range(QT):
                    for k in range(QT):
                        last = mm(bank[4 + t][:, h * SD:(h + 1) * SD], prT[:, h % 2, k, t * P:(t + 1) * P],
                                  av[:, k, h * SD:(h + 1) * SD], start=k == 0, stop=k == QT - 1)
                last.then_inc(s.ao_psum, 1)

            values(0)
            a_scores(0)
            a_scores(1)
            values(1)
            for h in range(2, SH + 3):
                if h < SH:
                    a_scores(h)
                if h - 2 < SH:
                    a_transpose(h - 2)
                if 0 <= h - 3:
                    a_out(h - 3)
            for t in range(QT):
                pe.wait_ge(s.an_done, t + 1)
                for c in range(CT):
                    last = nc.tensor.transpose(bank[6 + t][:, c * P:(c + 1) * P], an[:, t, c * P:(c + 1) * P],
                                               ident[:, :])
                last.then_inc(s.an_T, 1)
            pe.wait_ge(s.watt3_in, 16)
            for t in range(QT):
                pe.wait_ge(s.an_kept, t + 1)
                for k in range(CT):
                    last = mm(bank[t][:, :], anT[:, k, t * P:(t + 1) * P], w_att[3][:, k, :],
                              start=k == 0, stop=k == CT - 1)
                last.then_inc(s.ay_psum, 1)
            for t in range(QT):
                ln_pe(2, t, xn, bank[6 + t])
            pe.wait_ge(s.gate_lo, 1)
            for t in range(QT):
                pe.wait_ge(s.ln_out, 2 * QT + t + 1)
                cols = slice(t * P, (t + 1) * P)
                for k in range(CT):
                    for x_part in range(2):
                        for w_part in range(2):
                            last = mm(bank[4 + t][:, 0:NE], xn16T[:, x_part, k, cols], gate16[:, w_part, k, :],
                                      start=k + x_part + w_part == 0, stop=k + x_part + w_part == CT + 1)
                last.then_inc(s.g_psum, 1)

            def e_down(e, a):
                pe.wait_ge(s.h_kept, (e + 1) * len(HT))
                pe.wait_ge(s.wd_lo, e + 1)
                for t in range(QT):
                    if not isinstance(e, int) or e >= 1:
                        pe.wait_ge(s.moe_acc, (e - 1) * QT + t + 1)
                    cols = slice(t * P, (t + 1) * P)
                    for j, rows in enumerate(HT):
                        h_hi, h_lo = h16[0:rows, a, 0, j, cols], h16[0:rows, a, 1, j, cols]
                        w_hi, w_lo = wd16[a][0:rows, 0, j, :], wd16[a][0:rows, 1, j, :]
                        mm(bank[6 + t][:, :], h_hi, w_hi, start=j == 0, stop=False)
                        mm(bank[6 + t][:, :], h_hi, w_lo, start=False, stop=False)
                        last = mm(bank[6 + t][:, :], h_lo, w_hi, start=False, stop=j == len(HT) - 1)
                    last.then_inc(s.d_psum, 1)

            def expert(e, a, first, last_one):
                pe.wait_ge(s.gu_lo, e + 1)
                for j, rows in enumerate(HT):
                    u = e * len(HT) + j
                    b = (a * len(HT) + j) % 2
                    cols = slice(j * P, j * P + rows)
                    if not first or j >= 2:
                        pe.wait_ge(s.h_full, u - 1)
                    for w in range(2):
                        last = split_products(bank[2 * w + b][0:rows, 0:TOK],
                                              lambda k: gu16[a][:, 0, w, k, cols], lambda k: gu16[a][:, 1, w, k, cols],
                                              lambda k: xn16T[:, 0, k, :], lambda k: xn16T[:, 1, k, :], range(CT))
                    last.then_inc(s.h_psum, 1)
                if not first:
                    e_down(e - 1, 1 - a)

            experts(pe, expert)
            e_down(ALLE - 1, (ALLE - 1) % 2)


_INS = ['x', 'ctx_1024', 'L0_xattn_Wq', 'L0_xattn_Wk', 'L0_xattn_Wv', 'L0_xattn_Wo', 'L0_xattn_gq', 'L0_xattn_gk',
        'L0_attn_Wq', 'L0_attn_Wk', 'L0_attn_Wv', 'L0_attn_Wo', 'L0_ffn_gate_w', 'L0_ffn_w_gate', 'L0_ffn_w_up',
        'L0_ffn_w_down', 'L0_ffn_sw_gate', 'L0_ffn_sw_up', 'L0_ffn_sw_down']
_OUTS = [((1, 256, 512), 'float32')]


def kernel(**inputs):
    import numpy as _np
    import concourse.bacc as _bacc
    from concourse import mybir as _mybir
    from concourse.bass_utils import run_bass_kernel_spmd as _run

    nc = _bacc.Bacc("TRN2", target_bir_lowering=False, num_devices=1)
    arrays, args = {}, []
    for name in _INS:
        a = _np.ascontiguousarray(inputs[name])
        if name == 'ctx_1024':
            a = a.reshape(a.shape[1:])
        arrays[f"in_{name}_dram"] = a
        args.append(nc.dram_tensor(f"in_{name}_dram", a.shape, _mybir.dt.from_np(a.dtype), kind="ExternalInput").ap())
    for i, (shape, dtype) in enumerate(_OUTS):
        dt = _mybir.dt.from_np(_np.dtype(dtype))
        args.append(nc.dram_tensor(f"out_{i}_dram", shape, dt, kind="ExternalOutput").ap())
    perceiver_layer(nc, *args)
    r = _run(nc, [arrays], core_ids=[0])
    return r.results[0]["out_0_dram"]
```

```python
import concourse.bass as bass
from concourse import mybir
from contextlib import ExitStack

fp32 = mybir.dt.float32
fp16 = mybir.dt.float16
u32 = mybir.dt.uint32
ALU = mybir.AluOpType
ACT = mybir.ActivationFunctionType
AX = mybir.AxisListType

P = 128
TOK, DM = 256, 512
QT = TOK // P
CT = DM // P
CTX, CD = 4096, 256
KC = CD // P
XH, XD = 16, 128
NTILE = CTX // P
PER = 4
CHUNK = PER * P
NCH = NTILE // PER
TOTAL = XH * NCH
SLOTS = 2 * NCH
EXP_LAG, LO_LAG, PV_LAG = NCH + 1, NCH + 2, NCH + 3
WS = 64.0
KS = 0.5
SHIFT = 10.0
EPS = 1e-5
SH, SD = 16, 32
A_SCALE = 1.0 / TOK ** 0.5
HPT = P // SD
PR, T_LAG = 4, 3
NE, HID = 8, 352
ALLE = NE + 2
HT = [128, 128, 96]
WQG = 4


class Signals:

    def __init__(self, sem):
        self.x_in0 = sem("x_in0")
        self.x_in1 = sem("x_in1")
        self.gains_in = sem("gains_in")
        self.stage_in0 = sem("stage_in0")
        self.stage_in1 = sem("stage_in1")
        self.stage_in2 = sem("stage_in2")
        self.stage_in3 = sem("stage_in3")
        self.stage_in4 = sem("stage_in4")
        self.stage_in5 = sem("stage_in5")
        self.x1_in = sem("x1_in")
        self.wo_in = sem("wo_in")
        self.watt_in = sem("watt_in")
        self.watt3_in = sem("watt3_in")
        self.gate_in = sem("gate_in")
        self.gu_in0 = sem("gu_in0")
        self.gu_in1 = sem("gu_in1")
        self.wd_in0 = sem("wd_in0")
        self.wd_in1 = sem("wd_in1")
        self.out_done = sem("out_done")
        self.consts = sem("consts")
        self.w_hi = sem("w_hi")
        self.w_lo = sem("w_lo")
        self.dve_step = sem("dve_step")
        self.ln_stats = sem("ln_stats")
        self.ln_rstd = sem("ln_rstd")
        self.ln_xn = sem("ln_xn")
        self.ln_T = sem("ln_T")
        self.ln_hi = sem("ln_hi")
        self.ln_out = sem("ln_out")
        self.q_psum = sem("q_psum")
        self.q_raw = sem("q_raw")
        self.q_sq = sem("q_sq")
        self.q_ss = sem("q_ss")
        self.q_rms = sem("q_rms")
        self.q_scaled = sem("q_scaled")
        self.q_T = sem("q_T")
        self.q_hi = sem("q_hi")
        self.q_lo = sem("q_lo")
        self.c_khi = sem("c_khi")
        self.c_klo_g = sem("c_klo_g")
        self.c_klo_v = sem("c_klo_v")
        self.c_T = sem("c_T")
        self.c_hi = sem("c_hi")
        self.c_lo = sem("c_lo")
        self.k_psum = sem("k_psum")
        self.k_sq = sem("k_sq")
        self.k_hi = sem("k_hi")
        self.k_lo = sem("k_lo")
        self.sq_lo = sem("sq_lo")
        self.norm_psum = sem("norm_psum")
        self.norm_read = sem("norm_read")
        self.r_ready = sem("r_ready")
        self.s_psum = sem("s_psum")
        self.s_kept = sem("s_kept")
        self.s_shifted = sem("s_shifted")
        self.p_hi = sem("p_hi")
        self.p_full = sem("p_full")
        self.p_lo = sem("p_lo")
        self.pv_done = sem("pv_done")
        self.max_done = sem("max_done")
        self.max_T = sem("max_T")
        self.max_q = sem("max_q")
        self.max_diag = sem("max_diag")
        self.max_b = sem("max_b")
        self.max_row = sem("max_row")
        self.t_sum = sem("t_sum")
        self.t_rsum = sem("t_rsum")
        self.t_norm = sem("t_norm")
        self.t_T = sem("t_T")
        self.t_hi = sem("t_hi")
        self.t_lo = sem("t_lo")
        self.o_psum = sem("o_psum")
        self.o_kept = sem("o_kept")
        self.y_psum = sem("y_psum")
        self.qk_psum = sem("qk_psum")
        self.qk_hi = sem("qk_hi")
        self.qk_lo = sem("qk_lo")
        self.v_kept = sem("v_kept")
        self.mask_done = sem("mask_done")
        self.a_psum = sem("a_psum")
        self.a_masked = sem("a_masked")
        self.a_exp = sem("a_exp")
        self.a_T = sem("a_T")
        self.a_Tkept = sem("a_Tkept")
        self.a_rden = sem("a_rden")
        self.a_norm = sem("a_norm")
        self.ao_psum = sem("ao_psum")
        self.an_kept = sem("an_kept")
        self.ay_psum = sem("ay_psum")
        self.gate_hi = sem("gate_hi")
        self.gate_lo = sem("gate_lo")
        self.g_psum = sem("g_psum")
        self.gate_max = sem("gate_max")
        self.g_exp = sem("g_exp")
        self.gu_hi = sem("gu_hi")
        self.gu_lo = sem("gu_lo")
        self.wd_hi = sem("wd_hi")
        self.wd_lo = sem("wd_lo")
        self.h_psum = sem("h_psum")
        self.h_silu = sem("h_silu")
        self.h_full = sem("h_full")
        self.h_hi = sem("h_hi")
        self.h_kept = sem("h_kept")
        self.d_psum = sem("d_psum")
        self.moe_acc = sem("moe_acc")


def perceiver_layer(nc, x, ctx, wq, wk, wv, wo, gq, gk, swq, swk, swv, swo,
                    gate_w, w_gate, w_up, w_down, sw_gate, sw_up, sw_down, out):
    stack = ExitStack()
    with stack:
        def sem(name):
            return stack.enter_context(nc.semaphore(name))

        def pool_of(st):
            return lambda name, shape, dt: st.enter_context(nc.sbuf_tensor(name, shape, dt))

        keep = pool_of(stack)
        ident = keep("ident", [P, P], fp32)
        ones = keep("ones", [P, P], fp32)
        ones16 = keep("ones16", [P, 2], fp16)
        half_neg = keep("half_neg", [P, 32], fp32)
        ggT = keep("ggT", [P, 4], fp32)
        stats = keep("stats", [P, QT, 6], fp32)
        moments = keep("moments", [P, QT, 2], fp32)
        rstd = keep("rstd", [P, QT], fp32)
        q16 = keep("q16", [P, XH, 2, TOK], fp16)
        o32 = q16[:, :, :, :].rearrange("p h a q -> p (h a q)").bitcast(fp32).rearrange(
            "p (h q) -> p h q", h=XH)

        main = ExitStack()
        buf = pool_of(main)
        ctxT = buf("ctxT", [P, 2, KC, CTX], fp16)
        wk16 = buf("wk16", [P, 2, KC, XH * XD], fp16)
        early_end = nc.sbuf_base
        ctx_hi = buf("ctx_hi", [P, NTILE, CD + 2], fp16)
        ctx_lo = buf("ctx_lo", [P, NTILE, CD], fp16)
        ctx_end = nc.sbuf_base
        wv16 = buf("wv16", [P, 2, KC, XH * XD], fp16)
        k16 = buf("k16", [P, 2, 2, CHUNK], fp16)
        ksq = buf("ksq", [P, CHUNK], fp32)
        ksq16 = buf("ksq16", [P, 2, 2, CHUNK], fp16)
        p16 = buf("p16", [P, 2, 2, PER, TOK], fp16)
        norm = buf("norm", [P, 2, PER], fp32)
        r_key = buf("r_key", [P, 2, PER], fp32)
        runmax = buf("runmax", [P, PER, TOK], fp32)
        foldmax = buf("foldmax", [P, TOK], fp32)
        maxq = buf("maxq", [P, QT], fp32)
        diag = buf("diag", [P, QT, P], fp32)
        maxrow = buf("maxrow", [P, TOK], fp32)
        rsum = buf("rsum", [P, QT], fp32)
        tn = buf("tn", [P, QT, CD], fp32)
        tT16 = buf("tT16", [P, 2, KC, TOK], fp16)
        scores_at = nc.sbuf_base
        scores = buf("scores", [P, SLOTS, PER, TOK], fp32)
        main_end = nc.sbuf_base
        main.close()

        pre = ExitStack()
        pad = pre.enter_context(nc.sbuf_tensor("pad", [P, (scores_at - nc.sbuf_base) // 4], fp32))
        buf = pool_of(pre)
        stage = [buf("stage0", [P, 2048], fp32)]
        x0 = buf("x0", [P, QT, DM], fp32)
        stage += [buf(f"stage{i}", [P, 2048], fp32) for i in range(1, 5)]
        xn0T = buf("xn0T", [P, CT, TOK], fp32)
        q32 = buf("q32", [P, 2, QT, 4, XD], fp32)
        stage += [buf("stage5", [P, 2048], fp32)]
        assert nc.sbuf_base <= main_end, (nc.sbuf_base, main_end)
        pre.close()
        qsq = p16[:, 0, :, :, :].rearrange("p a k q -> p (a k q)").bitcast(fp32)
        q_ms, q_rs = diag[:, 0, :], diag[:, 1, :]

        tail = ExitStack()
        buf = pool_of(tail)
        wo_x = buf("wo_x", [P, XH, DM], fp32)
        x1 = buf("x1", [P, QT, DM], fp32)
        w_att3 = buf("w_att3", [P, CT, DM], fp32)
        gate_sb = buf("gate_sb", [P, CT, NE], fp32)
        assert nc.sbuf_base <= early_end
        gu_raw = [buf(f"gu_raw{i}", [P, 2, CT, HID], fp32) for i in range(2)]
        wd_raw = [buf(f"wd_raw{i}", [P, len(HT), DM], fp32) for i in range(2)]
        assert nc.sbuf_base <= ctx_end
        gu16 = [buf(f"gu16_{i}", [P, 2, 2, CT, HID], fp16) for i in range(2)]
        wd16_0 = buf("wd16_0", [P, 2, len(HT), DM], fp16)
        xn = buf("xn", [P, QT, DM], fp32)
        xnT = buf("xnT", [P, CT, TOK], fp32)
        tail.enter_context(nc.sbuf_tensor("gap", [P, (scores_at - nc.sbuf_base) // 4], fp32))
        w_att = [buf(f"w_att{i}", [P, CT, DM], fp32) for i in range(3)] + [w_att3]
        assert nc.sbuf_base <= scores_at + (main_end - scores_at) // 2
        wd16 = [wd16_0, buf("wd16_1", [P, 2, len(HT), DM], fp16)]
        xn16T = buf("xn16T", [P, 2, CT, TOK], fp16)
        aq = buf("aq", [P, 2, CT, TOK], fp16)
        ak = buf("ak", [P, 2, CT, TOK], fp16)
        av = buf("av", [P, QT, DM], fp32)
        anT = xnT
        lg = buf("lg", [P, QT, NE], fp32)
        gate16 = buf("gate16", [P, 2, CT, NE], fp16)
        gmax = buf("gmax", [P, QT], fp32)
        gsum = buf("gsum", [P, QT], fp32)
        grs = buf("grs", [P, QT], fp32)
        probs = buf("probs", [P, QT, NE], fp32)
        top = buf("top", [P, QT, 8], fp32)
        topi = buf("topi", [P, QT, 8], u32)
        topf = buf("topf", [P, QT, 8], fp32)
        lane = buf("lane", [P, NE], fp32)
        pick = buf("pick", [P, QT, 2, NE], fp32)
        comb = buf("comb", [P, QT, ALLE], fp32)
        att = ExitStack()
        buf = pool_of(att)
        mask = buf("mask", [P, QT, TOK], fp32)
        sm = buf("sm", [P, 2, QT, TOK], fp32)
        pr = buf("pr", [P, PR, QT, TOK], fp32)
        prT = buf("prT", [P, 2, QT, TOK], fp32)
        nmax = buf("nmax", [P, SH, QT], fp32)
        den = buf("den", [P, SH, QT], fp32)
        rden = buf("rden", [P, SH, QT], fp32)
        att.close()
        buf = pool_of(tail)
        silu = buf("silu", [P, 2, TOK], fp32)
        h32 = buf("h32", [P, 2, TOK], fp32)
        h16 = buf("h16", [P, 2, 2, len(HT), TOK], fp16)
        tail.close()

        bank = [stack.enter_context(nc.psum_tensor(f"bank{i}", [P, 512], fp32)) for i in range(8)]
        K_BANK, S_BANK, T_BANK, NORM_BANK, MISC = (0, 1), (2, 3), (4, 5), 6, 7

        Y_BANK = (0, 5)

        def Q_BANK(b):
            return (S_BANK if b < 2 else T_BANK)[b % 2]

        s = Signals(sem)
        x_in = [s.x_in0, s.x_in1]
        stage_in = [s.stage_in0, s.stage_in1, s.stage_in2, s.stage_in3, s.stage_in4, s.stage_in5]
        gu_in, wd_in = [s.gu_in0, s.gu_in1], [s.wd_in0, s.wd_in1]

        block = stack.enter_context(nc.Block())

        def due(value):
            return not isinstance(value, int) or value > 0

        ctx_v = ctx.rearrange("(p t) c -> p t c", p=P)
        STAGED = {("wq", 0): (0, 1), ("wk", 0): (2, 1), ("ctx", 0): (1, 1), ("ctx", 1): (3, 1),
                  ("ctx", 2): (4, 1), ("ctx", 3): (5, 1), ("wq", 1): (2, 2), ("wq", 2): (3, 2),
                  ("wq", 3): (4, 2), ("wv", 0): (5, 2), ("wv", 1): (5, 3), ("wk", 1): (5, 4)}

        def source(kind, g):
            if kind == "wq":
                return wq.rearrange("(t p) n -> p t n", p=P)[:, :, g * DM:(g + 1) * DM]
            if kind == "ctx":
                return ctx_v[:, g * 8:(g + 1) * 8, :]
            w = wk if kind == "wk" else wv
            return w.rearrange("(t p) n -> p t n", p=P)[:, :, g * 1024:(g + 1) * 1024]

        def staged(kind, g):
            t = {"wq": CT, "ctx": 8, "wk": KC, "wv": KC}[kind]
            return stage[STAGED[kind, g][0]][:, :].rearrange("p (t n) -> p t n", t=t)

        def arrived(kind, g):
            b, n = STAGED[kind, g]
            return stage_in[b], 16 * n

        def weight_part(kind, g, part):
            w = wk16 if kind == "wk" else wv16
            return w[:, part, :, g * 1024:(g + 1) * 1024]

        Q_BLOCK = {-2: 2, -1: 3, 3: 4, 4: 5, 6: 6, 7: 7}
        Q_SUMS = {2: 1, 4: 2, 7: 3}
        Q_RMS = {3: 1, 5: 2, 7: 3}
        Q_SCALE = {-2: 0, 4: 1, 6: 2, 8: 3}
        Q_TURN = {-1: 0, 5: 1, 7: 2, 9: 3}
        W_SPLIT = {7: ("wv", 0), 10: ("wv", 1), 13: ("wk", 1)}
        KLO_POOL = {-1: 0, 0: 1, 2: 4, 3: 5}
        KLO_DVE = (2, 3, 6, 7)
        W_ORDER = [("wk", 0), ("wv", 0), ("wv", 1), ("wk", 1)]

        def in_loops(eng, step, lo_peel, hi_peel, last):
            for n in range(*lo_peel):
                step(0, 0, n)
            with eng.Fori(hi_peel[0] // NCH, hi_peel[1] // NCH, 2) as hb:
                for i in range(SLOTS):
                    step(hb * NCH, hb, i)
            for i in range(last - hi_peel[1]):
                step(hi_peel[1], hi_peel[1] // NCH, i)

        def opening(base):
            return isinstance(base, int) and base == 0

        def staged_chunk(c):
            return staged("ctx", c // 2)[:, c % 2 * PER:(c % 2 + 1) * PER, :]

        def pipeline(eng, step):
            in_loops(eng, step, (-2, SLOTS), (SLOTS, TOTAL - SLOTS), TOTAL + PV_LAG + 3)

        def active(base, i, off):
            return not isinstance(base, int) or 0 <= base + i + off < TOTAL

        def head_ended(base, i):
            return not isinstance(base, int) or 1 <= (base + i - PV_LAG) // NCH <= XH

        def expert_loads(e, a):
            return (e - a) * 16 + 32

        def experts(eng, expert):
            expert(0, 0, True, False)
            expert(1, 1, False, False)
            with eng.Fori(2, NE - 1, 2) as e0:
                for a in range(2):
                    expert(e0 + a, a, False, False)
            expert(NE, 0, False, False)
            expert(NE + 1, 1, False, True)

        @block.sync
        def _(sp):
            x_v = x.rearrange("b (t p) d -> p (b t) d", p=P)
            for t in range(QT):
                sp.dma_start(x0[:, t, :], x_v[:, t, :]).then_inc(x_in[t], 16)
            sp.dma_start(ggT[:, 0:1], gq.rearrange("(p a) -> p a", a=1)).then_inc(s.gains_in, 16)
            sp.dma_start(ggT[:, 1:2], gk.rearrange("(p a) -> p a", a=1)).then_inc(s.gains_in, 16)

            def load(kind, g):
                b = STAGED[kind, g][0]
                sp.dma_start(staged(kind, g), source(kind, g)).then_inc(stage_in[b], 16)

            for what in (("wq", 0), ("wk", 0), ("ctx", 0), ("ctx", 1), ("ctx", 2)):
                load(*what)
            sp.wait_ge(s.w_lo, 1)
            load("wq", 1)
            load("ctx", 3)
            sp.wait_ge(s.c_T, 8)
            sp.wait_ge(s.c_khi, 4)
            sp.wait_ge(s.c_klo_v, 2)
            load("wq", 2)
            sp.wait_ge(s.c_T, 12)
            sp.wait_ge(s.c_khi, 6)
            sp.wait_ge(s.c_klo_g, 4)
            load("wq", 3)
            sp.wait_ge(s.c_T, 16)
            sp.wait_ge(s.c_khi, 8)
            sp.wait_ge(s.c_klo_v, 4)
            load("wv", 0)
            sp.wait_ge(s.w_lo, 2)
            load("wv", 1)
            sp.wait_ge(s.w_lo, 3)
            load("wk", 1)

            sp.wait_ge(s.k_psum, TOTAL)
            sp.dma_start(wo_x[:, :, :], wo.rearrange("(h p) n -> p h n", p=P)).then_inc(s.wo_in, 16)
            sp.dma_start(x1[:, :, :], x_v).then_inc(s.x1_in, 16)
            sp.dma_start(w_att3[:, :, :], swo.rearrange("(t p) n -> p t n", p=P)).then_inc(s.watt3_in, 16)
            sp.dma_start(gate_sb[:, :, :], gate_w.rearrange("(t p) n -> p t n", p=P)).then_inc(s.gate_in, 16)
            sp.wait_ge(s.p_lo, TOTAL - SLOTS // 2)
            for w, dst in zip((swq, swk, swv), w_att):
                sp.dma_start(dst[:, :, :], w.rearrange("(t p) n -> p t n", p=P)).then_inc(s.watt_in, 16)
            sp.wait_ge(s.pv_done, TOTAL)

            def load_gate_up(a, w_g, w_u):
                sp.dma_start(gu_raw[a][:, 0, :, :], w_g.rearrange("(t p) n -> p t n", p=P)).then_inc(gu_in[a], 16)
                sp.dma_start(gu_raw[a][:, 1, :, :], w_u.rearrange("(t p) n -> p t n", p=P)).then_inc(gu_in[a], 16)

            def load_down(a, w_d):
                sp.dma_start(wd_raw[a][:, 0:2, :],
                             w_d[0:2 * P, :].rearrange("(t p) n -> p t n", p=P)).then_inc(wd_in[a], 16)
                sp.dma_start(wd_raw[a][0:HT[2], 2, :], w_d[2 * P:HID, :]).then_inc(wd_in[a], 16)

            for e in range(2):
                load_gate_up(e, w_gate[e], w_up[e])
                load_down(e, w_down[e])
            with sp.Fori(2, NE - 1, 2) as e0:
                for a in range(2):
                    e = e0 + a
                    sp.wait_ge(s.gu_lo, e - 1)
                    row = bass.ds(e, 1)
                    load_gate_up(a, w_gate[row].rearrange("a d n -> (a d) n"),
                                 w_up[row].rearrange("a d n -> (a d) n"))
                    sp.wait_ge(s.wd_lo, e - 1)
                    load_down(a, w_down[row].rearrange("a d n -> (a d) n"))
            for e in range(NE, ALLE):
                a, c = e % 2, slice((e - NE) * HID, (e - NE + 1) * HID)
                sp.wait_ge(s.gu_lo, e - 1)
                load_gate_up(a, sw_gate[:, c], sw_up[:, c])
                sp.wait_ge(s.wd_lo, e - 1)
                load_down(a, sw_down[c, :])
            sp.wait_ge(s.moe_acc, ALLE * QT)
            sp.dma_start(out.rearrange("b (t p) d -> p (b t) d", p=P), x1[:, :, :]).then_inc(s.out_done, 16)
            sp.wait_ge(s.out_done, 16)

        @block.gpsimd
        def _(pool):
            pool.memset(ident[:, :], 0.0).then_inc(s.consts, 1)
            pool.wait_ge(s.consts, 1)
            pool.affine_select(out=ident[:, :], in_=ident[:, :], compare_op=ALU.not_equal, fill=1.0, base=0,
                               pattern=[[-1, P]], channel_multiplier=1).then_inc(s.consts, 1)
            pool.memset(ones[:, :], 1.0).then_inc(s.consts, 1)
            pool.memset(ones16[:, :], 1.0).then_inc(s.consts, 1)
            pool.memset(half_neg[:, :], -0.5).then_inc(s.consts, 1)
            pool.wait_ge(s.consts, 5)

            def ln_pool(k):
                for t in range(QT):
                    pool.wait_ge(s.ln_stats, k * QT + t + 1)
                    pool.tensor_tensor(out=rstd[:, t:t + 1], in0=moments[:, t, 1:2], in1=half_neg[:, 0:1],
                                       op=ALU.pow).then_inc(s.ln_rstd, 1)

            ln_pool(0)

            def q_rms(g):
                pool.wait_ge(s.q_ss, g + 1)
                pool.tensor_tensor(out=q_rs[:, g * 8:(g + 1) * 8], in0=q_ms[:, g * 8:(g + 1) * 8],
                                   in1=half_neg[:, 0:8], op=ALU.pow).then_inc(s.q_rms, 1)

            q_rms(0)

            def step(base, hb, i):
                n = base + i
                if active(base, i, 2):
                    a = (i + 2) % 2
                    pool.wait_ge(s.k_sq, (n + 3) * 2)
                    pool.tensor_tensor(out=ksq16[:, a, 1, :], in0=ksq[:, :], in1=ksq16[:, a, 0, :],
                                       op=ALU.subtract).then_inc(s.sq_lo, 1)
                if active(base, i, 1):
                    a = (i + 1) % 2
                    pool.wait_ge(s.norm_read, n + 2)
                    if not isinstance(base, int) or n + 1 >= 2:
                        pool.wait_ge(s.s_kept, (n - 1 + 1) * PER)
                    pool.tensor_tensor(out=r_key[:, a, :], in0=norm[:, a, :], in1=half_neg[:, 0:PER],
                                       op=ALU.pow).then_inc(s.r_ready, 1)
                if opening(base):
                    if n in Q_RMS:
                        q_rms(Q_RMS[n])
                    if n in KLO_POOL:
                        c = KLO_POOL[n]
                        pool.wait_ge(s.c_khi, c + 1)
                        rows = slice(c * PER, (c + 1) * PER)
                        pool.tensor_tensor(out=ctx_lo[:, rows, :], in0=staged_chunk(c), in1=ctx_hi[:, rows, 0:CD],
                                           op=ALU.subtract).then_inc(s.c_klo_g, 1)

            pipeline(pool, step)

            pool.wait_ge(s.pv_done, TOTAL)
            pool.memset(mask[:, :, :], A_SCALE).then_inc(s.mask_done, 1)
            pool.memset(comb[:, :, :], 1.0 / WS).then_inc(s.mask_done, 1)
            pool.wait_ge(s.mask_done, 2)
            pool.iota(lane[:, :], [[1, NE]], channel_multiplier=0, allow_small_or_imprecise_dtypes=True
                      ).then_inc(s.mask_done, 1)
            pool.affine_select(out=mask[:, :, :], in_=mask[:, :, :], compare_op=ALU.is_ge, fill=0.0, base=0,
                               pattern=[[P, QT], [-1, TOK]], channel_multiplier=1).then_inc(s.mask_done, 1)
            ln_pool(1)
            for h in range(SH):
                pool.wait_ge(s.a_rden, h + 1)
                pool.tensor_tensor(out=pr[:, h % PR, :, :], in0=pr[:, h % PR, :, :],
                                   in1=rden[:, h, :].unsqueeze(2).to_broadcast([P, QT, TOK]),
                                   op=ALU.mult).then_inc(s.a_norm, 1)
            ln_pool(2)

        @block.scalar
        def _(act):
            act_ = nc.scalar

            def q_raw(u):
                g, t = u // QT, u % QT
                src = bank[S_BANK[t] if u < QT else MISC]
                act.wait_ge(s.q_psum, u + 1)
                act_.activation(q32[:, g % 2, t, :, :], src[:, :].rearrange("p (h d) -> p h d", h=4),
                                ACT.Copy).then_inc(s.q_raw, 1)

            def q_square(g):
                act.wait_ge(s.q_raw, (g + 1) * QT)
                if g:
                    act.wait_ge(s.q_ss, g)
                act_.activation(qsq, q32[:, g % 2, :, :, :].rearrange("p t h d -> p (t h d)"), ACT.Square
                                ).then_inc(s.q_sq, 1)

            def q_hi(g):
                for b in (2 * g, 2 * g + 1):
                    act.wait_ge(s.q_T, b + 1)
                    act_.activation(q16[:, 2 * b:2 * b + 2, 0, :],
                                    bank[Q_BANK(b)][:, :].rearrange("p (h q) -> p h q", h=2),
                                    ACT.Copy, scale=ggT[:, 2:3]).then_inc(s.q_hi, 1)

            def w_hi(kind, g):
                act.wait_ge(*arrived(kind, g))
                act_.activation(weight_part(kind, g, 0), staged(kind, g), ACT.Copy, scale=WS).then_inc(s.w_hi, 1)

            def c_hi(c):
                for b in range(2):
                    act.wait_ge(s.c_T, 2 * c + b + 1)
                    act_.activation(ctxT[:, 0, :, (2 * c + b) * 2 * P:(2 * c + b + 1) * 2 * P],
                                    bank[T_BANK[b]][:, :].rearrange("p (c r) -> p c r", c=KC),
                                    ACT.Copy).then_inc(s.c_hi, 1)

            w_hi("wk", 0)
            q_raw(0)
            q_raw(1)
            c_hi(0)
            q_square(0)

            def step(base, hb, i):
                n = base + i
                if active(base, i, 2):
                    a = (i + 2) % 2
                    act.wait_ge(s.k_psum, n + 3)
                    if due(n + 2):
                        act.wait_ge(s.sq_lo, n + 2)
                    act_.activation(ksq[:, :], bank[K_BANK[a]][:, :], ACT.Square,
                                    scale=KS / WS).then_inc(s.k_sq, 1)
                    if due(n + 1):
                        act.wait_ge(s.norm_psum, n + 1)
                    act_.activation(ksq16[:, a, 0, :], bank[K_BANK[a]][:, :], ACT.Square,
                                    scale=KS / WS).then_inc(s.k_sq, 1)
                    if opening(base):
                        if n in Q_TURN:
                            q_hi(Q_TURN[n])
                        if n + 3 < NCH:
                            c_hi(n + 3)
                        if n in Q_BLOCK:
                            q_raw(Q_BLOCK[n])
                    if not isinstance(base, int) or n >= 0:
                        act.wait_ge(s.s_psum, (n + 1) * 2)
                    act_.activation(k16[:, a, 0, :], bank[K_BANK[a]][:, :], ACT.Copy,
                                    scale=1.0 / WS).then_inc(s.k_hi, 1)
                if active(base, i, -LO_LAG):
                    v = n - LO_LAG
                    slot = (i - LO_LAG) % SLOTS
                    a = (i - LO_LAG) % 2
                    act.wait_ge(s.p_full, v + 1)
                    if not isinstance(base, int) or v >= 2:
                        act.wait_ge(s.pv_done, v - 1)
                    act_.activation(p16[:, a, 0, :, :], scores[:, slot, :, :], ACT.Copy).then_inc(s.p_hi, 1)
                if active(base, i, 0):
                    a = i % 2
                    slot = i % SLOTS
                    act.wait_ge(s.r_ready, n + 1)
                    if not isinstance(base, int) or n >= SLOTS:
                        act.wait_ge(s.p_lo, n - SLOTS + 1)
                    if opening(base) and n == SLOTS - 2:
                        act.wait_ge(s.w_lo, len(W_ORDER))
                    for b in range(2):
                        act.wait_ge(s.s_psum, n * 2 + b + 1)
                        for k in range(2):
                            kt = 2 * b + k
                            act_.activation(scores[:, slot, kt, :], bank[S_BANK[b]][:, k * TOK:(k + 1) * TOK],
                                            ACT.Copy, scale=r_key[:, a, kt:kt + 1]).then_inc(s.s_kept, 1)
                if opening(base):
                    if n in Q_SUMS:
                        q_square(Q_SUMS[n])
                    if n in W_SPLIT:
                        w_hi(*W_SPLIT[n])
                if active(base, i, -EXP_LAG):
                    v = n - EXP_LAG
                    slot = (i - EXP_LAG) % SLOTS
                    act.wait_ge(s.s_shifted, v + 1)
                    act_.activation(scores[:, slot, :, :], scores[:, slot, :, :], ACT.Exp).then_inc(s.p_full, 1)
                if (i - PV_LAG) % NCH == 1 and head_ended(base, i):
                    h = hb + (i - PV_LAG - 1) // NCH
                    act.wait_ge(s.t_T, h)
                    act_.activation(tT16[:, 0, :, :], bank[MISC][:, :].rearrange("p (c q) -> p c q", c=KC),
                                    ACT.Copy).then_inc(s.t_hi, 1)

            pipeline(act, step)

            def gu_hi(e, a, expert_used):
                act.wait_ge(gu_in[a], expert_loads(e, a))
                if expert_used:
                    act.wait_ge(s.h_psum, (e - 1) * len(HT))
                for w in range(2):
                    act_.activation(gu16[a][:, 0, w, :, :], gu_raw[a][:, w, :, :], ACT.Copy, scale=WS
                                    ).then_inc(s.gu_hi, 1)

            def wd_hi(e, a, expert_used):
                act.wait_ge(wd_in[a], expert_loads(e, a))
                if expert_used:
                    act.wait_ge(s.d_psum, (e - 1) * QT)
                act_.activation(wd16[a][:, 0, 0:2, :], wd_raw[a][:, 0:2, :], ACT.Copy, scale=WS
                                ).then_inc(s.wd_hi, 1)
                act_.activation(wd16[a][0:HT[2], 0, 2, :], wd_raw[a][0:HT[2], 2, :], ACT.Copy, scale=WS
                                ).then_inc(s.wd_hi, 1)

            act.wait_ge(s.o_kept, XH + 1)
            for e in range(2):
                gu_hi(e, e, False)
                wd_hi(e, e, False)
            for w, dst in enumerate((aq, ak)):
                act.wait_ge(s.qk_psum, 2 * QT - 1 + w)
                for m in range(2):
                    act_.activation(dst[:, 0, 2 * m:2 * m + 2, :],
                                    bank[2 * w + m][:, :].rearrange("p (a q) -> p a q", a=2), ACT.Copy
                                    ).then_inc(s.qk_hi, 1)

            def a_exps(h):
                a = h % 2
                act.wait_ge(s.a_masked, h + 1)
                if h >= PR:
                    act.wait_ge(s.a_T, h - PR + 1)
                for t in range(QT):
                    act_.activation(pr[:, h % PR, t, :], sm[:, a, t, :], ACT.Exp,
                                    bias=nmax[:, h, t:t + 1], accum_out=den[:, h, t:t + 1]
                                    ).then_inc(s.a_exp, 1)

            def pT_kept(h):
                a = h % 2
                act.wait_ge(s.a_T, h + 1)
                if h >= 2:
                    act.wait_ge(s.ao_psum, h - 1)
                act_.activation(prT[:, a, :, :], bank[2 + a][:, :].rearrange("p (t q) -> p t q", t=QT), ACT.Copy
                                ).then_inc(s.a_Tkept, 1)

            for h in range(SH + T_LAG):
                if h >= T_LAG:
                    pT_kept(h - T_LAG)
                if h < SH:
                    a_exps(h)
            act.wait_ge(s.gate_in, 16)
            act_.activation(gate16[:, 0, :, :], gate_sb[:, :, :], ACT.Copy, scale=WS).then_inc(s.gate_hi, 1)
            for t in range(QT):
                act.wait_ge(s.ln_T, 2 * QT + t + 1)
                act_.activation(xn16T[:, 0, :, t * P:(t + 1) * P], bank[6 + t][:, :].rearrange("p (a q) -> p a q", a=CT),
                                ACT.Copy).then_inc(s.ln_hi, 1)
            act.wait_ge(s.gate_max, 1)
            for t in range(QT):
                act_.activation(probs[:, t, :], lg[:, t, :], ACT.Exp, bias=gmax[:, t:t + 1],
                                accum_out=gsum[:, t:t + 1]).then_inc(s.g_exp, 1)

            def expert(e, a, first, last):
                for j, rows in enumerate(HT):
                    u = e * len(HT) + j
                    b = (a * len(HT) + j) % 2
                    act.wait_ge(s.h_psum, u + 1)
                    if not first or j >= 2:
                        act.wait_ge(s.h_full, u - 1)
                    act_.activation(silu[0:rows, b, :], bank[b][0:rows, 0:TOK], ACT.Silu, scale=1.0 / WS
                                    ).then_inc(s.h_silu, 1)
                    act.wait_ge(s.h_full, u + 1)
                    if not first and j == 0:
                        if not isinstance(e, int) or e >= 2:
                            act.wait_ge(s.d_psum, (e - 1) * QT)
                    act_.activation(h16[0:rows, a, 0, j, :], h32[0:rows, b, :], ACT.Copy).then_inc(s.h_hi, 1)
                    if j == 0 and not first and not last:
                        gu_hi(e + 1, 1 - a, True)
                if not isinstance(e, int) or e >= 2:
                    wd_hi(e, a, True)

            experts(act, expert)

        @block.vector
        def _(dve):
            vec = nc.vector

            def chained(ins, count):
                ins.then_inc(s.dve_step, 1)
                dve.wait_ge(s.dve_step, count)

            steps = [0]

            def then(ins):
                steps[0] += 1
                chained(ins, steps[0])

            def ln_stats(k, t, src):
                then(vec.bn_stats(out=stats[:, t, :], in_=src[:, t, :]))
                then(vec.bn_aggr(out=moments[:, t, :], in_=stats[:, t, :]))
                vec.tensor_scalar(moments[:, t, 1:2], moments[:, t, 1:2], EPS, None, ALU.add
                                  ).then_inc(s.ln_stats, 1)

            def ln_scale(k, t, src, dst):
                dve.wait_ge(s.ln_rstd, k * QT + t + 1)
                vec.tensor_scalar(dst[:, t, :], src[:, t, :], moments[:, t, 0:1], rstd[:, t:t + 1],
                                  ALU.subtract, ALU.mult).then_inc(s.ln_xn, 1)

            def ln_lo(k, t, b, dst):
                cols = slice(t * P, (t + 1) * P)
                dve.wait_ge(s.ln_hi, t + 1)
                vec.tensor_tensor(dst[:, 1, :, cols], bank[b][:, :].rearrange("p (a q) -> p a q", a=CT),
                                  dst[:, 0, :, cols], ALU.subtract).then_inc(s.ln_out, 1)

            vec.memset(ctx_hi[:, :, CD:CD + 2], 1.0).then_inc(s.o_kept, 1)
            for t in range(QT):
                dve.wait_ge(x_in[t], 16)
                ln_stats(0, t, x0)
            for t in range(QT):
                ln_scale(0, t, x0, x0)
            for t in range(QT):
                dve.wait_ge(s.ln_T, t + 1)
                vec.tensor_copy(xn0T[:, :, t * P:(t + 1) * P],
                                bank[t][:, :].rearrange("p (a q) -> p a q", a=CT)).then_inc(s.ln_out, 1)

            def q_sums(g):
                dve.wait_ge(s.q_sq, g + 1)
                cols = slice(g * 8, (g + 1) * 8)
                then(vec.tensor_reduce(q_ms[:, cols], qsq.rearrange("p (h d) -> p h d", d=XD), AX.X, ALU.add))
                vec.tensor_scalar(q_ms[:, cols], q_ms[:, cols], 1.0 / XD, EPS, ALU.mult, ALU.add
                                  ).then_inc(s.q_ss, 1)

            def q_scale(g):
                dve.wait_ge(s.q_rms, g + 1)
                q = q32[:, g % 2, :, :, :].rearrange("p t h d -> p (t h) d")
                vec.tensor_tensor(q, q, q_rs[:, g * 8:(g + 1) * 8].unsqueeze(2).to_broadcast([P, 8, XD]), ALU.mult
                                  ).then_inc(s.q_scaled, 1)

            def q_lo(g):
                for b in (2 * g, 2 * g + 1):
                    dve.wait_ge(s.q_hi, b + 1)
                    vec.scalar_tensor_tensor(out=q16[:, 2 * b:2 * b + 2, 1, :],
                                             in0=bank[Q_BANK(b)][:, :].rearrange("p (h q) -> p h q", h=2),
                                             scalar=ggT[:, 2:3], in1=q16[:, 2 * b:2 * b + 2, 0, :],
                                             op0=ALU.mult, op1=ALU.subtract).then_inc(s.q_lo, 1)

            def w_lo(kind, g):
                dve.wait_ge(s.w_hi, W_ORDER.index((kind, g)) + 1)
                vec.scalar_tensor_tensor(out=weight_part(kind, g, 1), in0=staged(kind, g), scalar=WS,
                                         in1=weight_part(kind, g, 0), op0=ALU.mult, op1=ALU.subtract
                                         ).then_inc(s.w_lo, 1)

            def c_lo(c):
                for b in range(2):
                    dve.wait_ge(s.c_hi, 2 * c + b + 1)
                    cols = slice((2 * c + b) * 2 * P, (2 * c + b + 1) * 2 * P)
                    vec.tensor_tensor(ctxT[:, 1, :, cols],
                                      bank[T_BANK[b]][:, :].rearrange("p (c r) -> p c r", c=KC),
                                      ctxT[:, 0, :, cols], ALU.subtract).then_inc(s.c_lo, 1)

            def c_operand(c):
                rows = slice(c * PER, (c + 1) * PER)
                dve.wait_ge(*arrived("ctx", c // 2))
                vec.tensor_copy(ctx_hi[:, rows, 0:CD], staged_chunk(c)).then_inc(s.c_khi, 1)
                if c in KLO_DVE:
                    dve.wait_ge(s.c_khi, c + 1)
                    vec.tensor_tensor(ctx_lo[:, rows, :], staged_chunk(c), ctx_hi[:, rows, 0:CD],
                                      ALU.subtract).then_inc(s.c_klo_v, 1)

            dve.wait_ge(s.gains_in, 32)
            then(vec.tensor_tensor(ggT[:, 2:3], ggT[:, 0:1], ggT[:, 1:2], ALU.mult))
            w_lo("wk", 0)
            c_lo(0)
            q_sums(0)
            c_operand(0)

            def step(base, hb, i):
                n = base + i
                if i % NCH == 1 and active(base, i, -2):
                    h = hb + i // NCH - 1
                    dve.wait_ge(s.max_T, h + 1)
                    vec.tensor_reduce(maxq[:, :], bank[MISC][:, 0:TOK].rearrange("p (t r) -> p t r", t=QT),
                                      AX.X, ALU.max).then_inc(s.max_q, 1)
                    dve.wait_ge(s.max_q, h + 1)
                    for t in range(QT):
                        last = vec.tensor_scalar(diag[:, t, :], ident[:, :], maxq[:, t:t + 1], None, ALU.mult)
                    last.then_inc(s.max_diag, 1)
                if opening(base):
                    if n in Q_TURN:
                        q_lo(Q_TURN[n])
                    if n + 3 < NCH:
                        c_lo(n + 3)
                    if n in Q_SCALE:
                        q_scale(Q_SCALE[n])
                if active(base, i, 2):
                    a = (i + 2) % 2
                    dve.wait_ge(s.k_hi, n + 3)
                    vec.scalar_tensor_tensor(out=k16[:, a, 1, :], in0=bank[K_BANK[a]][:, :], scalar=1.0 / WS,
                                             in1=k16[:, a, 0, :], op0=ALU.mult, op1=ALU.subtract
                                             ).then_inc(s.k_lo, 1)
                if active(base, i, 1):
                    a = (i + 1) % 2
                    dve.wait_ge(s.norm_psum, n + 2)
                    if not isinstance(base, int) or n + 1 >= 2:
                        dve.wait_ge(s.r_ready, n)
                    vec.tensor_scalar(norm[:, a, :], bank[NORM_BANK][:, a * PER:(a + 1) * PER],
                                      1.0 / KS ** 2, XD * EPS, ALU.mult, ALU.add).then_inc(s.norm_read, 1)
                if opening(base):
                    if n + 3 < NCH:
                        c_operand(n + 3)
                if i % NCH == 1 and active(base, i, -2):
                    h = hb + i // NCH - 1
                    dve.wait_ge(s.max_b, h + 1)
                    vec.tensor_scalar(maxrow[:, :], bank[MISC][:, 0:TOK], -SHIFT, None, ALU.add
                                      ).then_inc(s.max_row, 1)
                if active(base, i, -EXP_LAG):
                    v = n - EXP_LAG
                    slot = (i - EXP_LAG) % SLOTS
                    dve.wait_ge(s.max_row, hb + (i - EXP_LAG) // NCH + 1)
                    vec.tensor_tensor(scores[:, slot, :, :], scores[:, slot, :, :],
                                      maxrow[:, :].unsqueeze(1).to_broadcast([P, PER, TOK]),
                                      ALU.subtract).then_inc(s.s_shifted, 1)
                if active(base, i, -LO_LAG):
                    a = (i - LO_LAG) % 2
                    slot = (i - LO_LAG) % SLOTS
                    dve.wait_ge(s.p_hi, n - LO_LAG + 1)
                    vec.tensor_tensor(p16[:, a, 1, :, :], scores[:, slot, :, :], p16[:, a, 0, :, :], ALU.subtract
                                      ).then_inc(s.p_lo, 1)
                if (i - PV_LAG) % NCH == NCH - 1 and head_ended(base, i + 1):
                    h = hb + (i + 1 - PV_LAG) // NCH
                    for t in range(QT):
                        if t == 0:
                            dve.wait_ge(s.t_sum, h)
                        else:
                            dve.wait_ge(s.pv_done, h * NCH)
                        vec.reciprocal(rsum[:, t:t + 1], bank[T_BANK[t]][:, CD:CD + 1]).then_inc(s.t_rsum, 1)
                        dve.wait_ge(s.t_rsum, h * QT - QT + t + 1)
                        vec.tensor_scalar(tn[:, t, :], bank[T_BANK[t]][:, 0:CD], rsum[:, t:t + 1], None,
                                          ALU.mult).then_inc(s.t_norm, 1)
                if active(base, i, 0):
                    j, slot = i % NCH, i % SLOTS
                    if j:
                        dve.wait_ge(s.s_kept, (n + 1) * PER)
                        first = scores[:, slot - 1, :, :] if j == 1 else runmax[:, :, :]
                        vec.tensor_tensor(runmax[:, :, :], first, scores[:, slot, :, :], ALU.max
                                          ).then_inc(s.max_done, 1)
                    if j == NCH - 1:
                        h = hb + i // NCH
                        done = h * (NCH + 1) + NCH - 1
                        dve.wait_ge(s.max_done, done)
                        vec.tensor_tensor(runmax[:, 0:2, :], runmax[:, 0:2, :], runmax[:, 2:4, :], ALU.max
                                          ).then_inc(s.max_done, 1)
                        dve.wait_ge(s.max_done, done + 1)
                        if not isinstance(base, int) or h >= 1:
                            dve.wait_ge(s.max_T, h)
                        vec.tensor_tensor(foldmax[:, :], runmax[:, 0, :], runmax[:, 1, :], ALU.max
                                          ).then_inc(s.max_done, 1)
                    elif j >= 1:
                        done = (hb + i // NCH) * (NCH + 1) + j
                        dve.wait_ge(s.max_done, done)
                if opening(base):
                    if n in Q_SUMS:
                        q_sums(Q_SUMS[n])
                    if n in W_SPLIT:
                        w_lo(*W_SPLIT[n])
                if (i - PV_LAG) % NCH == 1 and head_ended(base, i):
                    h = hb + (i - PV_LAG - 1) // NCH
                    dve.wait_ge(s.t_hi, h)
                    vec.tensor_tensor(tT16[:, 1, :, :], bank[MISC][:, :].rearrange("p (c q) -> p c q", c=KC),
                                      tT16[:, 0, :, :], ALU.subtract).then_inc(s.t_lo, 1)
                if (i - PV_LAG) % NCH == 2 and head_ended(base, i):
                    h = hb + (i - PV_LAG - 2) // NCH
                    dve.wait_ge(s.o_psum, h)
                    vec.tensor_scalar(o32[:, h - 1, :], bank[MISC][:, 0:TOK], 1.0 / WS, None, ALU.mult
                                      ).then_inc(s.o_kept, 1)

            pipeline(dve, step)

            def gu_lo(e, a):
                for w in range(2):
                    dve.wait_ge(s.gu_hi, 2 * e + w + 1)
                    last = vec.scalar_tensor_tensor(out=gu16[a][:, 1, w, :, :], in0=gu_raw[a][:, w, :, :], scalar=WS,
                                                    in1=gu16[a][:, 0, w, :, :], op0=ALU.mult, op1=ALU.subtract)
                    if w:
                        last.then_inc(s.gu_lo, 1)

            def wd_lo(e, a):
                for part in (slice(0, 2), slice(2, 3)):
                    rows = slice(0, P) if part.start == 0 else slice(0, HT[2])
                    dve.wait_ge(s.wd_hi, 2 * e + (part.start > 0) + 1)
                    last = vec.scalar_tensor_tensor(out=wd16[a][rows, 1, part, :], in0=wd_raw[a][rows, part, :],
                                                    scalar=WS, in1=wd16[a][rows, 0, part, :],
                                                    op0=ALU.mult, op1=ALU.subtract)
                last.then_inc(s.wd_lo, 1)

            gu_lo(0, 0)
            wd_lo(0, 0)
            dve.wait_ge(s.x1_in, 16)
            for t in range(QT):
                dve.wait_ge(s.y_psum, t + 1)
                then(vec.tensor_tensor(x1[:, t, :], bank[Y_BANK[t]][:, :], x1[:, t, :], ALU.add))
                ln_stats(1, t, x1)
                ln_scale(1, t, x1, xn)
                dve.wait_ge(s.ln_T, QT + t + 1)
                vec.tensor_copy(xnT[:, :, t * P:(t + 1) * P],
                                bank[6 + t][:, :].rearrange("p (a q) -> p a q", a=CT)).then_inc(s.ln_out, 1)
            gu_lo(1, 1)
            wd_lo(1, 1)
            for w, dst in enumerate((aq, ak)):
                for m in range(2):
                    dve.wait_ge(s.qk_hi, 2 * w + m + 1)
                    vec.tensor_tensor(dst[:, 1, 2 * m:2 * m + 2, :],
                                      bank[2 * w + m][:, :].rearrange("p (a q) -> p a q", a=2),
                                      dst[:, 0, 2 * m:2 * m + 2, :], ALU.subtract).then_inc(s.qk_lo, 1)
            dve.wait_ge(s.mask_done, 4)

            def masked(h):
                a = h % 2
                dve.wait_ge(s.a_psum, h + 1)
                if h >= 2:
                    dve.wait_ge(s.a_exp, (h - 1) * QT)
                then(vec.tensor_tensor(sm[:, a, :, :], bank[a][:, :].rearrange("p (t q) -> p t q", t=QT),
                                       mask[:, :, :], ALU.mult))
                vec.tensor_reduce(nmax[:, h, :], sm[:, a, :, :], AX.X, ALU.max, negate=True
                                  ).then_inc(s.a_masked, 1)

            def reciprocals(h):
                dve.wait_ge(s.a_exp, (h + 1) * QT)
                vec.reciprocal(rden[:, h, :], den[:, h, :]).then_inc(s.a_rden, 1)

            masked(0)
            masked(1)
            reciprocals(0)
            for t in range(QT):
                dve.wait_ge(s.qk_psum, 2 * QT + t + 1)
                vec.tensor_copy(av[:, t, :], bank[4 + t][:, :]).then_inc(s.v_kept, 1)
            def a_kept(m):
                dve.wait_ge(s.ao_psum, (m + 1) * HPT)
                vec.tensor_copy(anT[:, m, :], bank[4 + m][:, 0:TOK]
                                ).then_inc(s.an_kept, 1)

            for h in range(2, SH + T_LAG + 2):
                if h < SH:
                    masked(h)
                if h - 1 < SH:
                    reciprocals(h - 1)
                if h > T_LAG + 1 and (h - T_LAG - 2) % HPT == HPT - 1:
                    a_kept((h - T_LAG - 2) // HPT)
            dve.wait_ge(s.gate_hi, 1)
            vec.scalar_tensor_tensor(out=gate16[:, 1, :, :], in0=gate_sb[:, :, :], scalar=WS, in1=gate16[:, 0, :, :],
                                     op0=ALU.mult, op1=ALU.subtract).then_inc(s.gate_lo, 1)
            for t in range(QT):
                dve.wait_ge(s.ay_psum, t + 1)
                then(vec.tensor_tensor(x1[:, t, :], bank[t][:, :], x1[:, t, :], ALU.add))
                ln_stats(2, t, x1)
                ln_scale(2, t, x1, xn)
                ln_lo(2, t, 6 + t, xn16T)
            for t in range(QT):
                dve.wait_ge(s.g_psum, t + 1)
                then(vec.tensor_scalar(lg[:, t, :], bank[4 + t][:, 0:NE], 1.0 / WS, None, ALU.mult))
            vec.tensor_reduce(gmax[:, :], lg[:, :, :], AX.X, ALU.max, negate=True).then_inc(s.gate_max, 1)

            def gate_shares(t):
                dve.wait_ge(s.g_exp, t + 1)
                then(vec.reciprocal(grs[:, t:t + 1], gsum[:, t:t + 1]))
                then(vec.tensor_scalar(probs[:, t, :], probs[:, t, :], grs[:, t:t + 1], None, ALU.mult))
                then(vec.max(out=top[:, t, :], in_=probs[:, t, :]))
                then(vec.max_index(out=topi[:, t, :], in_max=top[:, t, :], in_values=probs[:, t, :]))
                then(vec.tensor_copy(topf[:, t, :], topi[:, t, :]))
                for c in range(2):
                    then(vec.tensor_scalar(pick[:, t, c, :], lane[:, :], topf[:, t, c:c + 1], 1.0 / WS,
                                           ALU.is_equal, ALU.mult))
                then(vec.tensor_tensor(pick[:, t, 0, :], pick[:, t, 0, :], pick[:, t, 1, :], ALU.add))
                then(vec.tensor_tensor(comb[:, t, 0:NE], pick[:, t, 0, :], probs[:, t, :], ALU.mult))

            def down(e, at):
                for t in range(QT):
                    dve.wait_ge(s.d_psum, e * QT + t + 1)
                    vec.scalar_tensor_tensor(out=x1[:, t, :], in0=bank[6 + t][:, :], scalar=comb[:, t, at],
                                             in1=x1[:, t, :], op0=ALU.mult, op1=ALU.add
                                             ).then_inc(s.moe_acc, 1)

            def expert(e, a, first, last):
                for j, rows in enumerate(HT):
                    u = e * len(HT) + j
                    b = (a * len(HT) + j) % 2
                    dve.wait_ge(s.h_silu, u + 1)
                    if not first or j >= 2:
                        dve.wait_ge(s.h_hi, u - 1)
                    vec.scalar_tensor_tensor(out=h32[0:rows, b, :], in0=bank[2 + b][0:rows, 0:TOK], scalar=1.0 / WS,
                                             in1=silu[0:rows, b, :], op0=ALU.mult, op1=ALU.mult
                                             ).then_inc(s.h_full, 1)
                    dve.wait_ge(s.h_hi, u + 1)
                    vec.tensor_tensor(h16[0:rows, a, 1, j, :], h32[0:rows, b, :], h16[0:rows, a, 0, j, :],
                                      ALU.subtract).then_inc(s.h_kept, 1)
                    if first and j < QT:
                        gate_shares(j)
                    if j == 0 and not first and not last:
                        gu_lo(e + 1, 1 - a)
                if not isinstance(e, int) or e >= 2:
                    wd_lo(e, a)
                if not first:
                    down(e - 1, bass.ds(e - 1, 1))

            experts(dve, expert)
            down(ALLE - 1, slice(ALLE - 1, ALLE))

        @block.tensor
        def _(pe):
            mm = nc.tensor.matmul

            def split_products(out_, w_hi, w_lo, x_hi, x_lo, steps):
                last = None
                for k in steps:
                    first, final = k == steps[0], k == steps[-1]
                    mm(out_, w_hi(k), x_hi(k), start=first, stop=False)
                    mm(out_, w_hi(k), x_lo(k), start=False, stop=False)
                    last = mm(out_, w_lo(k), x_hi(k), start=False, stop=final)
                return last

            def ln_pe(k, t, src, dst):
                pe.wait_ge(s.ln_xn, k * QT + t + 1)
                for c in range(CT):
                    last = nc.tensor.transpose(dst[:, c * P:(c + 1) * P], src[:, t, c * P:(c + 1) * P], ident[:, :])
                last.then_inc(s.ln_T, 1)

            pe.wait_ge(s.consts, 5)
            for t in range(QT):
                ln_pe(0, t, x0, bank[t])
            pe.wait_ge(s.ln_out, QT)

            def ctx_transpose(c):
                pe.wait_ge(*arrived("ctx", c // 2))
                for b in range(2):
                    if c:
                        pe.wait_ge(s.c_lo, 2 * c + b - 1)
                    for f in range(KC):
                        for k in range(2):
                            last = nc.tensor.transpose(bank[T_BANK[b]][:, (f * 2 + k) * P:(f * 2 + k + 1) * P],
                                                       staged_chunk(c)[:, 2 * b + k, f * P:(f + 1) * P],
                                                       ident[:, :])
                    last.then_inc(s.c_T, 1)

            def q_project(u):
                g, t = u // QT, u % QT
                pe.wait_ge(*arrived("wq", g))
                if u > QT:
                    pe.wait_ge(s.q_raw, u)
                for k in range(CT):
                    last = mm(bank[S_BANK[t] if u < QT else MISC][:, :], xn0T[:, k, t * P:(t + 1) * P],
                              staged("wq", g)[:, k, :], start=k == 0, stop=k == CT - 1)
                last.then_inc(s.q_psum, 1)

            def q_transpose(g):
                pe.wait_ge(s.q_scaled, g + 1)
                for b in (2 * g, 2 * g + 1):
                    if b >= 4:
                        pe.wait_ge(s.q_lo, b - 1)
                    for c in range(2):
                        for t in range(QT):
                            last = nc.tensor.transpose(bank[Q_BANK(b)][:, (c * QT + t) * P:(c * QT + t + 1) * P],
                                                       q32[:, g % 2, t, 2 * (b % 2) + c, :], ident[:, :])
                    last.then_inc(s.q_T, 1)

            q_project(0)
            q_project(1)
            ctx_transpose(0)
            pe.wait_ge(s.w_lo, 1)

            def out_project(t, heads):
                for h in heads:
                    last = mm(bank[Y_BANK[t]][:, :], o32[:, h, t * P:(t + 1) * P], wo_x[:, h, :],
                              start=h == 0, stop=h == XH - 1)
                if h == XH - 1:
                    last.then_inc(s.y_psum, 1)

            def head_slice(hb, i, off):
                return bass.ds((hb + (i + off) // NCH) * XD, XD)

            def step(base, hb, i):
                n = base + i
                if active(base, i, 2):
                    a, j = (i + 2) % 2, (i + 2) % NCH
                    if due(n + 1):
                        pe.wait_ge(s.k_lo, n + 1)
                    if opening(base) and n + 2 < NCH:
                        pe.wait_ge(s.c_lo, 2 * (n + 3))
                    cols = slice(j * CHUNK, (j + 1) * CHUNK)
                    hs = head_slice(hb, i, 2)
                    split_products(bank[K_BANK[a]][:, :],
                                   lambda k: wk16[:, 0, k, hs], lambda k: wk16[:, 1, k, hs],
                                   lambda k: ctxT[:, 0, k, cols], lambda k: ctxT[:, 1, k, cols], range(KC)
                                   ).then_inc(s.k_psum, 1)
                if opening(base):
                    if n in Q_TURN:
                        q_transpose(Q_TURN[n])
                    if n + 3 < NCH:
                        ctx_transpose(n + 3)
                    if n in Q_BLOCK:
                        q_project(Q_BLOCK[n])
                if active(base, i, 1):
                    a = (i + 1) % 2
                    pe.wait_ge(s.sq_lo, n + 2)
                    if due(n + 1):
                        pe.wait_ge(s.norm_read, n + 1)
                    for kt in range(PER):
                        for part in range(2):
                            last = mm(bank[NORM_BANK][:, a * PER + kt:a * PER + kt + 1],
                                      ksq16[:, a, part, kt * P:(kt + 1) * P], ones16[:, 0:1],
                                      start=part == 0, stop=part == 1)
                    last.then_inc(s.norm_psum, 1)
                if active(base, i, 0):
                    a = i % 2
                    h = hb + i // NCH
                    pe.wait_ge(s.k_lo, n + 1)
                    if opening(base) and n == 0:
                        pe.wait_ge(s.q_lo, 2)
                    for b in range(2):
                        if due(n * PER - PER + 2 * b + 2):
                            pe.wait_ge(s.s_kept, n * PER - PER + 2 * b + 2)
                        for k in range(2):
                            rows = slice((2 * b + k) * P, (2 * b + k + 1) * P)
                            dst = bank[S_BANK[b]][:, k * TOK:(k + 1) * TOK]
                            q_hi, q_lo = (q16[:, bass.ds(h, 1), part, :] for part in range(2))
                            mm(dst, k16[:, a, 0, rows], q_hi, start=True, stop=False)
                            mm(dst, k16[:, a, 0, rows], q_lo, start=False, stop=False)
                            last = mm(dst, k16[:, a, 1, rows], q_hi, start=False, stop=True)
                        last.then_inc(s.s_psum, 1)
                if i % NCH == 1 and active(base, i, -2):
                    h = hb + i // NCH - 1
                    pe.wait_ge(s.max_diag, h + 1)
                    mm(bank[MISC][:, 0:TOK], ones[:, :], diag[:, :, :], start=True, stop=True
                       ).then_inc(s.max_b, 1)
                if active(base, i, -PV_LAG):
                    v = n - PV_LAG
                    a, j = (i - PV_LAG) % 2, (i - PV_LAG) % NCH
                    pe.wait_ge(s.p_lo, v + 1)
                    if opening(base) and v == 0:
                        pe.wait_ge(s.c_khi, NCH)
                        pe.wait_ge(s.c_klo_g, len(KLO_POOL))
                        pe.wait_ge(s.c_klo_v, len(KLO_DVE))
                        pe.wait_ge(s.q_lo, XH // 2)
                    if opening(base) and n == SLOTS - 1:
                        pe.wait_ge(s.w_lo, len(W_ORDER))
                    for t in range(QT):
                        cols = slice(t * P, (t + 1) * P)
                        dst = bank[T_BANK[t]]
                        ended = (hb + (i - PV_LAG) // NCH) * QT - QT + t + 1
                        if j == 0 and due(ended):
                            pe.wait_ge(s.t_norm, ended)
                        for kt in range(PER):
                            tile = j * PER + kt
                            mm(dst[:, 0:CD + 1], p16[:, a, 0, kt, cols], ctx_hi[:, tile, 0:CD + 1],
                               start=j == 0 and kt == 0, stop=False)
                            mm(dst[:, 0:CD], p16[:, a, 0, kt, cols], ctx_lo[:, tile, :], start=False, stop=False)
                            last = mm(dst[:, 0:CD + 1], p16[:, a, 1, kt, cols], ctx_hi[:, tile, 0:CD + 1],
                                      start=False, stop=j == NCH - 1 and kt == PER - 1)
                        if j == NCH - 1 and t == 0:
                            last.then_inc(s.t_sum, 1)
                    last.then_inc(s.pv_done, 1)
                if i % NCH == 0 and active(base, i, -1):
                    h = hb + i // NCH - 1
                    pe.wait_ge(s.max_done, (h + 1) * (NCH + 1))
                    if opening(base) and h == 0:
                        pe.wait_ge(s.q_raw, WQG * QT)
                    if due(h):
                        pe.wait_ge(s.max_row, h)
                    if due(h):
                        pe.wait_ge(s.o_kept, h)
                    for t in range(QT):
                        last = nc.tensor.transpose(bank[MISC][:, t * P:(t + 1) * P],
                                                   foldmax[:, t * P:(t + 1) * P], ident[:, :])
                    last.then_inc(s.max_T, 1)
                if isinstance(base, int) and base and n == TOTAL + PV_LAG:
                    pe.wait_ge(s.wo_in, 16)
                    pe.wait_ge(s.o_kept, XH)
                    out_project(0, range(XH - 4))
                if (i - PV_LAG) % NCH == 1 and head_ended(base, i):
                    h = hb + (i - PV_LAG - 1) // NCH
                    pe.wait_ge(s.t_norm, h * QT)
                    pe.wait_ge(s.max_row, min(h + 1, XH) if isinstance(h, int) else h + 1)
                    for c in range(KC):
                        for t in range(QT):
                            last = nc.tensor.transpose(bank[MISC][:, c * TOK + t * P:c * TOK + (t + 1) * P],
                                                       tn[:, t, c * P:(c + 1) * P], ident[:, :])
                    last.then_inc(s.t_T, 1)
                if isinstance(base, int) and base and n == TOTAL + PV_LAG + 1:
                    out_project(0, range(XH - 4, XH - 1))
                if (i - PV_LAG) % NCH == 2 and head_ended(base, i):
                    h = hb + (i - PV_LAG - 2) // NCH
                    pe.wait_ge(s.t_lo, h)
                    hs = bass.ds((h - 1) * XD, XD)
                    split_products(bank[MISC][:, 0:TOK],
                                   lambda k: wv16[:, 0, k, hs], lambda k: wv16[:, 1, k, hs],
                                   lambda k: tT16[:, 0, k, :], lambda k: tT16[:, 1, k, :], range(KC)
                                   ).then_inc(s.o_psum, 1)

            pipeline(pe, step)

            out_project(1, range(4))
            pe.wait_ge(s.o_kept, XH + 1)
            out_project(0, (XH - 1,))
            out_project(1, range(4, 12))
            ln_pe(1, 0, xn, bank[6])
            out_project(1, range(12, XH))
            pe.wait_ge(s.watt_in, 48)
            for t in range(QT):
                pe.wait_ge(s.ln_out, QT + t + 1)
                for w, b0 in ((w_att[0], 0), (w_att[1], 2)):
                    if t == 0 and b0:
                        ln_pe(1, 1, xn, bank[7])
                    for m in range(CT):
                        at = (m % 2) * TOK + t * P
                        for k in range(CT):
                            last = mm(bank[b0 + m // 2][:, at:at + P], w[:, k, m * P:(m + 1) * P],
                                      xnT[:, k, t * P:(t + 1) * P], start=k == 0, stop=k == CT - 1)
                    last.then_inc(s.qk_psum, 1)

            def values(t):
                for k in range(CT):
                    last = mm(bank[4 + t][:, :], xnT[:, k, t * P:(t + 1) * P], w_att[2][:, k, :],
                              start=k == 0, stop=k == CT - 1)
                last.then_inc(s.qk_psum, 1)

            def a_scores(h):
                m, r = h // HPT, SD * (h % HPT)
                if h == 0:
                    pe.wait_ge(s.qk_lo, 4)
                if h >= 2:
                    pe.wait_ge(s.a_masked, h - 1)
                for t in range(QT):
                    q_hi, q_lo = (aq[r:r + SD, part, m, t * P:(t + 1) * P] for part in range(2))
                    k_hi, k_lo = (ak[r:r + SD, part, m, :] for part in range(2))
                    dst = bank[h % 2][:, t * TOK:(t + 1) * TOK]
                    mm(dst, q_hi, k_hi, start=True, stop=False)
                    mm(dst, q_hi, k_lo, start=False, stop=False)
                    last = mm(dst, q_lo, k_hi, start=False, stop=True)
                last.then_inc(s.a_psum, 1)

            def a_transpose(h):
                pe.wait_ge(s.a_norm, h + 1)
                if h >= 2:
                    pe.wait_ge(s.a_Tkept, h - 1)
                for k in range(QT):
                    for t in range(QT):
                        last = nc.tensor.transpose(bank[2 + h % 2][:, k * TOK + t * P:k * TOK + (t + 1) * P],
                                                   pr[:, h % PR, t, k * P:(k + 1) * P], ident[:, :])
                last.then_inc(s.a_T, 1)

            def a_out(h):
                pe.wait_ge(s.a_Tkept, h + 1)
                if h == 0:
                    pe.wait_ge(s.v_kept, 2)
                m, r = h // HPT, SD * (h % HPT)
                for k in range(QT):
                    last = mm(bank[4 + m][r:r + SD, 0:TOK],
                              av[:, k, h * SD:(h + 1) * SD], prT[:, h % 2, k, :], start=k == 0, stop=k == QT - 1)

                last.then_inc(s.ao_psum, 1)

            values(0)
            a_scores(0)
            a_scores(1)
            values(1)
            for h in range(2, SH + T_LAG + 1):
                if h < SH:
                    a_scores(h)
                if 0 <= h - T_LAG < SH:
                    a_transpose(h - T_LAG)
                if 0 <= h - T_LAG - 1:
                    a_out(h - T_LAG - 1)
            pe.wait_ge(s.watt3_in, 16)
            for t in range(QT):
                for k in range(CT):
                    if not t:
                        pe.wait_ge(s.an_kept, k + 1)
                    elif k == CT - 1:
                        ln_pe(2, 0, xn, bank[6])
                    last = mm(bank[t][:, :], anT[:, k, t * P:(t + 1) * P], w_att[3][:, k, :],
                              start=k == 0, stop=k == CT - 1)
                last.then_inc(s.ay_psum, 1)
            def hidden(e, a, j, cols):
                b, rows = (a * len(HT) + j) % 2, HT[j]
                units = slice(j * P, j * P + rows)
                for w in range(2):
                    last = split_products(bank[2 * w + b][0:rows, cols],
                                          lambda k: gu16[a][:, 0, w, k, units], lambda k: gu16[a][:, 1, w, k, units],
                                          lambda k: xn16T[:, 0, k, cols], lambda k: xn16T[:, 1, k, cols], range(CT))
                return last

            pe.wait_ge(s.gate_lo, 1)
            for t in range(QT):
                pe.wait_ge(s.ln_out, 2 * QT + t + 1)
                cols = slice(t * P, (t + 1) * P)
                for k in range(CT):
                    for x_part in range(2):
                        for w_part in range(2):
                            last = mm(bank[4 + t][:, 0:NE], xn16T[:, x_part, k, cols], gate16[:, w_part, k, :],
                                      start=k + x_part + w_part == 0, stop=k + x_part + w_part == CT + 1)
                last.then_inc(s.g_psum, 1)
                pe.wait_ge(s.gu_lo, 1)
                for j in range(2):
                    if t == 0 and j == 1:
                        ln_pe(2, 1, xn, bank[7])
                    last = hidden(0, 0, j, cols)
                    if t:
                        last.then_inc(s.h_psum, 1)

            def e_down(e, a):
                pe.wait_ge(s.h_kept, (e + 1) * len(HT))
                pe.wait_ge(s.wd_lo, e + 1)
                for t in range(QT):
                    if not isinstance(e, int) or e >= 1:
                        pe.wait_ge(s.moe_acc, (e - 1) * QT + t + 1)
                    cols = slice(t * P, (t + 1) * P)
                    for j, rows in enumerate(HT):
                        h_hi, h_lo = h16[0:rows, a, 0, j, cols], h16[0:rows, a, 1, j, cols]
                        w_hi, w_lo = wd16[a][0:rows, 0, j, :], wd16[a][0:rows, 1, j, :]
                        mm(bank[6 + t][:, :], h_hi, w_hi, start=j == 0, stop=False)
                        mm(bank[6 + t][:, :], h_hi, w_lo, start=False, stop=False)
                        last = mm(bank[6 + t][:, :], h_lo, w_hi, start=False, stop=j == len(HT) - 1)
                    last.then_inc(s.d_psum, 1)

            def expert(e, a, first, last_one):
                pe.wait_ge(s.gu_lo, e + 1)
                for j in range(2 if first else 0, len(HT)):
                    pe.wait_ge(s.h_full, e * len(HT) + j - 1)
                    hidden(e, a, j, slice(0, TOK)).then_inc(s.h_psum, 1)
                if not first:
                    e_down(e - 1, 1 - a)

            experts(pe, expert)
            e_down(ALLE - 1, (ALLE - 1) % 2)


_INS = ['x', 'ctx_1024', 'L0_xattn_Wq', 'L0_xattn_Wk', 'L0_xattn_Wv', 'L0_xattn_Wo', 'L0_xattn_gq', 'L0_xattn_gk',
        'L0_attn_Wq', 'L0_attn_Wk', 'L0_attn_Wv', 'L0_attn_Wo', 'L0_ffn_gate_w', 'L0_ffn_w_gate', 'L0_ffn_w_up',
        'L0_ffn_w_down', 'L0_ffn_sw_gate', 'L0_ffn_sw_up', 'L0_ffn_sw_down']
_OUTS = [((1, 256, 512), 'float32')]


def kernel(**inputs):
    import numpy as _np
    import concourse.bacc as _bacc
    from concourse import mybir as _mybir
    from concourse.bass_utils import run_bass_kernel_spmd as _run

    nc = _bacc.Bacc("TRN2", target_bir_lowering=False, num_devices=1)
    arrays, args = {}, []
    for name in _INS:
        a = _np.ascontiguousarray(inputs[name])
        if name == 'ctx_1024':
            a = a.reshape(a.shape[1:])
        arrays[f"in_{name}_dram"] = a
        args.append(nc.dram_tensor(f"in_{name}_dram", a.shape, _mybir.dt.from_np(a.dtype), kind="ExternalInput").ap())
    for i, (shape, dtype) in enumerate(_OUTS):
        dt = _mybir.dt.from_np(_np.dtype(dtype))
        args.append(nc.dram_tensor(f"out_{i}_dram", shape, dt, kind="ExternalOutput").ap())
    perceiver_layer(nc, *args)
    r = _run(nc, [arrays], core_ids=[0])
    return r.results[0]["out_0_dram"]
```
